# Optimizing a Trainium2 kernel written in Bass

```python
import numpy as np
import jax
import jax.numpy as jnp

def _softmax(x, axis=-1):
    return jax.nn.softmax(x, axis=axis)

def _gelu(x):
    return jax.nn.gelu(x, approximate=True)

def _silu(x):
    return jax.nn.silu(x)

def _sigmoid(x):
    return jax.nn.sigmoid(x)

def _layernorm(x, axis=-1, eps=1e-05):
    m = jnp.mean(x, axis=axis, keepdims=True)
    v = jnp.var(x, axis=axis, keepdims=True)
    return (x - m) / jnp.sqrt(v + eps)

def _scatter_add(tgt, idx, src, axis=0):
    return tgt.at[idx].add(src)

def _segment_sum(src, seg, n):
    return jax.ops.segment_sum(src, seg, n)
kernel_name = 'mk_early_fusion_d1_tok_img768_r4_b605f3'

def setup_inputs(seed: int=0):
    np.random.seed(seed)
    _w = jnp.asarray

    def _rec_inputs():
        import jax
        import jax.numpy as jnp
        _rk = jax.random.key(seed)
        x = 7.57192e-06 + 1.00007 * jax.random.normal(jax.random.fold_in(_rk, 1), (32, 3, 96, 96), jnp.float32)
        txt = 0.000375391 + 0.999744 * jax.random.normal(jax.random.fold_in(_rk, 2), (32, 128, 192), jnp.float32)
        return (x, txt)
    x, txt = _rec_inputs()

    def _L0_tok_setup():
        import jax, jax.numpy as jnp
        import numpy as np
        PATCH = 16
        HALF = PATCH // 2
        DIM = 192
        CH = 3
        PATCH_DIM = PATCH * PATCH * 5 * CH
        LN_EPS = 1e-05

        def _shift2d(x, t, l):
            H, W = (x.shape[-2], x.shape[-1])
            at, al = (abs(t), abs(l))
            xp = jnp.pad(x, ((0, 0), (0, 0), (at, at), (al, al)))
            return xp[:, :, at - t:at - t + H, al - l:al - l + W]
        key = jax.random.key(seed)
        k1, k2 = jax.random.split(key, 2)
        x = jax.random.normal(k1, (64, CH, 224, 224), dtype=jnp.float32)
        ln_gamma = jnp.ones((PATCH_DIM,), dtype=jnp.float32)
        ln_beta = jnp.zeros((PATCH_DIM,), dtype=jnp.float32)
        W = jax.random.normal(k2, (DIM, PATCH_DIM), dtype=jnp.float32) * np.float32(1.0 / np.sqrt(PATCH_DIM))
        b = jnp.zeros((DIM,), dtype=jnp.float32)
        return {'x': x, 'ln_gamma': ln_gamma, 'ln_beta': ln_beta, 'W': W, 'b': b}
    _L0_tok_all = _L0_tok_setup()
    _L0_tok_in = {k: v for k, v in _L0_tok_all.items() if k in ('ln_gamma', 'ln_beta', 'W', 'b')}
    del _L0_tok_all

    def _L0_attn_setup():
        import jax, jax.numpy as jnp
        import numpy as np
        NH, DK, DV, D = (8, 64, 64, 192)
        DECAY = 0.95
        WRITE_STRENGTH = 0.1
        key = jax.random.key(seed)
        ks = jax.random.split(key, 6)
        s = 0.02
        return {'x': jax.random.normal(ks[0], (4, 1024, D), dtype=jnp.float32), 'w_key': jax.random.normal(ks[1], (NH * DK, D), dtype=jnp.float32) * s, 'w_value': jax.random.normal(ks[2], (NH * DV, D), dtype=jnp.float32) * s, 'w_query': jax.random.normal(ks[3], (NH * DK, D), dtype=jnp.float32) * s, 'w_gate': jax.random.normal(ks[4], (NH, D), dtype=jnp.float32) * s, 'w_out': jax.random.normal(ks[5], (D, NH * DV), dtype=jnp.float32) * s}
    _L0_attn_all = _L0_attn_setup()
    _L0_attn_in = {k: v for k, v in _L0_attn_all.items() if k in ('w_key', 'w_value', 'w_query', 'w_gate', 'w_out')}
    del _L0_attn_all

    def _L0_ffn_setup():
        import jax, jax.numpy as jnp
        import numpy as np
        D_MODEL = 192
        D_EXPERT = 384
        N_EXPERTS = 8
        TOP_K = 2
        EPS = 1e-06

        def _rms_norm(x, w):
            var = jnp.mean(jnp.square(x), axis=-1, keepdims=True)
            return x * jax.lax.rsqrt(var + EPS) * w
        key = jax.random.key(seed)
        ks = jax.random.split(key, 6)
        s_in = 1.0 / np.sqrt(D_MODEL)
        s_mid = 1.0 / np.sqrt(D_EXPERT)
        return {'x': jax.random.normal(ks[0], (2, 512, D_MODEL), dtype=jnp.float32), 'norm_w': jnp.ones((D_MODEL,), dtype=jnp.float32), 'router_w': jax.random.normal(ks[1], (N_EXPERTS, D_MODEL), dtype=jnp.float32) * s_in, 'gate_w': jax.random.normal(ks[2], (N_EXPERTS, D_EXPERT, D_MODEL), dtype=jnp.float32) * s_in, 'up_w': jax.random.normal(ks[3], (N_EXPERTS, D_EXPERT, D_MODEL), dtype=jnp.float32) * s_in, 'down_w': jax.random.normal(ks[4], (N_EXPERTS, D_MODEL, D_EXPERT), dtype=jnp.float32) * s_mid}
    _L0_ffn_all = _L0_ffn_setup()
    _L0_ffn_in = {k: v for k, v in _L0_ffn_all.items() if k in ('norm_w', 'router_w', 'gate_w', 'up_w', 'down_w')}
    del _L0_ffn_all
    return {'x': x, 'txt': txt, 'L0_tok_ln_gamma': _L0_tok_in['ln_gamma'], 'L0_tok_ln_beta': _L0_tok_in['ln_beta'], 'L0_tok_W': _L0_tok_in['W'], 'L0_tok_b': _L0_tok_in['b'], 'L0_attn_w_key': _L0_attn_in['w_key'], 'L0_attn_w_value': _L0_attn_in['w_value'], 'L0_attn_w_query': _L0_attn_in['w_query'], 'L0_attn_w_gate': _L0_attn_in['w_gate'], 'L0_attn_w_out': _L0_attn_in['w_out'], 'L0_ffn_norm_w': _L0_ffn_in['norm_w'], 'L0_ffn_router_w': _L0_ffn_in['router_w'], 'L0_ffn_gate_w': _L0_ffn_in['gate_w'], 'L0_ffn_up_w': _L0_ffn_in['up_w'], 'L0_ffn_down_w': _L0_ffn_in['down_w']}

def reference(x, txt, L0_tok_ln_gamma, L0_tok_ln_beta, L0_tok_W, L0_tok_b, L0_attn_w_key, L0_attn_w_value, L0_attn_w_query, L0_attn_w_gate, L0_attn_w_out, L0_ffn_norm_w, L0_ffn_router_w, L0_ffn_gate_w, L0_ffn_up_w, L0_ffn_down_w):
    import jax
    import jax.numpy as jnp

    def _L0_tok_ref(x, ln_gamma, ln_beta, W, b):
        import jax, jax.numpy as jnp
        import numpy as np
        PATCH = 16
        HALF = PATCH // 2
        DIM = 192
        CH = 3
        PATCH_DIM = PATCH * PATCH * 5 * CH
        LN_EPS = 1e-05

        def _shift2d(x, t, l):
            H, W = (x.shape[-2], x.shape[-1])
            at, al = (abs(t), abs(l))
            xp = jnp.pad(x, ((0, 0), (0, 0), (at, at), (al, al)))
            return xp[:, :, at - t:at - t + H, al - l:al - l + W]
        p = PATCH
        shifts = ((1, -1, 1, -1), (-1, 1, -1, 1), (-1, 1, 1, -1), (1, -1, -1, 1))
        parts = [x] + [_shift2d(x, HALF * s[2], HALF * s[0]) for s in shifts]
        xc = jnp.concatenate(parts, axis=1)
        B, C5, H, Wd = xc.shape
        h, w = (H // p, Wd // p)
        patches = xc.reshape(B, C5, h, p, w, p)
        patches = patches.transpose(0, 2, 4, 3, 5, 1).reshape(B, h * w, p * p * C5)
        mu = patches.mean(axis=-1, keepdims=True)
        var = patches.var(axis=-1, keepdims=True)
        xn = (patches - mu) * jax.lax.rsqrt(var + LN_EPS) * ln_gamma + ln_beta
        return jnp.einsum('bnp,dp->bnd', xn, W) + b

    def _L0_attn_ref(x, w_key, w_value, w_query, w_gate, w_out):
        import jax, jax.numpy as jnp
        import numpy as np
        NH, DK, DV, D = (8, 64, 64, 192)
        DECAY = 0.95
        WRITE_STRENGTH = 0.1
        B, S, _ = x.shape
        k = (x @ w_key.T).reshape(B, S, NH, DK)
        v = (x @ w_value.T).reshape(B, S, NH, DV)
        q = (x @ w_query.T).reshape(B, S, NH, DK)
        gate = jax.nn.sigmoid(x @ w_gate.T)
        k0 = k[0]
        v0 = v[0]
        g0 = gate[0]

        def step(fw, inp):
            q_t, k0_t, v0_t, g0_t = inp
            retrieved = jnp.einsum('bhk,hkv->bhv', q_t, fw)
            write = (WRITE_STRENGTH * g0_t)[:, None, None] * (k0_t[:, :, None] * v0_t[:, None, :])
            fw_new = DECAY * fw + jax.lax.stop_gradient(write)
            return (fw_new, retrieved)
        fw0 = jnp.zeros((NH, DK, DV), dtype=x.dtype)
        inputs = (q.transpose(1, 0, 2, 3), k0, v0, g0)
        _, retrieved = jax.lax.scan(step, fw0, inputs)
        retrieved = retrieved.transpose(1, 0, 2, 3).reshape(B, S, NH * DV)
        return x + retrieved @ w_out.T

    def _L0_ffn_ref(x, norm_w, router_w, gate_w, up_w, down_w):
        import jax, jax.numpy as jnp
        import numpy as np
        D_MODEL = 192
        D_EXPERT = 384
        N_EXPERTS = 8
        TOP_K = 2
        EPS = 1e-06

        def _rms_norm(x, w):
            var = jnp.mean(jnp.square(x), axis=-1, keepdims=True)
            return x * jax.lax.rsqrt(var + EPS) * w
        residual = x
        B, S, D = x.shape
        xn = _rms_norm(x, norm_w)
        xf = xn.reshape(-1, D)
        logits = xf @ router_w.T
        probs = jax.nn.softmax(logits, axis=-1)
        _, top_idx = jax.lax.top_k(probs, TOP_K)
        sel = jax.nn.one_hot(top_idx, N_EXPERTS, dtype=probs.dtype).sum(axis=1)
        comb_w = probs * sel
        g = jnp.einsum('td,efd->tef', xf, gate_w)
        u = jnp.einsum('td,efd->tef', xf, up_w)
        h = jax.nn.silu(g) * u
        h = h * comb_w[:, :, None]
        y = jnp.einsum('tef,edf->td', h, down_w)
        return y.reshape(B, S, D) + residual
    h = _L0_tok_ref(x, L0_tok_ln_gamma, L0_tok_ln_beta, L0_tok_W, L0_tok_b)
    h = jnp.concatenate([h, txt], axis=1)
    h = h + _L0_attn_ref(_layernorm(h, axis=-1), L0_attn_w_key, L0_attn_w_value, L0_attn_w_query, L0_attn_w_gate, L0_attn_w_out)
    h = h + _L0_ffn_ref(_layernorm(h, axis=-1), L0_ffn_norm_w, L0_ffn_router_w, L0_ffn_gate_w, L0_ffn_up_w, L0_ffn_down_w)
    return h

_drawn_inputs = setup_inputs


def setup_inputs(seed=0):
    import zlib

    import numpy as np

    out = dict(_drawn_inputs(seed))
    spreads = {'L0_tok_ln_gamma': (1.0, 0.2),
     'L0_tok_ln_beta': (0.0, 0.1),
     'L0_tok_b': (0.0, 0.1),
     'L0_ffn_norm_w': (1.0, 0.6)}
    factors = {'L0_attn_w_key': 6.437,
     'L0_attn_w_value': 6.737,
     'L0_attn_w_query': 6.516,
     'L0_attn_w_gate': 8.0,
     'L0_attn_w_out': 6.391,
     'L0_ffn_router_w': 6.664,
     'L0_ffn_gate_w': 6.348,
     'L0_ffn_up_w': 5.928,
     'L0_ffn_down_w': 5.924}
    for name, (base, spread) in spreads.items():
        noise = np.random.default_rng([zlib.crc32(name.encode()), seed]).standard_normal(out[name].shape)
        drawn = base * np.exp(spread * noise) if base else spread * noise
        out[name] = jnp.asarray(drawn.astype(out[name].dtype))
    for name, factor in factors.items():
        out[name] = (out[name] * factor).astype(out[name].dtype)
    return out
```

```python
from contextlib import ExitStack

import concourse.bass as bass
from concourse import mybir

ALU = mybir.AluOpType
ACT = mybir.ActivationFunctionType
AX = mybir.AxisListType
F32 = mybir.dt.float32
BF16 = mybir.dt.bfloat16
I32 = mybir.dt.int32
U32 = mybir.dt.uint32

P = 128
B = 32
D = 192
DH = 96
GRID = 6
NPATCH = GRID * GRID
CH = 3
PARTS = 5
PFEAT = 16 * 16 * PARTS * CH
SEQ = 164
TQ = 4
TILES = SEQ // TQ
PTILES = NPATCH // TQ
CHUNK = 16
CT_TILES = CHUNK // TQ
CHUNKS = -(-SEQ // CHUNK)
NH = 8
DK = 64
SPAD = CHUNKS * CHUNK
NE = 8
DE = 384
FC = DE // P
REGION = TILES * P + P
SLOTS = TILES * 2 + NE
LN_EPS = 1e-5
RMS_EPS = 1e-6
DECAY = 0.95
WRITE = 0.1

C_KEY, C_TOK = 0, CHUNKS
C_MASK = C_TOK + TILES
C_STAT = C_MASK + CHUNK
C_EXP = C_STAT + 24
C_SLOT = C_EXP + NE
C_ALL = C_SLOT + SLOTS


class Steps:

    def __init__(self, eng, sem):
        self.eng, self.sem, self.base, self.n = eng, sem, 0, 0

    def mark(self, ins):
        self.n += 1
        return ins.then_inc(self.sem, 1)

    def wait(self):
        self.eng.wait_ge(self.sem, self.base + self.n)

    def wait_apart(self):
        self.wait()
        self.eng.nop(nofuse=True)

    def link(self, ins):
        self.mark(ins)
        self.wait()

    def enter(self, trip, per_trip):
        self.start, self.per = self.base + self.n, per_trip
        self.base, self.n = trip * per_trip + self.start, 0

    def leave(self, trips):
        assert self.n == self.per, (self.n, self.per)
        self.base, self.n = self.start + trips * self.per, 0


def build(nc, x, txt, gamma, beta, W, bias, w_key, w_value, w_query, w_gate, w_out,
          norm_w, router_w, gate_w, up_w, down_w, consts, out):
    with ExitStack() as ctx:
        ctx.enter_context(nc.allow_non_contiguous_dma("small transposed parameters"))
        base0 = nc.sbuf_base + (-nc.sbuf_base) % 64
        top = [base0]

        def at(name, shape, dt, offset):
            return nc.alloc_sbuf_tensor_at(name, shape, dt, offset=offset)

        def room(nbytes):
            a = top[0]
            top[0] = a + nbytes + (-nbytes) % 32
            assert top[0] <= nc.sbuf_usable_end, (name_of, top[0])
            return a

        name_of = "sbuf"

        def sb(name, shape, dt=F32):
            n = 4 if dt != BF16 else 2
            for s in shape[1:]:
                n *= s
            return at(name, shape, dt, room(n))

        def sem(name):
            return ctx.enter_context(nc.semaphore(name))

        r_img = room(CH * 64 * 64 * 4)
        r_xt = room(CH * 64 * 64 * 4)
        r_wc = room(24 * 193 * 4)
        r_hres = room(TILES * D * 4)
        r_gh = room(2 * 2 * NH * D * 4)
        img = at("img", [P, CH, 64, 64], F32, r_img)
        w_gu = at("w_gu", [DH, 2, NE, 2 * DE], F32, r_img)
        wraw = at("wraw", [DH, 2, PFEAT], F32, r_xt)
        gam = at("gam", [DH, PFEAT], F32, r_xt + 2 * PFEAT * 4)
        imgT = at("imgT", [P, 8, 4, CH, P], F32, r_xt)
        raw_g = at("raw_g", [P, NE * FC, D], F32, r_xt)
        raw_u = at("raw_u", [P, NE * FC, D], F32, r_xt + NE * FC * D * 4)
        r_tail = r_xt + 2 * NE * FC * D * 4
        wk = at("wk", [P, 4, D], F32, r_wc)
        wq = at("wq", [P, 4, D], F32, r_wc + 3072)
        wv = at("wv", [P, 4, D], F32, r_wc + 6144)
        woraw = at("woraw", [DH, 2, NH * DK], F32, r_wc + 9216)
        woT = at("woT", [P, 4, D], F32, r_wc + 13312)
        wcT = at("wcT", [P, 24, 193], F32, r_wc)
        w_dn = at("w_dn", [P, NE, FC, D], F32, r_wc)
        bet = at("bet", [DH, PFEAT], F32, r_hres)
        junk = at("junk", [DH, PFEAT], F32, r_hres + PFEAT * 4)
        hres = at("hres", [P, TILES * D], F32, r_hres)
        gT = at("gT", [DH, 2, NH, D], F32, r_gh)
        hT = at("hT", [DH, 2, NH, D], F32, r_gh + 2 * NH * D * 4)
        raw_d = at("raw_d", [DH, 2, NE, DE], F32, r_gh)
        xT = at("xT", [DH, 2, 512], F32, r_tail)
        xfT = at("xfT", [DH, 2, 512], F32, r_tail + 4096)
        sm = at("sm", [P, 512], F32, r_tail + 8192)
        r_act = room(2 * 2 * SPAD * NH * 4)
        keysT = at("keysT", [DH, 2, CHUNKS, P], F32, r_act)
        valsT = at("valsT", [DH, 2, CHUNKS, P], F32, r_act + 2 * SPAD * NH * 4)
        sqjunk = at("sqjunk", [P, CH, 32, 32], BF16, r_act)
        strip = [at(f"strip{i}", [P, CH, 4, P], F32, r_act + 6144 + 6144 * i) for i in range(2)]
        xs = [at(f"xs{i}", [P, D], F32, r_act + 768 * i) for i in range(2)]
        xsT = [at(f"xsT{i}", [DH, 2, P], F32, r_act + 1536 + 1024 * i) for i in range(2)]
        sg = [at(f"sg{i}", [P, DE], F32, r_act + 3584 + 1536 * i) for i in range(2)]
        hh = [at(f"hh{i}", [P, DE], F32, r_act + 6656 + 1536 * i) for i in range(2)]
        hhT = [at(f"hhT{i}", [P, FC, P], F32, r_act + 9728 + 1536 * i) for i in range(2)]
        ysb = [at(f"ysb{i}", [P, D], F32, r_act + 12800 + 768 * i) for i in range(2)]
        yg = [[at(f"yg{i}_{k}", [P, D], F32, r_act + 768 * (2 * i + k)) for k in range(2)] for i in range(4)]
        ofin = [at(f"ofin{i}", [P, D], F32, r_act + 6144 + 768 * i) for i in range(4)]
        oacc = [at(f"oacc{i}", [P, D], F32, r_act + 9216 + 768 * i) for i in range(4)]

        cst = sb("cst", [P, C_ALL])
        ident = sb("ident", [P, P])
        ltri = sb("ltri", [P, P], BF16)
        onesb = sb("onesb", [P, P], BF16)
        sumwb = sb("sumwb", [P, D])
        constb = sb("constb", [P, D])
        colsum = sb("colsum", [DH, 2, 2])
        biasc = sb("biasc", [DH, 2])
        nwc = sb("nwc", [DH, 2])
        wgT = sb("wgT", [DH, 2, NH])
        rwT = sb("rwT", [DH, 2, NE])
        rws = sb("rws", [DH, 2, NE])
        g8 = sb("g8", [NH, SPAD])
        kgate = sb("kgate", [P, CHUNKS])
        stats = sb("stats", [P, 4, 6])
        mv = sb("mv", [P, 4, 2])
        sc = sb("sc", [P, 32])
        stats2 = sb("stats2", [P, 4, 6])
        mv2 = sb("mv2", [P, 4, 2])
        sd2 = sb("sd2", [P, 48])
        nst = sb("nst", [DH, 2, D])
        kc = sb("kc", [DH, 4, P])
        top8 = sb("top8", [P, TILES * 8])
        t8 = sb("t8", [P, 4, 8])
        i8 = sb("i8", [P, 4, 8], U32)
        idxf = sb("idxf", [P, TILES * 2])
        rankf = sb("rankf", [P, TILES * 2])
        r_small = room(4 * 1024)
        xn = [at(f"xn{j}", [P, D], F32, r_small + 768 * j) for j in range(4)]
        vb = at("vb", [DH, 2, 2, P], F32, r_small)
        oh = sb("oh", [P, 64])
        ohm = sb("ohm", [P, 64])
        eb = sb("eb", [P, 4, 8], BF16)
        ecum = sb("ecum", [P, 5, 8], BF16)
        posf = sb("posf", [P, 8])
        posu = [sb(f"posu{p}", [P, 8], U32) for p in range(2)]
        arow = sb("arow", [P, D])
        crow = sb("crow", [P, D])
        xf = [[at(f"xf{p}_{j}", [P, D], F32, r_img + 43008 + 768 * (4 * p + j)) for j in range(4)] for p in range(2)]
        h2 = [at(f"h2_{j}", [P, D], F32, r_img + 768 * j) for j in range(4)]
        x0 = [at(f"x0_{j}", [P, D], F32, r_img + 4096 + 768 * j) for j in range(2)]
        x0n = [at(f"x0n_{j}", [P, D], F32, r_img + 6144 + 768 * j) for j in range(2)]
        x0T = at("x0T", [DH, 2, SPAD], F32, r_img + 8192)
        zrow = at("zrow", [P, D], F32, r_small + 3072)
        tmp = [at(f"tmp{i}", [P, D], F32, r_small + 768 * i) for i in range(2)]
        top_small, top[0] = top[0], r_act + 14336
        tab = sb("tab", [P, 2, SLOTS], I32)
        tabf = at("tabf", [P, SLOTS, NE], F32, r_tail)
        slotf = sb("slotf", [P, 3, SLOTS])
        ct = sb("ct", [P, 8, NE])
        cti = sb("cti", [P, 2, NE], I32)
        wts = sb("wts", [P, TILES * 2])
        esum = sb("esum", [P, TILES])
        ypos = sb("ypos", [P, TILES * 2])
        yposu = sb("yposu", [P, TILES * 2], U32)
        assert top[0] <= r_act + 2 * 2 * SPAD * NH * 4
        top[0] = top_small
        ygi = [sb(f"ygi{i}", [P, 2], U32) for i in range(4)]
        ypj = at("ypj", [P, TILES * 2, NE], F32, r_tail + 4096)
        print("sbuf left", nc.sbuf_usable_end - top[0])

        disp = nc.dram_tensor("disp", [(NE + 1) * REGION, D], F32, kind="Internal").ap()
        ydram = nc.dram_tensor("ydram", [SLOTS * P, D], F32, kind="Internal").ap()

        bank = [ctx.enter_context(nc.psum_tensor(f"bank{i}", [P, 512], F32)) for i in range(8)]

        s_attw, s_wraw, s_gam, s_bet, s_cst, s_par = (sem(n) for n in (
            "attn_weights_in", "patch_weights_in", "gamma_in", "beta_in", "consts_in", "params_in"))
        s_img, s_border, s_strip, s_txt, s_x0 = (sem(n) for n in ("image_in", "border_zero", "strip_ready", "text_in", "batch0_in"))
        s_rawg, s_rawd = sem("raw_gate_up_in"), sem("raw_down_in")
        s_pool = sem("pool_steps")
        s_dve, s_act = sem("dve_steps"), sem("act_steps")
        s_cons = sem("pool_constants")
        s_pg, s_eg = sem("product_mm"), sem("product_out")
        s_wprep, s_vb, s_row, s_rowout = sem("patch_weights_ready"), sem("row_lhs"), sem("row_mm"), sem("row_out")
        s_wt, s_wtout = sem("wT_mm"), sem("wT_out")
        s_it, s_itout = sem("imgT_mm"), sem("imgT_out")
        s_sq = sem("squares")
        s_pat, s_patout, s_pv, s_psd = sem("patch_mm"), sem("patch_read"), sem("patch_var"), sem("patch_std")
        s_ptok = sem("patch_tokens")
        s_v0, s_sd0, s_x0n, s_x0t, s_x0T = (sem(n) for n in ("var0", "std0", "x0_norm", "x0T_mm", "x0T_out"))
        s_kv, s_kvout, s_vvout, s_g8, s_g8out, s_kg, s_kgr = (sem(n) for n in (
            "kv_mm", "keys_out", "vals_out", "gate_mm", "gate_out", "gate_spread", "gate_ready"))
        s_v1, s_sd1, s_r1, s_xn = sem("var1"), sem("std1"), sem("rstd1"), sem("xn_ready")
        s_t, s_xT = sem("xT_mm"), sem("xT_out")
        s_kc, s_sc, s_sm = sem("keys_copied"), sem("scores_mm"), sem("scores_masked")
        s_rt, s_ar, s_cr = sem("rows_mm"), sem("key_rows"), sem("value_rows")
        s_o, s_h2, s_nu, s_ns = sem("attn_mm"), sem("h2_ready"), sem("state_mm"), sem("state_ready")
        s_v2, s_sd2, s_s2, s_xf = sem("var2"), sem("std2"), sem("rstd2"), sem("xf_ready")
        s_t2, s_xfT, s_lg, s_e, s_pf, s_pos = (sem(n) for n in (
            "xfT_mm", "xfT_out", "logits_mm", "onehots", "prefix_mm", "positions"))
        s_scat = [[sem(f"scattered{p}_{j}") for j in range(4)] for p in range(2)]
        s_et, s_eout = sem("expertT_mm"), [sem("expertT_out_dve"), sem("expertT_out_act")]
        s_cread, s_tab, s_zf = sem("counts_mm"), sem("table"), sem("tail_zeroed")
        s_xs = [sem(f"xs_in{i}") for i in range(2)]
        s_ys = [sem(f"y_stored{i}") for i in range(2)]
        s_xst, s_xsT, s_gu, s_sg, s_hh = (sem(n) for n in ("xsT_mm", "xsT_out", "gate_up_mm", "silu", "hidden"))
        s_ht, s_hhT, s_dn, s_y = (sem(n) for n in ("hiddenT_mm", "hiddenT_out", "down_mm", "y_ready"))
        s_exp, s_w, s_yp = sem("softmax_exp"), sem("weights_ready"), sem("y_positions")
        s_ygi = sem("gather_index")
        s_yg = [sem(f"gathered{i}") for i in range(4)]
        s_fin = sem("final_ready")
        s_out = [sem(f"out_stored{i}") for i in range(4)]

        txt_q = txt.rearrange("b (n q) d -> q b n d", q=TQ)
        out_t = out.rearrange("b s d -> s b d")
        hres3 = hres.rearrange("p (n d) -> p n d", d=D)

        block = ctx.enter_context(nc.Block())

        def part_of(dr, s):
            return (1 if s == 0 else 3) if dr <= 0 else (4 if s == 0 else 2)

        wv5 = wraw[:].rearrange("p m (y x c) -> p m y x c", y=16, x=16)

        def experts_out(eng, side):
            for n in range(side, 44, 2):
                eng.wait_ge(s_et, n + 1)
                b = bank[n % 4]
                if n < 32:
                    e, which, m = n // 4, n // 2 % 2, n % 2
                    dst = w_gu[:, m, e, DE * which:DE * which + DE]
                    if side:
                        ins = nc.scalar.activation(dst, b[0:DH, 0:DE], ACT.Copy, scale=nwc[:, m:m + 1])
                    else:
                        ins = nc.vector.tensor_scalar(dst, b[0:DH, 0:DE], nwc[:, m:m + 1], None, ALU.mult)
                else:
                    g = n - 32
                    dst = w_dn[:].rearrange("p e c d -> p (e c) d")[:, 2 * g:2 * g + 2, :]
                    src = b[:, 0:384].rearrange("p (k d) -> p k d", k=2)
                    ins = nc.scalar.copy(dst, src) if side else nc.vector.tensor_copy(dst, src)
                ins.then_inc(s_eout[side], 1)

        @block.sync
        def _(sp):
            sp.dma_start(wraw[:], W.rearrange("(m p) f -> p m f", p=DH)).then_inc(s_wraw, 16)
            sp.dma_start(bet[:], beta.partition_broadcast(DH)).then_inc(s_bet, 16)
            sp.dma_start(gam[:], gamma.partition_broadcast(DH)).then_inc(s_gam, 16)
            for c in range(CH):
                for ih in range(2):
                    for jh in range(2):
                        q = 32 * (2 * ih + jh)
                        r0, c0 = 8 - 8 * ih, 8 - 8 * jh
                        sp.dma_start(img[q:q + 32, c, r0:r0 + 56, c0:c0 + 56],
                                     x[:, c, 40 * ih:40 * ih + 56, 40 * jh:40 * jh + 56]).then_inc(s_img, 16)
            sp.wait_ge(s_wprep, 1)
            for q in range(TQ):
                sp.dma_start(hres3[32 * q:32 * q + 32, PTILES:TILES, :], txt_q[q]).then_inc(s_txt, 16)
            sp.wait_ge(s_it, 32)
            sp.wait_ge(s_sq, 18)
            sp.dma_start(x0[0][:], txt[0]).then_inc(s_x0, 16)
            sp.wait_ge(s_ptok, PTILES)
            for q in range(TQ):
                sp.dma_start(x0[1][PTILES * q:PTILES * q + PTILES, :],
                             hres3[32 * q:32 * q + 1, 0:PTILES, :]).then_inc(s_x0, 16)
            sp.wait_ge(s_pat, PTILES)
            sp.dma_start(raw_g[:], gate_w.rearrange("e (c f) d -> f (e c) d", f=P)).then_inc(s_rawg, 16)
            sp.dma_start(raw_u[:], up_w.rearrange("e (c f) d -> f (e c) d", f=P)).then_inc(s_rawg, 16)
            sp.wait_ge(s_kv, 2 * NH)
            for m in range(2):
                sp.dma_start(raw_d[:, m], down_w[:, DH * m:DH * m + DH].rearrange("e p f -> p e f")).then_inc(s_rawd, 16)
            sp.wait_ge(s_tab, 1)
            for e in range(NE):
                n = sp.value_load(cti[0:1, 1, e:e + 1], min_val=0, max_val=TILES * P)
                sp.dma_start(disp[bass.ds(n + e * REGION, P), :], zrow[:]).then_inc(s_zf, 16)
            sp.dma_start(disp[NE * REGION:NE * REGION + P, :], zrow[:]).then_inc(s_zf, 16)
            sp.wait_ge(s_zf, 16 * (NE + 1))
            for p in range(2):
                for j in range(4):
                    n = len([c for c in range(p, CHUNKS, 2) if 4 * c + j < TILES])
                    sp.wait_ge(s_scat[p][j], 32 * n)

            def load_slot(s, b, first=False):
                if not first:
                    sp.wait_ge(s_xst, s - 1)
                row = sp.value_load(tab[0:1, 0, bass.ds(s, 1)], min_val=0, max_val=NE * REGION)
                sp.dma_start(xs[b][:], disp[bass.ds(row, P), :]).then_inc(s_xs[b], 16)

            sp.wait_ge(s_kc, CHUNKS)
            load_slot(0, 0, True)
            load_slot(1, 1, True)
            with sp.Fori(0, SLOTS // 2 - 1) as i:
                for b in range(2):
                    load_slot(2 * i + 2 + b, b)

            def store_out(n, j):
                sp.wait_ge(s_fin, n + 1)
                sp.dma_start(out_t[bass.ds(n * TQ, TQ)], ofin[j][:]).then_inc(s_out[j], 16)

            with sp.Fori(0, TILES // 4) as i:
                for j in range(4):
                    store_out(4 * i + j, j)
            store_out(TILES - 1, 0)
            for j in range(4):
                sp.wait_ge(s_out[j], 16 * len(range(j, TILES, 4)) + 16)

        @block.scalar
        def _(act):
            steps = Steps(act, s_act)
            act.dma_start(wk[:], w_key.rearrange("(c p) d -> p c d", p=P)).then_inc(s_attw, 16)
            act.dma_start(wq[:], w_query.rearrange("(c p) d -> p c d", p=P)).then_inc(s_attw, 16)
            act.dma_start(wv[:], w_value.rearrange("(c p) d -> p c d", p=P)).then_inc(s_attw, 16)
            act.dma_start(woraw[:], w_out.rearrange("(m p) f -> p m f", p=DH)).then_inc(s_attw, 16)
            act.dma_start(cst[:], consts).then_inc(s_cst, 16)
            act.dma_start(biasc[:], bias.rearrange("(m p) -> p m", p=DH)).then_inc(s_par, 16)
            act.dma_start(nwc[:], norm_w.rearrange("(m p) -> p m", p=DH)).then_inc(s_par, 16)
            for m in range(2):
                act.dma_start(wgT[:, m, :], w_gate[:, DH * m:DH * m + DH].rearrange("h p -> p h")).then_inc(s_par, 16)
                act.dma_start(rwT[:, m, :], router_w[:, DH * m:DH * m + DH].rearrange("h p -> p h")).then_inc(s_par, 16)

            for k in range(2):
                act.wait_ge(s_pg, k + 1)
                nc.scalar.copy(woT[:, 2 * k:2 * k + 2, :], bank[k][:, 0:384]).then_inc(s_eg, 1)
            for n in range(2 * NH):
                act.wait_ge(s_pg, n + 3)
                dst = (gT if n % 2 == 0 else hT)[:, :, n // 2, :]
                nc.scalar.copy(dst, bank[n % 2][0:DH, 0:384].rearrange("p (m d) -> p m d", m=2)).then_inc(s_eg, 1)
            for g in range(12):
                act.wait_ge(s_wt, g + 1)
                nc.scalar.copy(wcT[:, 2 * g:2 * g + 2, 0:D],
                               bank[g % 2][:, 0:384].rearrange("p (k d) -> p k d", k=2)).then_inc(s_wtout, 1)
            act.wait_ge(s_border, 1)
            act.wait_ge(s_img, 16 * 12)

            def squares(p):
                i, j = p // 3, p % 3
                nc.scalar.activation(sqjunk[:], img[:, :, 16 * i:16 * i + 32, 16 * j:16 * j + 32], ACT.Square,
                                     accum_out=sc[:, p:p + 1]).then_inc(s_sq, 1)
                act.wait_ge(s_sq, 2 * p + 1)
                nc.scalar.activation(sqjunk[:, :, 0:16, 0:16], img[:, :, 16 * i + 8:16 * i + 24, 16 * j + 8:16 * j + 24],
                                     ACT.Square, accum_out=sc[:, 9 + p:10 + p]).then_inc(s_sq, 1)
                act.wait_ge(s_sq, 2 * p + 2)

            for p in range(9):
                squares(p)
            for p in range(9):
                act.wait_ge(s_pv, p + 1)
                nc.scalar.activation(sd2[:, p:p + 1], sd2[:, 16 + p:17 + p], ACT.Sqrt).then_inc(s_psd, 1)
            act.wait_ge(s_v0, 1)
            nc.scalar.activation(sd2[:, 0:2], sd2[:, 16:18], ACT.Sqrt).then_inc(s_sd0, 1)
            act.wait_ge(s_x0t, 1)
            nc.scalar.copy(x0T[:, :, NPATCH:SEQ], bank[0][0:DH, 0:256].rearrange("p (m s) -> p m s", m=2)).then_inc(s_x0T, 1)
            act.wait_ge(s_g8, 1)
            nc.scalar.activation(g8[:].rearrange("h (s c) -> h s c", s=CHUNK),
                                 bank[2][0:NH, 0:SPAD].rearrange("h (c s) -> h s c", s=CHUNK), ACT.Sigmoid).then_inc(s_g8out, 1)
            act.wait_ge(s_g8out, 1)
            for h in range(NH):
                act.dma_start(kgate[CHUNK * h:CHUNK * h + CHUNK, :],
                              g8[h:h + 1, :].rearrange("h (s c) -> h s c", s=CHUNK)).then_inc(s_kg, 16)
            for h in range(NH):
                act.wait_ge(s_kv, 2 * h + 1)
                nc.scalar.copy(keysT[:, :, :, CHUNK * h:CHUNK * h + CHUNK],
                               bank[4 + h % 2][0:DH, 0:2 * SPAD].rearrange("p (m c s) -> p m c s", m=2, s=CHUNK)
                               ).then_inc(s_kvout, 1)
            act.wait_ge(s_ns, 1)

            def ln1(c, nt):
                act.wait_ge(s_v1, c + 1)
                nc.scalar.activation(sc[:, 4:4 + nt], sc[:, 0:nt], ACT.Sqrt).then_inc(s_sd1, 1)
                act.wait_ge(s_r1, c + 1)
                for j in range(nt):
                    nc.scalar.activation(xn[j][:], hres[:, bass.ds((4 * c + j) * D, D)], ACT.Identity,
                                         scale=sc[:, 8 + j:9 + j], bias=sc[:, 12 + j:13 + j]).then_inc(s_xn, 1)

            def xT_out(c, nt):
                for k in range(-(-nt // 2)):
                    act.wait_ge(s_t, 2 * c + k + 1)
                    w = P * min(2, nt - 2 * k)
                    nc.scalar.copy(xT[:, :, 256 * k:256 * k + w],
                                   bank[1 + k][0:DH, :].rearrange("p (m s) -> p m s", m=2)[:, :, 0:w]).then_inc(s_xT, 1)

            def xfT_out(c, nt):
                for k in range(-(-nt // 2)):
                    act.wait_ge(s_t2, 2 * c + k + 1)
                    w = P * min(2, nt - 2 * k)
                    nc.scalar.copy(xfT[:, :, 256 * k:256 * k + w],
                                   bank[1 + k][0:DH, :].rearrange("p (m s) -> p m s", m=2)[:, :, 0:w]).then_inc(s_xfT, 1)

            def ln2(c, par, uses, nt):
                act.wait_ge(s_v2, c + 1)
                nc.scalar.activation(sd2[:, 8:16], sd2[:, 0:8], ACT.Sqrt).then_inc(s_sd2, 1)
                act.wait_ge(s_s2, c + 1)
                for j in range(nt):
                    if uses is not None:
                        act.wait_ge(s_scat[par][j], 32 * uses)
                    nc.scalar.activation(xf[par][j][:], h2[j][:], ACT.Identity,
                                         scale=sd2[:, 24 + j:25 + j], bias=sd2[:, 28 + j:29 + j]).then_inc(s_xf, 1)

            def chunk(c, par, uses, nt, prev, nxt):
                act.wait_ge(s_rt, c + 1)
                nc.scalar.activation(crow[:], bank[7][:, D:2 * D], ACT.Copy, scale=kgate[:, bass.ds(c, 1)]).then_inc(s_cr, 1)
                nc.scalar.copy(arow[:], bank[7][:, 0:D]).then_inc(s_ar, 1)
                if prev:
                    xfT_out(c - 1, prev)
                if nxt:
                    ln1(c + 1, nxt)
                    xT_out(c + 1, nxt)
                ln2(c, par, uses, nt)

            ln1(0, 4)
            xT_out(0, 4)
            chunk(0, 0, None, 4, 0, 4)
            chunk(1, 1, None, 4, 4, 4)
            chunk(2, 0, 1, 4, 4, 4)
            with act.Fori(0, 3) as i:
                chunk(2 * i + 3, 1, i + 1, 4, 4, 4)
                chunk(2 * i + 4, 0, i + 2, 4, 4, 4)
            chunk(9, 1, 4, 4, 4, 1)
            chunk(10, 0, 5, 1, 4, 0)
            xfT_out(10, 1)

            experts_out(act, 1)
            act.wait_ge(s_w, 1)
            nc.scalar.activation(top8[:], top8[:], ACT.Exp).then_inc(s_exp, 1)

            def silu(s, b):
                act.wait_ge(s_gu, s + 1)
                nc.scalar.activation(sg[b][:], bank[2 * b][:, 0:DE], ACT.Silu).then_inc(s_sg, 1)

            def hidden_out(s, b):
                act.wait_ge(s_ht, s + 1)
                nc.scalar.copy(hhT[b][:], bank[4][:, 0:DE].rearrange("p (c t) -> p c t", c=FC)).then_inc(s_hhT, 1)

            def store_slot(s, b):
                act.wait_ge(s_y, s + 1)
                act.dma_start(ydram[bass.ds(s * P, P), :], ysb[b][:]).then_inc(s_ys[b], 16)

            silu(0, 0)
            silu(1, 1)
            hidden_out(0, 0)
            with act.Fori(0, SLOTS // 2 - 1) as i:
                for b in range(2):
                    silu(2 * i + 2 + b, b)
                    hidden_out(2 * i + 1 + b, 1 - b)
                    store_slot(2 * i + b, b)
            hidden_out(SLOTS - 1, 1)
            for b in range(2):
                store_slot(SLOTS - 2 + b, b)

        @block.gpsimd
        def _(pool):
            pool.memset(ident[:], 0.0).then_inc(s_pool, 1)
            pool.memset(onesb[:], 1.0).then_inc(s_pool, 1)
            pool.memset(ltri[:], 1.0).then_inc(s_pool, 1)
            pool.wait_ge(s_pool, 3)
            pool.affine_select(out=ident[:], in_=ident[:], compare_op=ALU.not_equal, fill=1.0, base=0,
                               pattern=[[-1, P]], channel_multiplier=1)
            pool.affine_select(out=ltri[:], in_=ltri[:], compare_op=ALU.is_gt, fill=0.0, base=0,
                               pattern=[[1, P]], channel_multiplier=-1).then_inc(s_cons, 1)

            pool.wait_ge(s_img, 16 * 12)
            pool.wait_ge(s_border, 1)
            for r in range(8):
                if r >= 2:
                    pool.wait_ge(s_it, 4 * (r - 1))
                for c in range(CH):
                    ins = pool.tensor_copy(strip[r % 2][:, c].rearrange("p m (y x) -> p m y x", y=8),
                                           img[:, c, 8 * r:8 * r + 8, :].rearrange("p y (m x) -> p m y x", m=4))
                ins.then_inc(s_strip, 1)

            def keys(c, first=False):
                if not first:
                    pool.wait_ge(s_sc, c)
                    pool.wait_ge(s_rt, c)
                if first:
                    pool.wait_ge(s_kvout, NH)
                    pool.wait_ge(s_vvout, NH)
                for k, t in enumerate((keysT, valsT)):
                    ins = pool.tensor_copy(kc[:, 2 * k:2 * k + 2, :],
                                           t[:].rearrange("p m c s -> p m (c s)")[:, :, bass.ds(c * P, P)])
                ins.then_inc(s_kc, 1)

            def scatter(c, par, nt):
                pool.wait_ge(s_pos, c + 1)
                for j in range(nt):
                    pool.wait_ge(s_xf, 4 * c + j + 1)
                    pool.nop(nofuse=True)
                    for k in range(2):
                        pool.indirect_dma_start(disp, bass.IndirectOffsetOnAxis(
                            ap=posu[par][:, 2 * j + k:2 * j + k + 1], axis=0), xf[par][j][:], None
                            ).then_inc(s_scat[par][j], 16)

            keys(0, True)
            keys(1)
            with pool.Fori(0, 4) as i:
                keys(2 * i + 2)
                scatter(2 * i, 0, 4)
                keys(2 * i + 3)
                scatter(2 * i + 1, 1, 4)
            keys(10)
            scatter(8, 0, 4)
            scatter(9, 1, 4)
            scatter(10, 0, 1)

            for b in range(2):
                pool.wait_ge(s_ys[b], 16 * SLOTS // 2 + 16)

            def gather(n, j, reuse):
                pool.wait_ge(s_ygi, n + 1)
                if reuse is not None:
                    pool.wait_ge(s_fin, reuse)
                pool.nop(nofuse=True)
                for k in range(2):
                    pool.indirect_dma_start(yg[j][k][:], None, ydram, bass.IndirectOffsetOnAxis(
                        ap=ygi[j][:, k:k + 1], axis=0)).then_inc(s_yg[j], 16)

            for j in range(4):
                gather(j, j, None)
            with pool.Fori(1, TILES // 4) as i:
                for j in range(4):
                    gather(4 * i + j, j, 4 * i + j - 3)
            gather(TILES - 1, 0, TILES - 4)

        @block.tensor
        def _(pe):
            pe.wait_ge(s_cons, 1)
            pe.wait_ge(s_attw, 64)
            for k in range(4):
                for m in range(2):
                    ins = pe.transpose(bank[k // 2][:, 192 * (k % 2) + DH * m:192 * (k % 2) + DH * m + DH],
                                       woraw[:, m, P * k:P * k + P], ident[0:DH, 0:DH])
                if k % 2:
                    ins.then_inc(s_pg, 1)
            for n in range(2 * NH):
                h, o = n // 2, 64 * (n // 2 % 2)
                pe.wait_ge(s_eg, n + 1 if n else 2)
                lhs, rhs = (wk, wq) if n % 2 == 0 else (wv, woT)
                for m in range(2):
                    ins = pe.matmul(bank[n % 2][0:DH, D * m:D * m + D], lhs[o:o + 64, h // 2, DH * m:DH * m + DH],
                                    rhs[o:o + 64, h // 2, :], start=True, stop=True)
                ins.then_inc(s_pg, 1)
            pe.wait_ge(s_wprep, 1)
            for g in range(12):
                if g == 0:
                    pe.wait_ge(s_eg, 2 + 2 * NH)
                if g >= 2:
                    pe.wait_ge(s_wtout, g - 1)
                for kk in range(2):
                    k = 2 * g + kk
                    dr, s, c = k // 6 - 1, k // 3 % 2, k % 3
                    y0 = 8 * ((dr + 1) % 2)
                    for m in range(2):
                        ins = pe.transpose(bank[g % 2][:, D * kk + DH * m:D * kk + DH * m + DH],
                                           wv5[:, m, y0:y0 + 8, :, CH * part_of(dr, s) + c], ident[0:DH, 0:DH])
                ins.then_inc(s_wt, 1)
            pe.wait_ge(s_vb, 1)
            for k in range(2):
                for m in range(2):
                    ins = pe.matmul(bank[2][:, D * k + DH * m:D * k + DH * m + DH], vb[:, k, m, :],
                                    ident[0:DH, 0:DH], start=True, stop=True)
            ins.then_inc(s_row, 1)

            def img_t(g):
                if g >= 2:
                    pe.wait_ge(s_itout, g - 1)
                r, m = g // 4, g % 4
                pe.wait_ge(s_strip, r + 1)
                for c in range(CH):
                    ins = pe.transpose(bank[3 + g % 2][:, P * c:P * c + P], strip[r % 2][:, c, m, :], ident[:])
                ins.then_inc(s_it, 1)

            def patch(p):
                i, j = p // 3, p % 3
                pe.wait_ge(s_itout, min(32, 8 * i + 16))
                if p == 0:
                    pe.wait_ge(s_wtout, 12 + 1)
                if p >= 2:
                    pe.wait_ge(s_patout, p - 1)
                for k in range(24):
                    dr, s, c = k // 6, k // 3 % 2, k % 3
                    ins = pe.matmul(bank[5 + p % 2][:, 0:193], imgT[:, 2 * i + dr, j + s, c, :], wcT[:, k, :],
                                    start=(k == 0), stop=(k == 23))
                ins.then_inc(s_pat, 1)

            for g in range(16):
                img_t(g)
            for i in range(3):
                for j in range(3):
                    if i < 2 and j < 2:
                        for g in range(16 + 8 * i + 4 * j, 20 + 8 * i + 4 * j):
                            img_t(g)
                    patch(3 * i + j)

            pe.wait_ge(s_x0n, 2)
            for m in range(2):
                ins = pe.transpose(bank[0][0:DH, P * m:P * m + P], x0n[0][:, DH * m:DH * m + DH], ident[:])
            for m in range(2):
                ins = pe.transpose(bank[1][0:DH, P * m:P * m + NPATCH], x0n[1][0:NPATCH, DH * m:DH * m + DH],
                                   ident[0:NPATCH, 0:NPATCH])
            ins.then_inc(s_x0t, 1)
            pe.wait_ge(s_x0T, 2)
            for m in range(2):
                ins = pe.matmul(bank[2][0:NH, 0:SPAD], wgT[:, m, :], x0T[:, m, :], start=(m == 0), stop=(m == 1))
            ins.then_inc(s_g8, 1)
            for n in range(2 * NH):
                h, src = n // 2, (gT, hT)[n % 2]
                if n >= 4:
                    pe.wait_ge((s_kvout, s_vvout)[n % 2], h - 1)
                for m in range(2):
                    for k in range(2):
                        ins = pe.matmul(bank[4 + h % 2 + 2 * (n % 2)][0:DH, SPAD * m:SPAD * m + SPAD],
                                        src[:, k, h, DH * m:DH * m + DH], x0T[:, k, :], start=(k == 0), stop=(k == 1))
                ins.then_inc(s_kv, 1)

            def turn(tiles, nt, ready, c, done):
                for k in range(-(-nt // 2)):
                    pe.wait_ge(ready, 4 * c + min(2 * k + 2, nt))
                    for jj in range(min(2, nt - 2 * k)):
                        for m in range(2):
                            ins = pe.transpose(bank[1 + k][0:DH, 256 * m + P * jj:256 * m + P * jj + P],
                                               tiles[2 * k + jj][:, DH * m:DH * m + DH], ident[:])
                    ins.then_inc(done, 1)

            def route(c, par, nt):
                turn(xf[par], nt, s_xf, c, s_t2)
                for j in range(nt):
                    if j % 2 == 0:
                        pe.wait_ge(s_xfT, 2 * c + j // 2 + 1)
                    for m in range(2):
                        ins = pe.matmul(bank[3][:, 8 * j:8 * j + 8], xfT[:, m, P * j:P * j + P], rws[:, m, :],
                                        start=(m == 0), stop=(m == 1))
                ins.then_inc(s_lg, 1)

            def ranks(c, nt):
                pe.wait_ge(s_e, c + 1)
                w = 8 * nt
                pe.matmul(bank[3][:, 64:64 + w], ltri[:], eb[:, 0:nt, :], start=True, stop=False)
                pe.matmul(bank[3][:, 64:64 + w], onesb[:], ecum[:, 0:nt, :], start=False, stop=True).then_inc(s_pf, 1)

            def chunk(c, par, nt, prev, nxt, first=False):
                w = P * nt
                pe.wait_ge(s_kc, c + 1)
                pe.wait_ge(s_xT, 2 * c + (nt + 1) // 2)
                for m in range(2):
                    ins = pe.matmul(bank[0][:, 0:w], kc[:, m, :], xT[:, m, 0:w], start=(m == 0), stop=(m == 1))
                ins.then_inc(s_sc, 1)
                for k in range(4):
                    ins = pe.transpose(bank[7][:, DH * k:DH * k + DH], kc[:, k, :], ident[0:DH, 0:DH])
                ins.then_inc(s_rt, 1)
                if prev:
                    route(c - 1, 1 - par, prev)
                pe.wait_ge(s_sm, c + 1)
                pe.wait_ge(s_cr, c + 1)
                pe.wait_ge(s_ns, c + 1)
                for j in range(nt):
                    o = bank[5 + j // 2][:, D * (j % 2):D * (j % 2) + D]
                    for m in range(2):
                        pe.matmul(o, xT[:, m, P * j:P * j + P], nst[:, m, :], start=(m == 0), stop=False)
                    pe.matmul(o, sm[:, P * j:P * j + P], crow[:], start=False, stop=True).then_inc(s_o, 1)
                if prev:
                    ranks(c - 1, prev)
                pe.wait_ge(s_ar, c + 1)
                for m in range(2):
                    ins = pe.matmul(bank[4][0:DH, D * m:D * m + D], arow[:, DH * m:DH * m + DH], crow[:],
                                    start=True, stop=True)
                ins.then_inc(s_nu, 1)
                if nxt:
                    turn(xn, nxt, s_xn, c + 1, s_t)

            turn(xn, 4, s_xn, 0, s_t)
            chunk(0, 0, 4, 0, 4)
            chunk(1, 1, 4, 4, 4)
            chunk(2, 0, 4, 4, 4)
            with pe.Fori(0, 3) as i:
                chunk(2 * i + 3, 1, 4, 4, 4)
                chunk(2 * i + 4, 0, 4, 4, 4)
            chunk(9, 1, 4, 4, 1)
            chunk(10, 0, 1, 4, 0)
            route(10, 0, 1)
            ranks(10, 1)
            pe.wait_ge(s_pos, CHUNKS)
            pe.matmul(bank[3][:, 128:136], onesb[:], ecum[:, 4, :], start=True, stop=True).then_inc(s_cread, 1)

            pe.wait_ge(s_rawg, 32)
            pe.wait_ge(s_rawd, 32)
            pe.wait_ge(s_tab, 1)
            for n in range(44):
                if n >= 4:
                    pe.wait_ge(s_eout[n % 2], (n - 4) // 2 + 1)
                if n == 24:
                    for p in range(2):
                        for j in range(4):
                            pe.wait_ge(s_scat[p][j], 32 * len([c for c in range(p, CHUNKS, 2) if 4 * c + j < TILES]))
                b = bank[n % 4]
                if n < 32:
                    e, which, m = n // 4, n // 2 % 2, n % 2
                    for c in range(FC):
                        ins = pe.transpose(b[0:DH, P * c:P * c + P], (raw_g, raw_u)[which][:, FC * e + c, DH * m:DH * m + DH],
                                           ident[:])
                else:
                    for kk in range(2):
                        g = 2 * (n - 32) + kk
                        for m in range(2):
                            ins = pe.transpose(b[:, D * kk + DH * m:D * kk + DH * m + DH],
                                               raw_d[:, m, g // FC, P * (g % FC):P * (g % FC) + P], ident[0:DH, 0:DH])
                ins.then_inc(s_et, 1)
            pe.wait_ge(s_eout[0], 22)
            pe.wait_ge(s_eout[1], 22)

            def turn_in(s, b, half=None):
                pe.wait_ge(s_xs[b], 16 * half)
                for m in range(2):
                    ins = pe.transpose(bank[5][0:DH, P * m:P * m + P], xs[b][:, DH * m:DH * m + DH], ident[:])
                ins.then_inc(s_xst, 1)

            expert_reg = [pe.alloc_register(f"expert{b}") for b in range(2)]

            def load_expert(s, b):
                pe.reg_load(expert_reg[b], tab[0:1, 1, bass.ds(s, 1)])

            def gate_up(s, b):
                e = pe.snap(expert_reg[b], min_val=0, max_val=NE - 1)
                pe.wait_ge(s_xsT, s + 1)
                wflat = w_gu[:].rearrange("p m e f -> p m (e f)")
                for which in range(2):
                    for m in range(2):
                        ins = pe.matmul(bank[2 * b + which][:, 0:DE], xsT[b][:, m, :],
                                        wflat[:, m, bass.ds(e * (2 * DE) + DE * which, DE)], start=(m == 0), stop=(m == 1))
                ins.then_inc(s_gu, 1)

            def turn_hidden(s, b):
                pe.wait_ge(s_hh, s + 1)
                for c in range(FC):
                    ins = pe.transpose(bank[4][:, P * c:P * c + P], hh[b][:, P * c:P * c + P], ident[:])
                ins.then_inc(s_ht, 1)

            def down(s, b):
                e = pe.snap(expert_reg[b], min_val=0, max_val=NE - 1)
                pe.wait_ge(s_hhT, s + 1)
                dflat = w_dn[:].rearrange("p e c d -> p (e c d)")
                for c in range(FC):
                    ins = pe.matmul(bank[6 + b][:, 0:D], hhT[b][:, c, :], dflat[:, bass.ds(e * (FC * D) + c * D, D)],
                                    start=(c == 0), stop=(c == FC - 1))
                ins.then_inc(s_dn, 1)

            load_expert(0, 0)
            load_expert(1, 1)
            turn_in(0, 0, 1)
            gate_up(0, 0)
            turn_in(1, 1, 1)
            with pe.Fori(0, SLOTS // 2 - 1) as i:
                for b in range(2):
                    gate_up(2 * i + 1 + b, 1 - b)
                    turn_hidden(2 * i + b, b)
                    turn_in(2 * i + 2 + b, b, i + 2)
                    down(2 * i + b, b)
                    load_expert(2 * i + 2 + b, b)
            gate_up(SLOTS - 1, 1)
            turn_hidden(SLOTS - 2, 0)
            down(SLOTS - 2, 0)
            turn_hidden(SLOTS - 1, 1)
            down(SLOTS - 1, 1)

        @block.vector
        def _(v):
            st = Steps(v, s_dve)
            for k in s_ys + s_out:
                v.sem_inc(k, 16)
            for ih in range(2):
                v.memset(img[64 * ih:64 * ih + 64, :, 56 * ih:56 * ih + 8, :], 0.0)
                for jh in range(2):
                    a, r0 = 64 * ih + 32 * jh, 8 - 8 * ih
                    ins = v.memset(img[a:a + 32, :, r0:r0 + 56, 56 * jh:56 * jh + 8], 0.0)
            ins.then_inc(s_border, 1)
            v.wait_ge(s_wraw, 16)
            v.wait_ge(s_bet, 16)
            for m in range(2):
                st.link(v.tensor_tensor_reduce(junk[:], wraw[:, m, :], bet[:], 1.0, 0.0, ALU.mult, ALU.add,
                                               colsum[:, 1, m:m + 1]))
            v.wait_ge(s_gam, 16)
            for m in range(2):
                st.link(v.tensor_tensor_reduce(wraw[:, m, :], wraw[:, m, :], gam[:], 1.0, 0.0, ALU.mult, ALU.add,
                                               colsum[:, 0, m:m + 1]))
            for m in range(2):
                for dr in range(2):
                    for s in range(2):
                        px, ox = (8, 0) if s == 0 else (0, 8)
                        y0 = 8 * ((dr + 1) % 2)
                        k = CH * part_of(dr, s)
                        dst = wv5[:, m, y0:y0 + 8, px:px + 8, k:k + CH]
                        st.mark(v.tensor_tensor(dst, dst, wv5[:, m, 8 * dr:8 * dr + 8, ox:ox + 8, 0:CH], ALU.add))
            v.wait_ge(s_par, 16 * 6)
            st.mark(v.tensor_tensor(colsum[:, 1, :], colsum[:, 1, :], biasc[:], ALU.add))
            st.wait()
            v.memset(vb[:], 1.0).then_inc(s_wprep, 1)
            v.wait_ge(s_wprep, 1)
            for k in range(2):
                for m in range(2):
                    st.mark(v.tensor_scalar(vb[:, k, m, :], vb[:, k, m, :], colsum[:, k, m:m + 1], None, ALU.mult))
            st.wait()
            for m in range(2):
                st.mark(v.tensor_scalar(rws[:, m, :], rwT[:, m, :], nwc[:, m:m + 1], None, ALU.mult))
            v.memset(ecum[:], 0.0).then_inc(s_vb, 1)
            v.wait_ge(s_row, 1)
            st.mark(v.tensor_copy(sumwb[:], bank[2][:, 0:D]))
            st.mark(v.tensor_copy(constb[:], bank[2][:, D:2 * D]))
            v.wait_ge(s_cst, 16)
            v.wait_ge(s_wt, 12)
            v.tensor_copy(wcT[:, :, D:D + 1], cst[:, C_STAT:C_STAT + 24].unsqueeze(2)).then_inc(s_wtout, 1)

            def img_out(g):
                v.wait_ge(s_it, g + 1)
                v.tensor_copy(imgT[:, g // 4, g % 4, :, :],
                              bank[3 + g % 2][:, 0:CH * P].rearrange("p (c t) -> p c t", c=CH)).then_inc(s_itout, 1)

            def patch_out(p):
                i, j = p // 3, p % 3
                acc = bank[5 + p % 2]
                mean, var, q, rs = (sd2[:, 25 + k:26 + k] for k in range(4))
                v.wait_ge(s_pat, p + 1)
                v.wait_ge(s_sq, 2 * p + 2)
                st.mark(v.tensor_scalar(mean, acc[:, D:D + 1], -1.0 / PFEAT, None, ALU.mult))
                st.link(v.tensor_tensor(var, sc[:, p:p + 1], sc[:, 9 + p:10 + p], ALU.add))
                st.link(v.tensor_tensor(q, mean, mean, ALU.mult))
                st.link(v.tensor_scalar(var, var, 1.0 / PFEAT, LN_EPS, ALU.mult, ALU.add))
                v.tensor_tensor(sd2[:, 16 + p:17 + p], var, q, ALU.subtract).then_inc(s_pv, 1)
                t = tmp[p % 2]
                v.scalar_tensor_tensor(out=t[:], in0=sumwb[:], scalar=mean, in1=acc[:, 0:D],
                                       op0=ALU.mult, op1=ALU.add).then_inc(s_patout, 1)
                v.wait_ge(s_patout, p + 1)
                v.wait_ge(s_psd, p + 1)
                st.link(v.reciprocal(rs, sd2[:, p:p + 1]))
                for q4 in range(4):
                    tt = GRID * (3 * (q4 // 2) + i) + 3 * (q4 % 2) + j
                    a, o = 32 * q4, 32 * (tt % TQ)
                    ins = v.scalar_tensor_tensor(out=hres3[o:o + 32, tt // TQ, :], in0=t[a:a + 32, :],
                                                 scalar=rs[a:a + 32, :], in1=constb[a:a + 32, :],
                                                 op0=ALU.mult, op1=ALU.add)
                ins.then_inc(s_ptok, 1)

            for g in range(16):
                img_out(g)
            for i in range(3):
                for j in range(3):
                    if i < 2 and j < 2:
                        for g in range(16 + 8 * i + 4 * j, 20 + 8 * i + 4 * j):
                            img_out(g)
                    if 3 * i + j:
                        patch_out(3 * i + j - 1)
            patch_out(8)

            v.wait_ge(s_x0, 16 * 5)
            v.memset(x0T[:, :, SEQ:SPAD], 0.0)
            rows = (P, NPATCH)
            st.mark(v.memset(zrow[:], 0.0))
            st.mark(v.memset(sd2[:], 1.0))
            for k in range(2):
                st.mark(v.bn_stats(stats[0:rows[k], k, :], x0[k][0:rows[k], :]))
            st.wait()
            for k in range(2):
                st.mark(v.bn_aggr(mv[0:rows[k], k, :], stats[0:rows[k], k, :]))
            st.wait()
            for k in range(2):
                ins = v.tensor_scalar(sd2[0:rows[k], 16 + k:17 + k], mv[0:rows[k], k, 1:2], LN_EPS, None, ALU.add)
            ins.then_inc(s_v0, 1)
            v.wait_ge(s_sd0, 1)
            st.link(v.reciprocal(sd2[:, 4:6], sd2[:, 0:2]))
            for k in range(2):
                v.tensor_scalar(x0n[k][0:rows[k], :], x0[k][0:rows[k], :], mv[0:rows[k], k, 0:1],
                                sd2[0:rows[k], 4 + k:5 + k], ALU.subtract, ALU.mult).then_inc(s_x0n, 1)
            v.wait_ge(s_x0t, 1)
            for m in range(2):
                ins = v.tensor_copy(x0T[:, m, 0:NPATCH].rearrange("p (n q) -> p q n", q=TQ),
                                    bank[1][0:DH, P * m:P * m + NPATCH].rearrange("p (q n) -> p q n", q=TQ))
            ins.then_inc(s_x0T, 1)
            for h in range(NH):
                v.wait_ge(s_kv, 2 * h + 2)
                v.tensor_copy(valsT[:, :, :, CHUNK * h:CHUNK * h + CHUNK],
                              bank[6 + h % 2][0:DH, 0:2 * SPAD].rearrange("p (m c s) -> p m c s", m=2, s=CHUNK)
                              ).then_inc(s_vvout, 1)
            v.wait_ge(s_kg, 16 * NH)
            st.mark(v.tensor_tensor(kgate[:], kgate[:], cst[:, C_KEY:C_KEY + CHUNKS], ALU.mult))
            v.memset(nst[:], 0.0).then_inc(s_ns, 1)
            v.wait_ge(s_ns, 1)

            def ln1(c, nt, first=False):
                for j in range(nt):
                    st.mark(v.bn_stats(stats[:, j, :], hres[:, bass.ds((4 * c + j) * D, D)]))
                st.wait_apart()
                for j in range(nt):
                    st.mark(v.bn_aggr(mv[:, j, :], stats[:, j, :]))
                st.wait()
                v.tensor_scalar(sc[:, 0:nt], mv[:, 0:nt, 1], LN_EPS, None, ALU.add).then_inc(s_v1, 1)
                v.wait_ge(s_sd1, c + 1)
                if not first:
                    v.wait_ge(s_t, 2 * c)
                st.link(v.reciprocal(sc[:, 8:8 + nt], sc[:, 4:4 + nt]))
                st.mark(v.tensor_scalar(sc[:, 16:16 + nt], sc[:, 8:8 + nt], 1.0, None, ALU.add))
                v.scalar_tensor_tensor(out=sc[:, 12:12 + nt], in0=mv[:, 0:nt, 0], scalar=-1.0, in1=sc[:, 8:8 + nt],
                                       op0=ALU.mult, op1=ALU.mult).then_inc(s_r1, 1)
                v.wait_ge(s_r1, c + 1)
                for j in range(nt):
                    t = hres[:, bass.ds((4 * c + j) * D, D)]
                    v.wait_ge(s_xn, 4 * c + j + 1)
                    st.mark(v.tensor_scalar(t, t, sc[:, 16 + j:17 + j], sc[:, 12 + j:13 + j], ALU.mult, ALU.add))

            def attend(c, nt, first=False):
                w = P * nt
                v.wait_ge(s_sc, c + 1)
                v.tensor_tensor(sm[:, 0:w].rearrange("p (t b) -> p t b", b=B),
                                bank[0][:, 0:w].rearrange("p (t b) -> p t b", b=B),
                                cst[:, C_MASK:C_MASK + TQ * nt].unsqueeze(2).to_broadcast([P, TQ * nt, B]),
                                ALU.mult).then_inc(s_sm, 1)

            def picks(c, par, nt):
                v.wait_ge(s_lg, c + 1)
                v.nop(nofuse=True)
                for j in range(nt):
                    st.mark(v.max(t8[:, j, :], bank[3][:, 8 * j:8 * j + 8]))
                st.wait_apart()
                for j in range(nt):
                    st.mark(v.max_index(i8[:, j, :], t8[:, j, :], bank[3][:, 8 * j:8 * j + 8]))
                st.mark(v.tensor_copy(top8[:, bass.ds(c * 32, 8 * nt)], t8[:, 0:nt, :].rearrange("p j e -> p (j e)")))
                st.wait()
                fi = idxf[:, bass.ds(c * 8, 2 * nt)]
                st.link(v.tensor_copy(fi.rearrange("p (j k) -> p j k", k=2), i8[:, 0:nt, 0:2]))
                ohv = oh[:, 0:16 * nt]
                st.link(v.tensor_tensor(ohv.rearrange("p (a e) -> p a e", e=NE),
                                        cst[:, C_EXP:C_EXP + NE].unsqueeze(1).to_broadcast([P, 2 * nt, NE]),
                                        fi.unsqueeze(2).to_broadcast([P, 2 * nt, NE]), ALU.is_equal))
                o4 = ohv.rearrange("p (j k e) -> p j k e", k=2, e=NE)
                st.link(v.tensor_tensor(eb[:, 0:nt, :], o4[:, :, 0, :], o4[:, :, 1, :], ALU.add))
                for j in range(nt - 1):
                    st.link(v.tensor_tensor(ecum[:, j + 1, :], ecum[:, j, :], eb[:, j, :], ALU.add))
                v.tensor_tensor(ecum[:, 4, :], ecum[:, nt - 1, :], eb[:, nt - 1, :], ALU.add).then_inc(s_e, 1)

            def places(c, par, nt, wait_e=None):
                v.wait_ge(s_pf, c + 1)
                v.wait_ge(s_e, c + 1)
                st.mark(v.tensor_copy(ecum[:, 0, :], ecum[:, 4, :]))
                fi = idxf[:, bass.ds(c * 8, 2 * nt)]
                rk = rankf[:, bass.ds(c * 8, 2 * nt)]
                st.link(v.tensor_tensor(ohm[:, 0:16 * nt].rearrange("p (j k e) -> p j k e", k=2, e=NE),
                                        oh[:, 0:16 * nt].rearrange("p (j k e) -> p j k e", k=2, e=NE),
                                        bank[3][:, 64:64 + 8 * nt].rearrange("p (j e) -> p j e", e=NE).unsqueeze(2)
                                        .to_broadcast([P, nt, 2, NE]), ALU.mult))
                st.link(v.tensor_reduce(rk, ohm[:, 0:16 * nt].rearrange("p (a e) -> p a e", e=NE), AX.X, ALU.add))
                st.link(v.scalar_tensor_tensor(out=posf[:, 0:2 * nt], in0=fi, scalar=float(REGION), in1=rk,
                                               op0=ALU.mult, op1=ALU.add))
                v.tensor_copy(posu[par][:, 0:2 * nt], posf[:, 0:2 * nt]).then_inc(s_pos, 1)

            def residual(c, nt):
                for j in range(nt):
                    v.wait_ge(s_o, 4 * c + min(j // 2 * 2 + 2, nt))
                    v.scalar_tensor_tensor(out=h2[j][:], in0=bank[5 + j // 2][:, D * (j % 2):D * (j % 2) + D],
                                           scalar=cst[:, bass.ds(4 * c + (j + C_TOK), 1)],
                                           in1=hres[:, bass.ds((4 * c + j) * D, D)], op0=ALU.mult, op1=ALU.add
                                           ).then_inc(s_h2, 1)

            def state(c):
                v.wait_ge(s_nu, c + 1)
                v.tensor_tensor(nst[:], nst[:], bank[4][0:DH, 0:384].rearrange("p (m d) -> p m d", m=2),
                                ALU.add).then_inc(s_ns, 1)

            def ln2(c, nt):
                v.wait_ge(s_h2, 4 * c + nt)
                for j in range(nt):
                    st.mark(v.bn_stats(stats2[:, j, :], h2[j][:]))
                st.wait_apart()
                for j in range(nt):
                    st.mark(v.bn_aggr(mv2[:, j, :], stats2[:, j, :]))
                st.wait()
                st.link(v.tensor_scalar(sd2[:, 0:nt], mv2[:, 0:nt, 1], LN_EPS, None, ALU.add))
                st.link(v.reciprocal(sd2[:, 32:32 + nt], sd2[:, 0:nt]))
                st.link(v.tensor_tensor(sd2[:, 36:36 + nt], mv2[:, 0:nt, 1], sd2[:, 32:32 + nt], ALU.mult))
                v.tensor_scalar(sd2[:, 4:4 + nt], sd2[:, 36:36 + nt], RMS_EPS, None, ALU.add).then_inc(s_v2, 1)
                v.wait_ge(s_sd2, c + 1)
                st.link(v.reciprocal(sd2[:, 16:24], sd2[:, 8:16]))
                st.mark(v.tensor_scalar(sd2[:, 40:40 + nt], sd2[:, 16:16 + nt], 1.0, None, ALU.add))
                st.mark(v.scalar_tensor_tensor(out=sd2[:, 44:44 + nt], in0=mv2[:, 0:nt, 0], scalar=-1.0,
                                               in1=sd2[:, 16:16 + nt], op0=ALU.mult, op1=ALU.mult))
                st.link(v.tensor_tensor(sd2[:, 24:24 + nt], sd2[:, 16:16 + nt], sd2[:, 20:20 + nt], ALU.mult))
                v.scalar_tensor_tensor(out=sd2[:, 28:28 + nt], in0=mv2[:, 0:nt, 0], scalar=-1.0,
                                       in1=sd2[:, 24:24 + nt], op0=ALU.mult, op1=ALU.mult).then_inc(s_s2, 1)
                for j in range(nt):
                    st.mark(v.tensor_scalar(hres[:, bass.ds((4 * c + j) * D, D)], h2[j][:], sd2[:, 40 + j:41 + j],
                                            sd2[:, 44 + j:45 + j], ALU.mult, ALU.add))
                v.wait_ge(s_xf, 4 * c + nt)
                st.wait()

            def chunk(c, par, nt, prev, nxt):
                attend(c, nt)
                if prev:
                    picks(c - 1, 1 - par, prev)
                residual(c, nt)
                if prev:
                    places(c - 1, 1 - par, prev)
                state(c)
                if nxt:
                    ln1(c + 1, nxt)
                ln2(c, nt)

            v.wait_ge(s_txt, 64)
            v.wait_ge(s_x0, 16 * 5)
            ln1(0, 4, True)
            chunk(0, 0, 4, 0, 4)
            chunk(1, 1, 4, 4, 4)
            chunk(2, 0, 4, 4, 4)
            with v.Fori(0, 3) as i:
                st.enter(i, 2 * STEPS_PER_CHUNK)
                chunk(2 * i + 3, 1, 4, 4, 4)
                chunk(2 * i + 4, 0, 4, 4, 4)
            st.leave(3)
            chunk(9, 1, 4, 4, 1)
            chunk(10, 0, 1, 4, 0)
            picks(10, 0, 1)
            places(10, 0, 1)

            v.wait_ge(s_cread, 1)
            cnt, til, cum, fst, one = (ct[:, k, :] for k in range(5))
            st.mark(v.memset(one, 1.0))
            st.mark(v.tensor_scalar(cnt, bank[3][:, 128:136], float(P - 1), None, ALU.add))
            st.link(v.tensor_copy(cti[:, 1, :], bank[3][:, 128:136]))
            st.link(v.tensor_copy(cti[:, 0, :], cnt))
            st.link(v.tensor_scalar(cti[:, 0, :], cti[:, 0, :], 7, None, ALU.arith_shift_right))
            st.link(v.tensor_copy(til, cti[:, 0, :]))
            st.link(v.tensor_tensor_scan(cum, one, til, 0.0, ALU.mult, ALU.add))
            st.link(v.tensor_tensor(fst, cum, til, ALU.subtract))
            sl = cst[:, C_SLOT:C_SLOT + SLOTS]
            past = tabf[:]
            st.link(v.tensor_tensor(past, sl.unsqueeze(2).to_broadcast([P, SLOTS, NE]),
                                    cum.unsqueeze(1).to_broadcast([P, SLOTS, NE]), ALU.is_ge))
            st.link(v.tensor_reduce(slotf[:, 0, :], past, AX.X, ALU.add))
            st.link(v.tensor_tensor(past, past, til.unsqueeze(1).to_broadcast([P, SLOTS, NE]), ALU.mult))
            st.link(v.tensor_reduce(slotf[:, 1, :], past, AX.X, ALU.add))
            st.link(v.tensor_tensor(slotf[:, 1, :], sl, slotf[:, 1, :], ALU.subtract))
            st.link(v.tensor_scalar(slotf[:, 2, :], slotf[:, 0, :], float(REGION // P), None, ALU.mult))
            st.link(v.tensor_tensor(slotf[:, 1, :], slotf[:, 1, :], slotf[:, 2, :], ALU.add))
            st.link(v.tensor_scalar(slotf[:, 1, :], slotf[:, 1, :], float(P), float(NE * REGION), ALU.mult, ALU.min))
            st.link(v.tensor_scalar(slotf[:, 0, :], slotf[:, 0, :], float(NE - 1), None, ALU.min))
            st.mark(v.tensor_copy(tab[:, 0, :], slotf[:, 1, :]))
            v.tensor_copy(tab[:, 1, :], slotf[:, 0, :]).then_inc(s_tab, 1)
            st.wait()
            t3 = top8[:].rearrange("p (n e) -> p n e", e=8)
            st.link(v.tensor_copy(esum[:], t3[:, :, 0]))
            v.tensor_tensor(t3, t3, esum[:].unsqueeze(2).to_broadcast([P, TILES, 8]), ALU.subtract).then_inc(s_w, 1)
            for k in range(1):
                st.link(v.tensor_tensor(ypj[:], cst[:, C_EXP:C_EXP + NE].unsqueeze(1).to_broadcast([P, 2 * TILES, NE]),
                                        idxf[:].unsqueeze(2).to_broadcast([P, 2 * TILES, NE]), ALU.is_equal))
                st.link(v.tensor_tensor(ypj[:], ypj[:], fst.unsqueeze(1).to_broadcast([P, 2 * TILES, NE]), ALU.mult))
                st.link(v.tensor_reduce(ypos[:], ypj[:], AX.X, ALU.add))
                st.link(v.scalar_tensor_tensor(out=ypos[:], in0=ypos[:], scalar=float(P), in1=rankf[:],
                                               op0=ALU.mult, op1=ALU.add))
                st.link(v.tensor_copy(yposu[:], ypos[:]))
            experts_out(v, 0)
            v.wait_ge(s_exp, 1)
            st.link(v.tensor_reduce(esum[:], t3, AX.X, ALU.add))
            st.link(v.reciprocal(esum[:], esum[:]))
            st.link(v.tensor_tensor(wts[:].rearrange("p (n k) -> p n k", k=2), t3[:, :, 0:2],
                                    esum[:].unsqueeze(2).to_broadcast([P, TILES, 2]), ALU.mult))

            def turn_out(s, b):
                v.wait_ge(s_xst, s + 1)
                v.tensor_copy(xsT[b][:], bank[5][0:DH, 0:256].rearrange("p (m t) -> p m t", m=2)).then_inc(s_xsT, 1)

            def hidden(s, b):
                v.wait_ge(s_sg, s + 1)
                v.tensor_tensor(hh[b][:], sg[b][:], bank[2 * b + 1][:, 0:DE], ALU.mult).then_inc(s_hh, 1)

            def y_out(s, b, stored=None):
                v.wait_ge(s_dn, s + 1)
                if stored is not None:
                    v.wait_ge(s_ys[b], stored)
                v.tensor_copy(ysb[b][:], bank[6 + b][:, 0:D]).then_inc(s_y, 1)

            turn_out(0, 0)
            hidden(0, 0)
            turn_out(1, 1)
            with v.Fori(0, SLOTS // 2 - 1) as i:
                for b in range(2):
                    hidden(2 * i + 1 + b, 1 - b)
                    turn_out(2 * i + 2 + b, b)
                    y_out(2 * i + b, b, 16 * i + 16)
            hidden(SLOTS - 1, 1)
            y_out(SLOTS - 2, 0, 16 * (SLOTS // 2))
            y_out(SLOTS - 1, 1, 16 * (SLOTS // 2))

            def index(n, j):
                v.tensor_copy(ygi[j][:], yposu[:, bass.ds(2 * n, 2)]).then_inc(s_ygi, 1)

            def combine(n, j, k, stored):
                v.wait_ge(s_yg[j], 32 * k)
                v.scalar_tensor_tensor(out=oacc[j][:], in0=yg[j][0][:], scalar=wts[:, bass.ds(2 * n, 1)],
                                       in1=hres[:, bass.ds(n * D, D)], op0=ALU.mult, op1=ALU.add).then_inc(s_h2, 1)
                v.wait_ge(s_h2, TILES + 1 + n)
                if stored is not None:
                    v.wait_ge(s_out[j], stored)
                v.scalar_tensor_tensor(out=ofin[j][:], in0=yg[j][1][:], scalar=wts[:, bass.ds(2 * n + 1, 1)],
                                       in1=oacc[j][:], op0=ALU.mult, op1=ALU.add).then_inc(s_fin, 1)

            for j in range(4):
                index(j, j)
            with v.Fori(0, TILES // 4 - 1) as i:
                for j in range(4):
                    combine(4 * i + j, j, i + 1, 16 * i + 16)
                    index(4 * i + 4 + j, j)
            for j in range(4):
                combine(TILES - 5 + j, j, TILES // 4, 16 * (TILES // 4))
                if j == 0:
                    index(TILES - 1, 0)
            combine(TILES - 1, 0, TILES // 4 + 1, 16 * (TILES // 4) + 16)


STEPS_PER_CHUNK = 52

_INS = ['x', 'txt', 'L0_tok_ln_gamma', 'L0_tok_ln_beta', 'L0_tok_W', 'L0_tok_b', 'L0_attn_w_key', 'L0_attn_w_value',
        'L0_attn_w_query', 'L0_attn_w_gate', 'L0_attn_w_out', 'L0_ffn_norm_w', 'L0_ffn_router_w', 'L0_ffn_gate_w',
        'L0_ffn_up_w', 'L0_ffn_down_w']


def shape_constants():
    import numpy as np

    c = np.zeros((P, C_ALL), np.float64)
    p = np.arange(P)
    step = p % CHUNK
    for k in range(CHUNKS):
        c[:, C_KEY + k] = WRITE * DECAY ** (-1.0 - (CHUNK * k + step))
    for n in range(TILES):
        c[:, C_TOK + n] = DECAY ** (TQ * n + p // B)
    c[:, C_MASK:C_MASK + CHUNK] = step[:, None] < np.arange(CHUNK)[None]
    right = (p % 16) >= 8
    for k in range(24):
        dr, s = k // 6 - 1, k // 3 % 2
        inner = (right if s == 0 else ~right) if dr in (0, 1) else np.zeros(P, bool)
        c[:, C_STAT + k] = 1.0 + inner
    c[:, C_EXP:C_EXP + NE] = np.arange(NE)
    c[:, C_SLOT:C_SLOT + SLOTS] = np.arange(SLOTS)
    return c.astype(np.float32)


def kernel(**inputs):
    import numpy as np
    import concourse.bacc as bacc
    from concourse.bass_utils import run_bass_kernel_spmd

    nc = bacc.Bacc("TRN2", target_bir_lowering=False, num_devices=1)
    arrays, args = {}, []
    for name in _INS:
        a = np.ascontiguousarray(inputs[name])
        arrays[f"in_{name}"] = a
        args.append(nc.dram_tensor(f"in_{name}", a.shape, mybir.dt.from_np(a.dtype), kind="ExternalInput").ap())
    arrays["in_consts"] = shape_constants()
    args.append(nc.dram_tensor("in_consts", (P, C_ALL), F32, kind="ExternalInput").ap())
    args.append(nc.dram_tensor("out_0", (B, SEQ, D), F32, kind="ExternalOutput").ap())
    build(nc, *args)
    r = run_bass_kernel_spmd(nc, [arrays], core_ids=[0])
    return r.results[0]["out_0"]
```

```python
from contextlib import ExitStack

import concourse.bass as bass
from concourse import mybir

ALU = mybir.AluOpType
ACT = mybir.ActivationFunctionType
AX = mybir.AxisListType
F32 = mybir.dt.float32
F32R = mybir.dt.float32r
BF16 = mybir.dt.bfloat16
I32 = mybir.dt.int32
U32 = mybir.dt.uint32

P = 128
B = 32
D = 192
DH = 96
GRID = 6
NPATCH = GRID * GRID
CH = 3
PARTS = 5
PFEAT = 16 * 16 * PARTS * CH
SEQ = 164
TQ = 4
TILES = SEQ // TQ
PTILES = NPATCH // TQ
CHUNK = 16
CT_TILES = CHUNK // TQ
CHUNKS = -(-SEQ // CHUNK)
NH = 8
DK = 64
SPAD = CHUNKS * CHUNK
NE = 8
DE = 384
FC = DE // P
REGION = TILES * P + P
SLOTS = TILES * 2 + NE
TAB = SLOTS + 2
D1 = P
D2 = D - P
LN_EPS = 1e-5
RMS_EPS = 1e-6
DECAY = 0.95
WRITE = 0.1

C_KEY, C_TOK = 0, CHUNKS
C_MASK = C_TOK + TILES
C_STAT = C_MASK + CHUNK
C_EXP = C_STAT + 24
C_SLOT = C_EXP + NE
C_ALL = C_SLOT + TAB


class Steps:

    def __init__(self, eng, sem):
        self.eng, self.sem, self.base, self.n = eng, sem, 0, 0

    def mark(self, ins):
        self.n += 1
        return ins.then_inc(self.sem, 1)

    def wait(self):
        self.eng.wait_ge(self.sem, self.base + self.n)

    def wait_apart(self):
        self.wait()
        self.eng.nop(nofuse=True)

    def link(self, ins):
        self.mark(ins)
        self.wait()

    def enter(self, trip, per_trip):
        self.start, self.per = self.base + self.n, per_trip
        self.base, self.n = trip * per_trip + self.start, 0

    def leave(self, trips):
        assert self.n == self.per, (self.n, self.per)
        self.base, self.n = self.start + trips * self.per, 0


def build(nc, x, txt, gamma, beta, W, bias, w_key, w_value, w_query, w_gate, w_out,
          norm_w, router_w, gate_w, up_w, down_w, consts, out):
    with ExitStack() as ctx:
        ctx.enter_context(nc.allow_non_contiguous_dma("small transposed parameters"))
        base0 = nc.sbuf_base + (-nc.sbuf_base) % 64
        top = [base0]

        def at(name, shape, dt, offset):
            return nc.alloc_sbuf_tensor_at(name, shape, dt, offset=offset)

        def room(nbytes):
            a = top[0]
            top[0] = a + nbytes + (-nbytes) % 32
            assert top[0] <= nc.sbuf_usable_end, (name_of, top[0])
            return a

        name_of = "sbuf"

        def sb(name, shape, dt=F32):
            n = 4 if dt != BF16 else 2
            for s in shape[1:]:
                n *= s
            return at(name, shape, dt, room(n))

        def sem(name):
            return ctx.enter_context(nc.semaphore(name))

        r_img = room(CH * 64 * 64 * 4)
        r_xt = room(CH * 64 * 64 * 4)
        r_wc = room(24 * 193 * 4)
        r_hres = room(TILES * D * 4)
        r_gh = room(2 * 2 * NH * D * 4)
        img = at("img", [P, CH, 64, 64], F32, r_img)
        wa_h = at("wa_h", [P, NE * 2 * DE], F32R, r_img)
        wa_l = at("wa_l", [P, NE * 2 * DE], F32R, r_img + NE * 2 * DE * 4)
        wraw = at("wraw", [DH, 2, PFEAT], F32, r_xt)
        gam = at("gam", [DH, PFEAT], F32, r_xt + 2 * PFEAT * 4)
        imgT = at("imgT", [P, 8, 4, CH, P], F32, r_xt)
        raw_u = at("raw_u", [P, NE * FC, D], F32, r_xt)
        raw_g = at("raw_g", [P, NE * FC, D], F32, r_xt + NE * FC * D * 4)
        wd_l = at("wd_l", [P, NE * FC * D], F32R, r_xt)
        r_tail = r_xt + 2 * NE * FC * D * 4
        wk = at("wk", [P, 4, D], F32, r_wc)
        wq = at("wq", [P, 4, D], F32, r_wc + 3072)
        wv = at("wv", [P, 4, D], F32, r_wc + 6144)
        woraw = at("woraw", [DH, 2, NH * DK], F32, r_wc + 9216)
        woT = at("woT", [P, 4, D], F32, r_wc + 13312)
        wcT = at("wcT", [P, 24, 193], F32, r_wc)
        wd_h = at("wd_h", [P, NE * FC * D], F32R, r_wc)
        bet = at("bet", [DH, PFEAT], F32, r_hres)
        junk = at("junk", [DH, PFEAT], F32, r_hres + PFEAT * 4)
        hres = at("hres", [P, TILES * D], F32, r_hres)
        gT = at("gT", [DH, 2, NH, D], F32, r_gh)
        hT = at("hT", [DH, 2, NH, D], F32, r_gh + 2 * NH * D * 4)
        wb = at("wb", [P, NE * 2 * DE], F32R, r_gh)
        xT = at("xT", [DH, 2, 512], F32, r_tail)
        xfT = at("xfT", [DH, 2, 512], F32, r_tail + 4096)
        sm = at("sm", [P, 512], F32, r_tail + 8192)
        r_act = room(2 * 2 * SPAD * NH * 4)
        keysT = at("keysT", [DH, 2, CHUNKS, P], F32, r_act)
        valsT = at("valsT", [DH, 2, CHUNKS, P], F32, r_act + 2 * SPAD * NH * 4)
        sqjunk = at("sqjunk", [P, CH, 32, 32], BF16, r_act)
        strip = [at(f"strip{i}", [P, CH, 4, P], F32, r_act + 6144 + 6144 * i) for i in range(2)]
        raw_d1 = at("raw_d1", [D1, NE, DE], F32, r_tail)
        raw_d2 = at("raw_d2", [D2, NE, DE], F32, r_act)
        xs = [at(f"xs{i}", [P, 2 * P], F32, r_act + 12288 + 1024 * i) for i in range(2)]
        r_ffn = r_xt + NE * FC * D * 4
        xh = [at(f"xh{i}", [P, 2 * P], F32R, r_ffn + 1024 * i) for i in range(2)]
        xl = [at(f"xl{i}", [P, 2 * P], F32R, r_ffn + 2048 + 1024 * i) for i in range(2)]
        sg = [at(f"sg{i}", [P, DE], F32, r_ffn + 4096 + 1536 * i) for i in range(2)]
        hh = [at(f"hh{i}", [P, DE], F32, r_ffn + 7168 + 1536 * i) for i in range(2)]
        hth = [at(f"hth{i}", [P, DE], F32R, r_ffn + 10240 + 1536 * i) for i in range(2)]
        htl = [at(f"htl{i}", [P, DE], F32R, r_ffn + 13312 + 1536 * i) for i in range(2)]
        ysb = [at(f"ysb{i}", [P, D], F32, r_ffn + 16384 + 768 * i) for i in range(2)]
        yg = [[at(f"yg{i}_{k}", [P, D], F32, r_act + 768 * (2 * i + k)) for k in range(2)] for i in range(4)]
        ofin = [at(f"ofin{i}", [P, D], F32, r_act + 6144 + 768 * i) for i in range(4)]
        oacc = [at(f"oacc{i}", [P, D], F32, r_act + 9216 + 768 * i) for i in range(4)]

        cst = sb("cst", [P, C_ALL])
        ident = sb("ident", [P, P])
        ltri = sb("ltri", [P, P], BF16)
        onesb = sb("onesb", [P, P], BF16)
        sumwb = sb("sumwb", [P, D])
        constb = sb("constb", [P, D])
        colsum = sb("colsum", [DH, 2, 2])
        biasc = sb("biasc", [DH, 2])
        nwc = sb("nwc", [DH, 2])
        nwab = sb("nwab", [P, 2])
        wgT = sb("wgT", [DH, 2, NH])
        rwT = sb("rwT", [DH, 2, NE])
        rws = sb("rws", [DH, 2, NE])
        g8 = sb("g8", [NH, SPAD])
        kgate = sb("kgate", [P, CHUNKS])
        stats = sb("stats", [P, 4, 6])
        mv = sb("mv", [P, 4, 2])
        sc = sb("sc", [P, 32])
        stats2 = sb("stats2", [P, 4, 6])
        mv2 = sb("mv2", [P, 4, 2])
        sd2 = sb("sd2", [P, 48])
        nst = sb("nst", [DH, 2, D])
        kc = sb("kc", [DH, 4, P])
        top8 = sb("top8", [P, TILES * 8])
        t8 = sb("t8", [P, 4, 8])
        i8 = sb("i8", [P, 4, 8], U32)
        idxf = sb("idxf", [P, TILES * 2])
        rankf = sb("rankf", [P, TILES * 2])
        r_small = room(4 * 1024)
        xn = [at(f"xn{j}", [P, D], F32, r_small + 768 * j) for j in range(4)]
        vb = at("vb", [DH, 2, 2, P], F32, r_small)
        oh = sb("oh", [P, 64])
        ohm = sb("ohm", [P, 64])
        eb = sb("eb", [P, 4, 8], BF16)
        ecum = sb("ecum", [P, 5, 8], BF16)
        posf = sb("posf", [P, 8])
        posu = [sb(f"posu{p}", [P, 8], U32) for p in range(2)]
        arow = sb("arow", [P, D])
        crow = sb("crow", [P, D])
        xf = [[at(f"xf{p}_{j}", [P, D], F32, r_img + 43008 + 768 * (4 * p + j)) for j in range(4)] for p in range(2)]
        h2 = [at(f"h2_{j}", [P, D], F32, r_img + 768 * j) for j in range(4)]
        x0 = [at(f"x0_{j}", [P, D], F32, r_img + 4096 + 768 * j) for j in range(2)]
        x0n = [at(f"x0n_{j}", [P, D], F32, r_img + 6144 + 768 * j) for j in range(2)]
        x0T = at("x0T", [DH, 2, SPAD], F32, r_img + 8192)
        zrow = at("zrow", [P, D], F32, r_small + 3072)
        tmp = [at(f"tmp{i}", [P, D], F32, r_small + 768 * i) for i in range(2)]
        top_small, top[0] = top[0], r_act + 14336
        tab = sb("tab", [P, 2, TAB], I32)
        slotf = sb("slotf", [P, 3, TAB])
        tabf = sb("tabf", [P, TAB, NE])
        ypj = at("ypj", [P, TILES * 2, NE], F32, top[0] - TAB * NE * 4)
        ct = sb("ct", [P, 8, NE])
        cti = sb("cti", [P, 2, NE], I32)
        wts = sb("wts", [P, TILES * 2])
        esum = sb("esum", [P, TILES])
        ypos = sb("ypos", [P, TILES * 2])
        yposu = sb("yposu", [P, TILES * 2], U32)
        assert top[0] <= r_act + 2 * 2 * SPAD * NH * 4
        top[0] = top_small
        ygi = [sb(f"ygi{i}", [P, 2], U32) for i in range(4)]
        print("sbuf left", nc.sbuf_usable_end - top[0])

        disp = nc.dram_tensor("disp", [(NE + 1) * REGION, D], F32, kind="Internal").ap()
        ydram = nc.dram_tensor("ydram", [SLOTS * P, D], F32, kind="Internal").ap()

        bank = [ctx.enter_context(nc.psum_tensor(f"bank{i}", [P, 512], F32)) for i in range(8)]

        s_attw, s_wraw, s_gam, s_bet, s_cst, s_par = (sem(n) for n in (
            "attn_weights_in", "patch_weights_in", "gamma_in", "beta_in", "consts_in", "params_in"))
        s_img, s_border, s_strip, s_txt, s_x0 = (sem(n) for n in ("image_in", "border_zero", "strip_ready", "text_in", "batch0_in"))
        s_rawg, s_rawd = sem("raw_gate_up_in"), sem("raw_down_in")
        s_pool = sem("pool_steps")
        s_dve, s_act = sem("dve_steps"), sem("act_steps")
        s_cons = sem("pool_constants")
        s_pg, s_eg = sem("product_mm"), sem("product_out")
        s_wprep, s_vb, s_row, s_rowout = sem("patch_weights_ready"), sem("row_lhs"), sem("row_mm"), sem("row_out")
        s_wt, s_wtout = sem("wT_mm"), sem("wT_out")
        s_it, s_itout = sem("imgT_mm"), sem("imgT_out")
        s_sq = sem("squares")
        s_pat, s_patout, s_pv, s_psd = sem("patch_mm"), sem("patch_read"), sem("patch_var"), sem("patch_std")
        s_ptok = sem("patch_tokens")
        s_v0, s_sd0, s_x0n, s_x0t, s_x0T = (sem(n) for n in ("var0", "std0", "x0_norm", "x0T_mm", "x0T_out"))
        s_kv, s_kvout, s_vvout, s_g8, s_g8out, s_kg, s_kgr = (sem(n) for n in (
            "kv_mm", "keys_out", "vals_out", "gate_mm", "gate_out", "gate_spread", "gate_ready"))
        s_v1, s_sd1, s_r1, s_xn = sem("var1"), sem("std1"), sem("rstd1"), sem("xn_ready")
        s_t, s_xT = sem("xT_mm"), sem("xT_out")
        s_kc, s_sc, s_sm = sem("keys_copied"), sem("scores_mm"), sem("scores_masked")
        s_rt, s_ar, s_cr = sem("rows_mm"), sem("key_rows"), sem("value_rows")
        s_o, s_h2, s_nu, s_ns = sem("attn_mm"), sem("h2_ready"), sem("state_mm"), sem("state_ready")
        s_v2, s_sd2, s_s2, s_xf = sem("var2"), sem("std2"), sem("rstd2"), sem("xf_ready")
        s_t2, s_xfT, s_lg, s_e, s_pf, s_pos = (sem(n) for n in (
            "xfT_mm", "xfT_out", "logits_mm", "onehots", "prefix_mm", "positions"))
        s_scat = [[sem(f"scattered{p}_{j}") for j in range(4)] for p in range(2)]
        s_et, s_eout = sem("expertT_mm"), [sem("expertT_out_dve"), sem("expertT_out_act")]
        s_cread, s_tab, s_zf = sem("counts_mm"), sem("table"), sem("tail_zeroed")
        s_xs = [sem(f"xs_in{i}") for i in range(2)]
        s_ys = [sem(f"y_stored{i}") for i in range(2)]
        s_xst, s_xh, s_xlo, s_gu, s_sg, s_hh = (sem(n) for n in (
            "xsT_mm", "xsT_high", "xsT_low", "gate_up_mm", "silu", "hidden"))
        s_ht, s_hth, s_htl, s_dn, s_y = (sem(n) for n in (
            "hiddenT_mm", "hiddenT_high", "hiddenT_low", "down_mm", "y_ready"))
        s_exp, s_w, s_yp = sem("softmax_exp"), sem("weights_ready"), sem("y_positions")
        s_ygi = sem("gather_index")
        s_yg = [sem(f"gathered{i}") for i in range(4)]
        s_fin = sem("final_ready")
        s_out = [sem(f"out_stored{i}") for i in range(4)]

        txt_q = txt.rearrange("b (n q) d -> q b n d", q=TQ)
        out_t = out.rearrange("b s d -> s b d")
        hres3 = hres.rearrange("p (n d) -> p n d", d=D)

        block = ctx.enter_context(nc.Block())

        def part_of(dr, s):
            return (1 if s == 0 else 3) if dr <= 0 else (4 if s == 0 else 2)

        wv5 = wraw[:].rearrange("p m (y x c) -> p m y x c", y=16, x=16)

        def pipeline(eng, step, parts, ahead):
            first, last = -max(ahead), SLOTS - 1 - min(ahead)
            lo = -min(ahead) + (-min(ahead)) % 2
            n = (SLOTS - max(ahead) - lo) // 2

            def there(k):
                return "".join(p for p, a in zip(parts, ahead) if 0 <= k + a < SLOTS)

            for k in range(first, lo):
                step(k, k % 2, there(k))
            with eng.Fori(0, n) as i:
                for b in range(2):
                    step(2 * i + (lo + b), b)
            for k in range(lo + 2 * n, last + 1):
                step(k, k % 2, there(k))

        def experts_out(eng, side):
            done = s_eout[side]
            for n in range(32 + 12):
                eng.wait_ge(s_et, n + 1)
                b = bank[n % 4]
                if n < 32:
                    col, half, rows = DE * (n // 2), n % 2, (D1, D2)[n % 2]
                    src, nw = b[0:rows, 0:DE], nwab[0:rows, half:half + 1]
                    hi = (wb if half else wa_h)[0:rows, col:col + DE]
                    lo = wb[D2:P, col:col + DE] if half else wa_l[:, col:col + DE]
                    if side:
                        ins = nc.scalar.activation(hi, src, ACT.Copy, scale=nw)
                    else:
                        eng.wait_ge(s_eout[1], n + 1)
                        ins = nc.vector.scalar_tensor_tensor(out=lo, in0=src, scalar=nw, in1=hi.bitcast(F32),
                                                             op0=ALU.mult, op1=ALU.subtract)
                else:
                    col = 2 * D * (n - 32)
                    hi, lo = wd_h[:, col:col + 2 * D], wd_l[:, col:col + 2 * D]
                    if side:
                        ins = nc.scalar.copy(hi, b[:, 0:2 * D])
                    else:
                        eng.wait_ge(s_eout[1], n + 1)
                        ins = nc.vector.tensor_tensor(lo, b[:, 0:2 * D], hi.bitcast(F32), ALU.subtract)
                ins.then_inc(done, 1)

        @block.sync
        def _(sp):
            sp.dma_start(wraw[:], W.rearrange("(m p) f -> p m f", p=DH)).then_inc(s_wraw, 16)
            sp.dma_start(bet[:], beta.partition_broadcast(DH)).then_inc(s_bet, 16)
            sp.dma_start(gam[:], gamma.partition_broadcast(DH)).then_inc(s_gam, 16)
            for c in range(CH):
                for ih in range(2):
                    for jh in range(2):
                        q = 32 * (2 * ih + jh)
                        r0, c0 = 8 - 8 * ih, 8 - 8 * jh
                        sp.dma_start(img[q:q + 32, c, r0:r0 + 56, c0:c0 + 56],
                                     x[:, c, 40 * ih:40 * ih + 56, 40 * jh:40 * jh + 56]).then_inc(s_img, 16)
            sp.wait_ge(s_wprep, 1)
            for q in range(TQ):
                sp.dma_start(hres3[32 * q:32 * q + 32, PTILES:TILES, :], txt_q[q]).then_inc(s_txt, 16)
            sp.wait_ge(s_it, 32)
            sp.wait_ge(s_sq, 18)
            sp.dma_start(x0[0][:], txt[0]).then_inc(s_x0, 16)
            sp.wait_ge(s_ptok, PTILES)
            for q in range(TQ):
                sp.dma_start(x0[1][PTILES * q:PTILES * q + PTILES, :],
                             hres3[32 * q:32 * q + 1, 0:PTILES, :]).then_inc(s_x0, 16)
            sp.wait_ge(s_pat, PTILES)
            sp.dma_start(raw_g[:], gate_w.rearrange("e (c f) d -> f (e c) d", f=P)).then_inc(s_rawg, 16)
            sp.dma_start(raw_u[:], up_w.rearrange("e (c f) d -> f (e c) d", f=P)).then_inc(s_rawg, 16)
            sp.wait_ge(s_kc, CHUNKS)
            sp.dma_start(raw_d2[:], down_w[:, D1:D].rearrange("e p f -> p e f")).then_inc(s_rawd, 16)
            sp.wait_ge(s_lg, CHUNKS)
            sp.dma_start(raw_d1[:], down_w[:, 0:D1].rearrange("e p f -> p e f")).then_inc(s_rawd, 16)
            sp.wait_ge(s_tab, 1)
            for e in range(NE):
                n = sp.value_load(cti[0:1, 1, e:e + 1], min_val=0, max_val=TILES * P)
                sp.dma_start(disp[bass.ds(n + e * REGION, P), :], zrow[:]).then_inc(s_zf, 16)
            sp.dma_start(disp[NE * REGION:NE * REGION + P, :], zrow[:]).then_inc(s_zf, 16)
            sp.wait_ge(s_zf, 16 * (NE + 1))
            for p in range(2):
                for j in range(4):
                    n = len([c for c in range(p, CHUNKS, 2) if 4 * c + j < TILES])
                    sp.wait_ge(s_scat[p][j], 32 * n)

            def load_slot(s, b, first=False):
                if not first:
                    sp.wait_ge(s_xst, s - 1)
                row = sp.value_load(tab[0:1, 0, bass.ds(s, 1)], min_val=0, max_val=NE * REGION)
                sp.dma_start(xs[b][:, 0:D], disp[bass.ds(row, P), :]).then_inc(s_xs[b], 16)
                sp.dma_start(xs[b][:, D:2 * P], disp[bass.ds(row, P), D1:D]).then_inc(s_xs[b], 16)

            load_slot(0, 0, True)
            load_slot(1, 1, True)
            with sp.Fori(0, SLOTS // 2 - 1) as i:
                for b in range(2):
                    load_slot(2 * i + 2 + b, b)

            def store_out(n, j):
                sp.wait_ge(s_fin, n + 1)
                sp.dma_start(out_t[bass.ds(n * TQ, TQ)], ofin[j][:]).then_inc(s_out[j], 16)

            with sp.Fori(0, TILES // 4) as i:
                for j in range(4):
                    store_out(4 * i + j, j)
            store_out(TILES - 1, 0)
            for j in range(4):
                sp.wait_ge(s_out[j], 16 * len(range(j, TILES, 4)) + 16)

        @block.scalar
        def _(act):
            steps = Steps(act, s_act)
            act.dma_start(wk[:], w_key.rearrange("(c p) d -> p c d", p=P)).then_inc(s_attw, 16)
            act.dma_start(wq[:], w_query.rearrange("(c p) d -> p c d", p=P)).then_inc(s_attw, 16)
            act.dma_start(wv[:], w_value.rearrange("(c p) d -> p c d", p=P)).then_inc(s_attw, 16)
            act.dma_start(woraw[:], w_out.rearrange("(m p) f -> p m f", p=DH)).then_inc(s_attw, 16)
            act.dma_start(cst[:], consts).then_inc(s_cst, 16)
            act.dma_start(biasc[:], bias.rearrange("(m p) -> p m", p=DH)).then_inc(s_par, 16)
            act.dma_start(nwc[:], norm_w.rearrange("(m p) -> p m", p=DH)).then_inc(s_par, 16)
            act.dma_start(nwab[:, 0:1], norm_w[0:D1].unsqueeze(1)).then_inc(s_par, 16)
            act.dma_start(nwab[0:D2, 1:2], norm_w[D1:D].unsqueeze(1)).then_inc(s_par, 16)
            for m in range(2):
                act.dma_start(wgT[:, m, :], w_gate[:, DH * m:DH * m + DH].rearrange("h p -> p h")).then_inc(s_par, 16)
                act.dma_start(rwT[:, m, :], router_w[:, DH * m:DH * m + DH].rearrange("h p -> p h")).then_inc(s_par, 16)

            for k in range(2):
                act.wait_ge(s_pg, k + 1)
                nc.scalar.copy(woT[:, 2 * k:2 * k + 2, :], bank[k][:, 0:384]).then_inc(s_eg, 1)
            for n in range(2 * NH):
                act.wait_ge(s_pg, n + 3)
                dst = (gT if n % 2 == 0 else hT)[:, :, n // 2, :]
                nc.scalar.copy(dst, bank[n % 2][0:DH, 0:384].rearrange("p (m d) -> p m d", m=2)).then_inc(s_eg, 1)
            for g in range(12):
                act.wait_ge(s_wt, g + 1)
                nc.scalar.copy(wcT[:, 2 * g:2 * g + 2, 0:D],
                               bank[g % 2][:, 0:384].rearrange("p (k d) -> p k d", k=2)).then_inc(s_wtout, 1)
            act.wait_ge(s_border, 1)
            act.wait_ge(s_img, 16 * 12)

            def squares(p):
                i, j = p // 3, p % 3
                nc.scalar.activation(sqjunk[:], img[:, :, 16 * i:16 * i + 32, 16 * j:16 * j + 32], ACT.Square,
                                     accum_out=sc[:, p:p + 1]).then_inc(s_sq, 1)
                act.wait_ge(s_sq, 2 * p + 1)
                nc.scalar.activation(sqjunk[:, :, 0:16, 0:16], img[:, :, 16 * i + 8:16 * i + 24, 16 * j + 8:16 * j + 24],
                                     ACT.Square, accum_out=sc[:, 9 + p:10 + p]).then_inc(s_sq, 1)
                act.wait_ge(s_sq, 2 * p + 2)

            for p in range(9):
                squares(p)
            for p in range(9):
                act.wait_ge(s_pv, p + 1)
                nc.scalar.activation(sd2[:, p:p + 1], sd2[:, 16 + p:17 + p], ACT.Sqrt).then_inc(s_psd, 1)
            act.wait_ge(s_v0, 1)
            nc.scalar.activation(sd2[:, 0:2], sd2[:, 16:18], ACT.Sqrt).then_inc(s_sd0, 1)
            act.wait_ge(s_x0t, 1)
            nc.scalar.copy(x0T[:, :, NPATCH:SEQ], bank[0][0:DH, 0:256].rearrange("p (m s) -> p m s", m=2)).then_inc(s_x0T, 1)
            act.wait_ge(s_g8, 1)
            nc.scalar.activation(g8[:].rearrange("h (s c) -> h s c", s=CHUNK),
                                 bank[2][0:NH, 0:SPAD].rearrange("h (c s) -> h s c", s=CHUNK), ACT.Sigmoid).then_inc(s_g8out, 1)
            act.wait_ge(s_g8out, 1)
            for h in range(NH):
                act.dma_start(kgate[CHUNK * h:CHUNK * h + CHUNK, :],
                              g8[h:h + 1, :].rearrange("h (s c) -> h s c", s=CHUNK)).then_inc(s_kg, 16)
            for h in range(NH):
                act.wait_ge(s_kv, 2 * h + 1)
                nc.scalar.copy(keysT[:, :, :, CHUNK * h:CHUNK * h + CHUNK],
                               bank[4 + h % 2][0:DH, 0:2 * SPAD].rearrange("p (m c s) -> p m c s", m=2, s=CHUNK)
                               ).then_inc(s_kvout, 1)
            act.wait_ge(s_ns, 1)

            def ln1(c, nt):
                act.wait_ge(s_v1, c + 1)
                nc.scalar.activation(sc[:, 4:4 + nt], sc[:, 0:nt], ACT.Sqrt).then_inc(s_sd1, 1)
                act.wait_ge(s_r1, c + 1)
                for j in range(nt):
                    nc.scalar.activation(xn[j][:], hres[:, bass.ds((4 * c + j) * D, D)], ACT.Identity,
                                         scale=sc[:, 8 + j:9 + j], bias=sc[:, 12 + j:13 + j]).then_inc(s_xn, 1)

            def xT_out(c, nt):
                for k in range(-(-nt // 2)):
                    act.wait_ge(s_t, 2 * c + k + 1)
                    w = P * min(2, nt - 2 * k)
                    nc.scalar.copy(xT[:, :, 256 * k:256 * k + w],
                                   bank[1 + k][0:DH, :].rearrange("p (m s) -> p m s", m=2)[:, :, 0:w]).then_inc(s_xT, 1)

            def xfT_out(c, nt):
                for k in range(-(-nt // 2)):
                    act.wait_ge(s_t2, 2 * c + k + 1)
                    w = P * min(2, nt - 2 * k)
                    nc.scalar.copy(xfT[:, :, 256 * k:256 * k + w],
                                   bank[1 + k][0:DH, :].rearrange("p (m s) -> p m s", m=2)[:, :, 0:w]).then_inc(s_xfT, 1)

            def ln2(c, par, uses, nt):
                act.wait_ge(s_v2, c + 1)
                nc.scalar.activation(sd2[:, 8:16], sd2[:, 0:8], ACT.Sqrt).then_inc(s_sd2, 1)
                act.wait_ge(s_s2, c + 1)
                for j in range(nt):
                    if uses is not None:
                        act.wait_ge(s_scat[par][j], 32 * uses)
                    nc.scalar.activation(xf[par][j][:], h2[j][:], ACT.Identity,
                                         scale=sd2[:, 24 + j:25 + j], bias=sd2[:, 28 + j:29 + j]).then_inc(s_xf, 1)

            def chunk(c, par, uses, nt, prev, nxt):
                act.wait_ge(s_rt, c + 1)
                nc.scalar.activation(crow[:], bank[7][:, D:2 * D], ACT.Copy, scale=kgate[:, bass.ds(c, 1)]).then_inc(s_cr, 1)
                nc.scalar.copy(arow[:], bank[7][:, 0:D]).then_inc(s_ar, 1)
                if prev:
                    xfT_out(c - 1, prev)
                if nxt:
                    ln1(c + 1, nxt)
                    xT_out(c + 1, nxt)
                ln2(c, par, uses, nt)

            ln1(0, 4)
            xT_out(0, 4)
            chunk(0, 0, None, 4, 0, 4)
            chunk(1, 1, None, 4, 4, 4)
            chunk(2, 0, 1, 4, 4, 4)
            with act.Fori(0, 3) as i:
                chunk(2 * i + 3, 1, i + 1, 4, 4, 4)
                chunk(2 * i + 4, 0, i + 2, 4, 4, 4)
            chunk(9, 1, 4, 4, 4, 1)
            chunk(10, 0, 5, 1, 4, 0)
            xfT_out(10, 1)

            experts_out(act, 1)
            act.wait_ge(s_w, 1)
            nc.scalar.activation(top8[:], top8[:], ACT.Exp).then_inc(s_exp, 1)

            def step(k, b, parts="xsht"):
                if "x" in parts:
                    act.wait_ge(s_xst, k + 3)
                    nc.scalar.copy(xh[b][:], bank[5][:, 0:2 * P]).then_inc(s_xh, 1)
                if "s" in parts:
                    act.wait_ge(s_gu, k + 2)
                    nc.scalar.activation(sg[1 - b][:], bank[2 * (1 - b)][:, 0:DE], ACT.Silu).then_inc(s_sg, 1)
                if "h" in parts:
                    act.wait_ge(s_ht, k + 1)
                    nc.scalar.copy(hth[b][:], bank[4][:, 0:DE]).then_inc(s_hth, 1)
                if "t" in parts:
                    act.wait_ge(s_y, k - 1)
                    act.dma_start(ydram[bass.ds((k - 2) * P, P), :], ysb[b][:]).then_inc(s_ys[b], 16)

            pipeline(act, step, "xsht", (2, 1, 0, -2))

        @block.gpsimd
        def _(pool):
            pool.memset(ident[:], 0.0).then_inc(s_pool, 1)
            pool.memset(onesb[:], 1.0).then_inc(s_pool, 1)
            pool.memset(ltri[:], 1.0).then_inc(s_pool, 1)
            pool.wait_ge(s_pool, 3)
            pool.affine_select(out=ident[:], in_=ident[:], compare_op=ALU.not_equal, fill=1.0, base=0,
                               pattern=[[-1, P]], channel_multiplier=1)
            pool.affine_select(out=ltri[:], in_=ltri[:], compare_op=ALU.is_gt, fill=0.0, base=0,
                               pattern=[[1, P]], channel_multiplier=-1).then_inc(s_cons, 1)

            pool.wait_ge(s_img, 16 * 12)
            pool.wait_ge(s_border, 1)
            for r in range(8):
                if r >= 2:
                    pool.wait_ge(s_it, 4 * (r - 1))
                for c in range(CH):
                    ins = pool.tensor_copy(strip[r % 2][:, c].rearrange("p m (y x) -> p m y x", y=8),
                                           img[:, c, 8 * r:8 * r + 8, :].rearrange("p y (m x) -> p m y x", m=4))
                ins.then_inc(s_strip, 1)

            def keys(c, first=False):
                if not first:
                    pool.wait_ge(s_sc, c)
                    pool.wait_ge(s_rt, c)
                if first:
                    pool.wait_ge(s_kvout, NH)
                    pool.wait_ge(s_vvout, NH)
                for k, t in enumerate((keysT, valsT)):
                    ins = pool.tensor_copy(kc[:, 2 * k:2 * k + 2, :],
                                           t[:].rearrange("p m c s -> p m (c s)")[:, :, bass.ds(c * P, P)])
                ins.then_inc(s_kc, 1)

            def scatter(c, par, nt):
                pool.wait_ge(s_pos, c + 1)
                for j in range(nt):
                    pool.wait_ge(s_xf, 4 * c + j + 1)
                    pool.nop(nofuse=True)
                    for k in range(2):
                        pool.indirect_dma_start(disp, bass.IndirectOffsetOnAxis(
                            ap=posu[par][:, 2 * j + k:2 * j + k + 1], axis=0), xf[par][j][:], None
                            ).then_inc(s_scat[par][j], 16)

            keys(0, True)
            keys(1)
            with pool.Fori(0, 4) as i:
                keys(2 * i + 2)
                scatter(2 * i, 0, 4)
                keys(2 * i + 3)
                scatter(2 * i + 1, 1, 4)
            keys(10)
            scatter(8, 0, 4)
            scatter(9, 1, 4)
            scatter(10, 0, 1)

            for b in range(2):
                pool.wait_ge(s_ys[b], 16 * SLOTS // 2 + 16)

            def gather(n, j, reuse):
                pool.wait_ge(s_ygi, n + 1)
                if reuse is not None:
                    pool.wait_ge(s_fin, reuse)
                pool.nop(nofuse=True)
                for k in range(2):
                    pool.indirect_dma_start(yg[j][k][:], None, ydram, bass.IndirectOffsetOnAxis(
                        ap=ygi[j][:, k:k + 1], axis=0)).then_inc(s_yg[j], 16)

            for j in range(4):
                gather(j, j, None)
            with pool.Fori(1, TILES // 4) as i:
                for j in range(4):
                    gather(4 * i + j, j, 4 * i + j - 3)
            gather(TILES - 1, 0, TILES - 4)

        @block.tensor
        def _(pe):
            pe.wait_ge(s_cons, 1)
            pe.wait_ge(s_attw, 64)
            for k in range(4):
                for m in range(2):
                    ins = pe.transpose(bank[k // 2][:, 192 * (k % 2) + DH * m:192 * (k % 2) + DH * m + DH],
                                       woraw[:, m, P * k:P * k + P], ident[0:DH, 0:DH])
                if k % 2:
                    ins.then_inc(s_pg, 1)
            for n in range(2 * NH):
                h, o = n // 2, 64 * (n // 2 % 2)
                pe.wait_ge(s_eg, n + 1 if n else 2)
                lhs, rhs = (wk, wq) if n % 2 == 0 else (wv, woT)
                for m in range(2):
                    ins = pe.matmul(bank[n % 2][0:DH, D * m:D * m + D], lhs[o:o + 64, h // 2, DH * m:DH * m + DH],
                                    rhs[o:o + 64, h // 2, :], start=True, stop=True)
                ins.then_inc(s_pg, 1)
            pe.wait_ge(s_wprep, 1)
            for g in range(12):
                if g == 0:
                    pe.wait_ge(s_eg, 2 + 2 * NH)
                if g >= 2:
                    pe.wait_ge(s_wtout, g - 1)
                for kk in range(2):
                    k = 2 * g + kk
                    dr, s, c = k // 6 - 1, k // 3 % 2, k % 3
                    y0 = 8 * ((dr + 1) % 2)
                    for m in range(2):
                        ins = pe.transpose(bank[g % 2][:, D * kk + DH * m:D * kk + DH * m + DH],
                                           wv5[:, m, y0:y0 + 8, :, CH * part_of(dr, s) + c], ident[0:DH, 0:DH])
                ins.then_inc(s_wt, 1)
            pe.wait_ge(s_vb, 1)
            for k in range(2):
                for m in range(2):
                    ins = pe.matmul(bank[2][:, D * k + DH * m:D * k + DH * m + DH], vb[:, k, m, :],
                                    ident[0:DH, 0:DH], start=True, stop=True)
            ins.then_inc(s_row, 1)

            def img_t(g):
                if g >= 2:
                    pe.wait_ge(s_itout, g - 1)
                r, m = g // 4, g % 4
                pe.wait_ge(s_strip, r + 1)
                for c in range(CH):
                    ins = pe.transpose(bank[3 + g % 2][:, P * c:P * c + P], strip[r % 2][:, c, m, :], ident[:])
                ins.then_inc(s_it, 1)

            def patch(p):
                i, j = p // 3, p % 3
                pe.wait_ge(s_itout, min(32, 8 * i + 16))
                if p == 0:
                    pe.wait_ge(s_wtout, 12 + 1)
                if p >= 2:
                    pe.wait_ge(s_patout, p - 1)
                for k in range(24):
                    dr, s, c = k // 6, k // 3 % 2, k % 3
                    ins = pe.matmul(bank[5 + p % 2][:, 0:193], imgT[:, 2 * i + dr, j + s, c, :], wcT[:, k, :],
                                    start=(k == 0), stop=(k == 23))
                ins.then_inc(s_pat, 1)

            for g in range(16):
                img_t(g)
            for i in range(3):
                for j in range(3):
                    if i < 2 and j < 2:
                        for g in range(16 + 8 * i + 4 * j, 20 + 8 * i + 4 * j):
                            img_t(g)
                    patch(3 * i + j)

            pe.wait_ge(s_x0n, 2)
            for m in range(2):
                ins = pe.transpose(bank[0][0:DH, P * m:P * m + P], x0n[0][:, DH * m:DH * m + DH], ident[:])
            for m in range(2):
                ins = pe.transpose(bank[1][0:DH, P * m:P * m + NPATCH], x0n[1][0:NPATCH, DH * m:DH * m + DH],
                                   ident[0:NPATCH, 0:NPATCH])
            ins.then_inc(s_x0t, 1)
            pe.wait_ge(s_x0T, 2)
            for m in range(2):
                ins = pe.matmul(bank[2][0:NH, 0:SPAD], wgT[:, m, :], x0T[:, m, :], start=(m == 0), stop=(m == 1))
            ins.then_inc(s_g8, 1)
            for n in range(2 * NH):
                h, src = n // 2, (gT, hT)[n % 2]
                if n >= 4:
                    pe.wait_ge((s_kvout, s_vvout)[n % 2], h - 1)
                for m in range(2):
                    for k in range(2):
                        ins = pe.matmul(bank[4 + h % 2 + 2 * (n % 2)][0:DH, SPAD * m:SPAD * m + SPAD],
                                        src[:, k, h, DH * m:DH * m + DH], x0T[:, k, :], start=(k == 0), stop=(k == 1))
                ins.then_inc(s_kv, 1)

            def turn(tiles, nt, ready, c, done):
                for k in range(-(-nt // 2)):
                    pe.wait_ge(ready, 4 * c + min(2 * k + 2, nt))
                    for jj in range(min(2, nt - 2 * k)):
                        for m in range(2):
                            ins = pe.transpose(bank[1 + k][0:DH, 256 * m + P * jj:256 * m + P * jj + P],
                                               tiles[2 * k + jj][:, DH * m:DH * m + DH], ident[:])
                    ins.then_inc(done, 1)

            def route(c, par, nt):
                turn(xf[par], nt, s_xf, c, s_t2)
                for j in range(nt):
                    if j % 2 == 0:
                        pe.wait_ge(s_xfT, 2 * c + j // 2 + 1)
                    for m in range(2):
                        ins = pe.matmul(bank[3][:, 8 * j:8 * j + 8], xfT[:, m, P * j:P * j + P], rws[:, m, :],
                                        start=(m == 0), stop=(m == 1))
                ins.then_inc(s_lg, 1)

            def ranks(c, nt):
                pe.wait_ge(s_e, c + 1)
                w = 8 * nt
                pe.matmul(bank[3][:, 64:64 + w], ltri[:], eb[:, 0:nt, :], start=True, stop=False)
                pe.matmul(bank[3][:, 64:64 + w], onesb[:], ecum[:, 0:nt, :], start=False, stop=True).then_inc(s_pf, 1)

            def chunk(c, par, nt, prev, nxt, first=False):
                w = P * nt
                pe.wait_ge(s_kc, c + 1)
                pe.wait_ge(s_xT, 2 * c + (nt + 1) // 2)
                for m in range(2):
                    ins = pe.matmul(bank[0][:, 0:w], kc[:, m, :], xT[:, m, 0:w], start=(m == 0), stop=(m == 1))
                ins.then_inc(s_sc, 1)
                for k in range(4):
                    ins = pe.transpose(bank[7][:, DH * k:DH * k + DH], kc[:, k, :], ident[0:DH, 0:DH])
                ins.then_inc(s_rt, 1)
                if prev:
                    route(c - 1, 1 - par, prev)
                pe.wait_ge(s_sm, c + 1)
                pe.wait_ge(s_cr, c + 1)
                pe.wait_ge(s_ns, c + 1)
                for j in range(nt):
                    o = bank[5 + j // 2][:, D * (j % 2):D * (j % 2) + D]
                    for m in range(2):
                        pe.matmul(o, xT[:, m, P * j:P * j + P], nst[:, m, :], start=(m == 0), stop=False)
                    pe.matmul(o, sm[:, P * j:P * j + P], crow[:], start=False, stop=True).then_inc(s_o, 1)
                if prev:
                    ranks(c - 1, prev)
                pe.wait_ge(s_ar, c + 1)
                for m in range(2):
                    ins = pe.matmul(bank[4][0:DH, D * m:D * m + D], arow[:, DH * m:DH * m + DH], crow[:],
                                    start=True, stop=True)
                ins.then_inc(s_nu, 1)
                if nxt:
                    turn(xn, nxt, s_xn, c + 1, s_t)

            turn(xn, 4, s_xn, 0, s_t)
            chunk(0, 0, 4, 0, 4)
            chunk(1, 1, 4, 4, 4)
            chunk(2, 0, 4, 4, 4)
            with pe.Fori(0, 3) as i:
                chunk(2 * i + 3, 1, 4, 4, 4)
                chunk(2 * i + 4, 0, 4, 4, 4)
            chunk(9, 1, 4, 4, 1)
            chunk(10, 0, 1, 4, 0)
            route(10, 0, 1)
            ranks(10, 1)
            pe.wait_ge(s_pos, CHUNKS)
            pe.matmul(bank[3][:, 128:136], onesb[:], ecum[:, 4, :], start=True, stop=True).then_inc(s_cread, 1)

            pe.wait_ge(s_rawg, 32)
            pe.wait_ge(s_tab, 1)
            for n in range(44):
                if n >= 4:
                    pe.wait_ge(s_eout[0], n - 3)
                if n == 24:
                    for p in range(2):
                        for j in range(4):
                            pe.wait_ge(s_scat[p][j], 32 * len([c for c in range(p, CHUNKS, 2) if 4 * c + j < TILES]))
                b = bank[n % 4]
                if n < 32:
                    e, which, half = n // 4, n // 2 % 2, n % 2
                    for c in range(FC):
                        ins = pe.transpose(b[0:(D1, D2)[half], P * c:P * c + P],
                                           (raw_g, raw_u)[which][:, FC * e + c, D1 * half:(D1, D)[half]], ident[:])
                else:
                    if n == 32:
                        pe.wait_ge(s_rawd, 32)
                    for kk in range(2):
                        g = 2 * (n - 32) + kk
                        e, c = g // FC, g % FC
                        pe.transpose(b[:, D * kk:D * kk + D1], raw_d1[:, e, P * c:P * c + P], ident[:])
                        ins = pe.transpose(b[:, D * kk + D1:D * kk + D], raw_d2[:, e, P * c:P * c + P], ident[0:D2, 0:D2])
                ins.then_inc(s_et, 1)
            pe.wait_ge(s_eout[0], 44)

            gate_reg = [pe.alloc_register(f"gate_expert{b}") for b in range(2)]
            down_reg = [pe.alloc_register(f"down_expert{b}") for b in range(2)]
            for b in range(2):
                pe.reg_load(gate_reg[b], tab[0:1, 1, b:b + 1])
                pe.reg_load(down_reg[b], tab[0:1, 1, b:b + 1])

            def step(k, b, parts="xght"):
                if "x" in parts:
                    pe.wait_ge(s_xs[b], 16 * (k - b + 4))
                    if not isinstance(k, int) or k >= -1:
                        pe.wait_ge(s_xlo, k + 2)
                    for m in range(2):
                        ins = pe.transpose(bank[5][:, P * m:P * m + P], xs[b][:, P * m:P * m + P], ident[:])
                    ins.then_inc(s_xst, 1)
                if "g" in parts:
                    o = 1 - b
                    e = pe.snap(gate_reg[o], min_val=0, max_val=NE - 1)
                    pe.wait_ge(s_xlo, k + 2)
                    for which in range(2):
                        cols = bass.ds(e * (2 * DE) + DE * which, DE)
                        acc = bank[2 * o + which][:, 0:DE]
                        pe.matmul(acc, xh[o][:, 0:P], wa_h[:, cols], start=True, stop=False)
                        pe.matmul(acc, xh[o][:, 0:P], wa_l[:, cols], start=False, stop=False)
                        pe.matmul(acc, xl[o][:, 0:P], wa_h[:, cols], start=False, stop=False)
                        pe.matmul(acc, xh[o][:, P:2 * P], wb[:, cols], start=False, stop=False)
                        ins = pe.matmul(acc, xl[o][0:D2, P:2 * P], wb[0:D2, cols], start=False, stop=True)
                    ins.then_inc(s_gu, 1)
                if "h" in parts:
                    pe.wait_ge(s_hh, k + 1)
                    if not isinstance(k, int) or k >= 1:
                        pe.wait_ge(s_htl, k)
                    for c in range(FC):
                        ins = pe.transpose(bank[4][:, P * c:P * c + P], hh[b][:, P * c:P * c + P], ident[:])
                    ins.then_inc(s_ht, 1)
                if "t" in parts:
                    o = 1 - b
                    e = pe.snap(down_reg[o], min_val=0, max_val=NE - 1)
                    pe.wait_ge(s_htl, k)
                    for c in range(FC):
                        cols = bass.ds(e * (FC * D) + c * D, D)
                        acc = bank[6 + o][:, 0:D]
                        pe.matmul(acc, hth[o][:, P * c:P * c + P], wd_h[:, cols], start=(c == 0), stop=False)
                        pe.matmul(acc, hth[o][:, P * c:P * c + P], wd_l[:, cols], start=False, stop=False)
                        ins = pe.matmul(acc, htl[o][:, P * c:P * c + P], wd_h[:, cols], start=False, stop=(c == FC - 1))
                    ins.then_inc(s_dn, 1)
                if "g" in parts:
                    pe.reg_mov(down_reg[1 - b], gate_reg[1 - b])
                    if not isinstance(k, int) or k + 3 < TAB:
                        pe.reg_load(gate_reg[1 - b], tab[0:1, 1, bass.ds(k + 3, 1)])

            pipeline(pe, step, "xght", (2, 1, 0, -1))

        @block.vector
        def _(v):
            st = Steps(v, s_dve)
            for k in s_ys + s_out:
                v.sem_inc(k, 16)
            for ih in range(2):
                v.memset(img[64 * ih:64 * ih + 64, :, 56 * ih:56 * ih + 8, :], 0.0)
                for jh in range(2):
                    a, r0 = 64 * ih + 32 * jh, 8 - 8 * ih
                    ins = v.memset(img[a:a + 32, :, r0:r0 + 56, 56 * jh:56 * jh + 8], 0.0)
            ins.then_inc(s_border, 1)
            v.wait_ge(s_wraw, 16)
            v.wait_ge(s_bet, 16)
            for m in range(2):
                st.link(v.tensor_tensor_reduce(junk[:], wraw[:, m, :], bet[:], 1.0, 0.0, ALU.mult, ALU.add,
                                               colsum[:, 1, m:m + 1]))
            v.wait_ge(s_gam, 16)
            for m in range(2):
                st.link(v.tensor_tensor_reduce(wraw[:, m, :], wraw[:, m, :], gam[:], 1.0, 0.0, ALU.mult, ALU.add,
                                               colsum[:, 0, m:m + 1]))
            for m in range(2):
                for dr in range(2):
                    for s in range(2):
                        px, ox = (8, 0) if s == 0 else (0, 8)
                        y0 = 8 * ((dr + 1) % 2)
                        k = CH * part_of(dr, s)
                        dst = wv5[:, m, y0:y0 + 8, px:px + 8, k:k + CH]
                        st.mark(v.tensor_tensor(dst, dst, wv5[:, m, 8 * dr:8 * dr + 8, ox:ox + 8, 0:CH], ALU.add))
            v.wait_ge(s_par, 16 * 8)
            st.mark(v.tensor_tensor(colsum[:, 1, :], colsum[:, 1, :], biasc[:], ALU.add))
            st.wait()
            v.memset(vb[:], 1.0).then_inc(s_wprep, 1)
            v.wait_ge(s_wprep, 1)
            for k in range(2):
                for m in range(2):
                    st.mark(v.tensor_scalar(vb[:, k, m, :], vb[:, k, m, :], colsum[:, k, m:m + 1], None, ALU.mult))
            st.wait()
            for m in range(2):
                st.mark(v.tensor_scalar(rws[:, m, :], rwT[:, m, :], nwc[:, m:m + 1], None, ALU.mult))
            v.memset(ecum[:], 0.0).then_inc(s_vb, 1)
            v.wait_ge(s_row, 1)
            st.mark(v.tensor_copy(sumwb[:], bank[2][:, 0:D]))
            st.mark(v.tensor_copy(constb[:], bank[2][:, D:2 * D]))
            v.wait_ge(s_cst, 16)
            v.wait_ge(s_wt, 12)
            v.tensor_copy(wcT[:, :, D:D + 1], cst[:, C_STAT:C_STAT + 24].unsqueeze(2)).then_inc(s_wtout, 1)

            def img_out(g):
                v.wait_ge(s_it, g + 1)
                v.tensor_copy(imgT[:, g // 4, g % 4, :, :],
                              bank[3 + g % 2][:, 0:CH * P].rearrange("p (c t) -> p c t", c=CH)).then_inc(s_itout, 1)

            def patch_out(p):
                i, j = p // 3, p % 3
                acc = bank[5 + p % 2]
                mean, var, q, rs = (sd2[:, 25 + k:26 + k] for k in range(4))
                v.wait_ge(s_pat, p + 1)
                v.wait_ge(s_sq, 2 * p + 2)
                st.mark(v.tensor_scalar(mean, acc[:, D:D + 1], -1.0 / PFEAT, None, ALU.mult))
                st.link(v.tensor_tensor(var, sc[:, p:p + 1], sc[:, 9 + p:10 + p], ALU.add))
                st.link(v.tensor_tensor(q, mean, mean, ALU.mult))
                st.link(v.tensor_scalar(var, var, 1.0 / PFEAT, LN_EPS, ALU.mult, ALU.add))
                v.tensor_tensor(sd2[:, 16 + p:17 + p], var, q, ALU.subtract).then_inc(s_pv, 1)
                t = tmp[p % 2]
                v.scalar_tensor_tensor(out=t[:], in0=sumwb[:], scalar=mean, in1=acc[:, 0:D],
                                       op0=ALU.mult, op1=ALU.add).then_inc(s_patout, 1)
                v.wait_ge(s_patout, p + 1)
                v.wait_ge(s_psd, p + 1)
                st.link(v.reciprocal(rs, sd2[:, p:p + 1]))
                for q4 in range(4):
                    tt = GRID * (3 * (q4 // 2) + i) + 3 * (q4 % 2) + j
                    a, o = 32 * q4, 32 * (tt % TQ)
                    ins = v.scalar_tensor_tensor(out=hres3[o:o + 32, tt // TQ, :], in0=t[a:a + 32, :],
                                                 scalar=rs[a:a + 32, :], in1=constb[a:a + 32, :],
                                                 op0=ALU.mult, op1=ALU.add)
                ins.then_inc(s_ptok, 1)

            for g in range(16):
                img_out(g)
            for i in range(3):
                for j in range(3):
                    if i < 2 and j < 2:
                        for g in range(16 + 8 * i + 4 * j, 20 + 8 * i + 4 * j):
                            img_out(g)
                    if 3 * i + j:
                        patch_out(3 * i + j - 1)
            patch_out(8)

            v.wait_ge(s_x0, 16 * 5)
            v.memset(x0T[:, :, SEQ:SPAD], 0.0)
            rows = (P, NPATCH)
            st.mark(v.memset(zrow[:], 0.0))
            st.mark(v.memset(sd2[:], 1.0))
            for k in range(2):
                st.mark(v.bn_stats(stats[0:rows[k], k, :], x0[k][0:rows[k], :]))
            st.wait()
            for k in range(2):
                st.mark(v.bn_aggr(mv[0:rows[k], k, :], stats[0:rows[k], k, :]))
            st.wait()
            for k in range(2):
                ins = v.tensor_scalar(sd2[0:rows[k], 16 + k:17 + k], mv[0:rows[k], k, 1:2], LN_EPS, None, ALU.add)
            ins.then_inc(s_v0, 1)
            v.wait_ge(s_sd0, 1)
            st.link(v.reciprocal(sd2[:, 4:6], sd2[:, 0:2]))
            for k in range(2):
                v.tensor_scalar(x0n[k][0:rows[k], :], x0[k][0:rows[k], :], mv[0:rows[k], k, 0:1],
                                sd2[0:rows[k], 4 + k:5 + k], ALU.subtract, ALU.mult).then_inc(s_x0n, 1)
            v.wait_ge(s_x0t, 1)
            for m in range(2):
                ins = v.tensor_copy(x0T[:, m, 0:NPATCH].rearrange("p (n q) -> p q n", q=TQ),
                                    bank[1][0:DH, P * m:P * m + NPATCH].rearrange("p (q n) -> p q n", q=TQ))
            ins.then_inc(s_x0T, 1)
            for h in range(NH):
                v.wait_ge(s_kv, 2 * h + 2)
                v.tensor_copy(valsT[:, :, :, CHUNK * h:CHUNK * h + CHUNK],
                              bank[6 + h % 2][0:DH, 0:2 * SPAD].rearrange("p (m c s) -> p m c s", m=2, s=CHUNK)
                              ).then_inc(s_vvout, 1)
            v.wait_ge(s_kg, 16 * NH)
            st.mark(v.tensor_tensor(kgate[:], kgate[:], cst[:, C_KEY:C_KEY + CHUNKS], ALU.mult))
            v.memset(nst[:], 0.0).then_inc(s_ns, 1)
            v.wait_ge(s_ns, 1)

            def ln1(c, nt, first=False):
                for j in range(nt):
                    st.mark(v.bn_stats(stats[:, j, :], hres[:, bass.ds((4 * c + j) * D, D)]))
                st.wait_apart()
                for j in range(nt):
                    st.mark(v.bn_aggr(mv[:, j, :], stats[:, j, :]))
                st.wait()
                v.tensor_scalar(sc[:, 0:nt], mv[:, 0:nt, 1], LN_EPS, None, ALU.add).then_inc(s_v1, 1)
                v.wait_ge(s_sd1, c + 1)
                if not first:
                    v.wait_ge(s_t, 2 * c)
                st.link(v.reciprocal(sc[:, 8:8 + nt], sc[:, 4:4 + nt]))
                st.mark(v.tensor_scalar(sc[:, 16:16 + nt], sc[:, 8:8 + nt], 1.0, None, ALU.add))
                v.scalar_tensor_tensor(out=sc[:, 12:12 + nt], in0=mv[:, 0:nt, 0], scalar=-1.0, in1=sc[:, 8:8 + nt],
                                       op0=ALU.mult, op1=ALU.mult).then_inc(s_r1, 1)
                v.wait_ge(s_r1, c + 1)
                for j in range(nt):
                    t = hres[:, bass.ds((4 * c + j) * D, D)]
                    v.wait_ge(s_xn, 4 * c + j + 1)
                    st.mark(v.tensor_scalar(t, t, sc[:, 16 + j:17 + j], sc[:, 12 + j:13 + j], ALU.mult, ALU.add))

            def attend(c, nt, first=False):
                w = P * nt
                v.wait_ge(s_sc, c + 1)
                v.tensor_tensor(sm[:, 0:w].rearrange("p (t b) -> p t b", b=B),
                                bank[0][:, 0:w].rearrange("p (t b) -> p t b", b=B),
                                cst[:, C_MASK:C_MASK + TQ * nt].unsqueeze(2).to_broadcast([P, TQ * nt, B]),
                                ALU.mult).then_inc(s_sm, 1)

            def picks(c, par, nt):
                v.wait_ge(s_lg, c + 1)
                v.nop(nofuse=True)
                for j in range(nt):
                    st.mark(v.max(t8[:, j, :], bank[3][:, 8 * j:8 * j + 8]))
                st.wait_apart()
                for j in range(nt):
                    st.mark(v.max_index(i8[:, j, :], t8[:, j, :], bank[3][:, 8 * j:8 * j + 8]))
                st.mark(v.tensor_copy(top8[:, bass.ds(c * 32, 8 * nt)], t8[:, 0:nt, :].rearrange("p j e -> p (j e)")))
                st.wait()
                fi = idxf[:, bass.ds(c * 8, 2 * nt)]
                st.link(v.tensor_copy(fi.rearrange("p (j k) -> p j k", k=2), i8[:, 0:nt, 0:2]))
                ohv = oh[:, 0:16 * nt]
                st.link(v.tensor_tensor(ohv.rearrange("p (a e) -> p a e", e=NE),
                                        cst[:, C_EXP:C_EXP + NE].unsqueeze(1).to_broadcast([P, 2 * nt, NE]),
                                        fi.unsqueeze(2).to_broadcast([P, 2 * nt, NE]), ALU.is_equal))
                o4 = ohv.rearrange("p (j k e) -> p j k e", k=2, e=NE)
                st.link(v.tensor_tensor(eb[:, 0:nt, :], o4[:, :, 0, :], o4[:, :, 1, :], ALU.add))
                for j in range(nt - 1):
                    st.link(v.tensor_tensor(ecum[:, j + 1, :], ecum[:, j, :], eb[:, j, :], ALU.add))
                v.tensor_tensor(ecum[:, 4, :], ecum[:, nt - 1, :], eb[:, nt - 1, :], ALU.add).then_inc(s_e, 1)

            def places(c, par, nt, wait_e=None):
                v.wait_ge(s_pf, c + 1)
                v.wait_ge(s_e, c + 1)
                st.mark(v.tensor_copy(ecum[:, 0, :], ecum[:, 4, :]))
                fi = idxf[:, bass.ds(c * 8, 2 * nt)]
                rk = rankf[:, bass.ds(c * 8, 2 * nt)]
                st.link(v.tensor_tensor(ohm[:, 0:16 * nt].rearrange("p (j k e) -> p j k e", k=2, e=NE),
                                        oh[:, 0:16 * nt].rearrange("p (j k e) -> p j k e", k=2, e=NE),
                                        bank[3][:, 64:64 + 8 * nt].rearrange("p (j e) -> p j e", e=NE).unsqueeze(2)
                                        .to_broadcast([P, nt, 2, NE]), ALU.mult))
                st.link(v.tensor_reduce(rk, ohm[:, 0:16 * nt].rearrange("p (a e) -> p a e", e=NE), AX.X, ALU.add))
                st.link(v.scalar_tensor_tensor(out=posf[:, 0:2 * nt], in0=fi, scalar=float(REGION), in1=rk,
                                               op0=ALU.mult, op1=ALU.add))
                v.tensor_copy(posu[par][:, 0:2 * nt], posf[:, 0:2 * nt]).then_inc(s_pos, 1)

            def residual(c, nt):
                for j in range(nt):
                    v.wait_ge(s_o, 4 * c + min(j // 2 * 2 + 2, nt))
                    v.scalar_tensor_tensor(out=h2[j][:], in0=bank[5 + j // 2][:, D * (j % 2):D * (j % 2) + D],
                                           scalar=cst[:, bass.ds(4 * c + (j + C_TOK), 1)],
                                           in1=hres[:, bass.ds((4 * c + j) * D, D)], op0=ALU.mult, op1=ALU.add
                                           ).then_inc(s_h2, 1)

            def state(c):
                v.wait_ge(s_nu, c + 1)
                v.tensor_tensor(nst[:], nst[:], bank[4][0:DH, 0:384].rearrange("p (m d) -> p m d", m=2),
                                ALU.add).then_inc(s_ns, 1)

            def ln2(c, nt):
                v.wait_ge(s_h2, 4 * c + nt)
                for j in range(nt):
                    st.mark(v.bn_stats(stats2[:, j, :], h2[j][:]))
                st.wait_apart()
                for j in range(nt):
                    st.mark(v.bn_aggr(mv2[:, j, :], stats2[:, j, :]))
                st.wait()
                st.link(v.tensor_scalar(sd2[:, 0:nt], mv2[:, 0:nt, 1], LN_EPS, None, ALU.add))
                st.link(v.reciprocal(sd2[:, 32:32 + nt], sd2[:, 0:nt]))
                st.link(v.tensor_tensor(sd2[:, 36:36 + nt], mv2[:, 0:nt, 1], sd2[:, 32:32 + nt], ALU.mult))
                v.tensor_scalar(sd2[:, 4:4 + nt], sd2[:, 36:36 + nt], RMS_EPS, None, ALU.add).then_inc(s_v2, 1)
                v.wait_ge(s_sd2, c + 1)
                st.link(v.reciprocal(sd2[:, 16:24], sd2[:, 8:16]))
                st.mark(v.tensor_scalar(sd2[:, 40:40 + nt], sd2[:, 16:16 + nt], 1.0, None, ALU.add))
                st.mark(v.scalar_tensor_tensor(out=sd2[:, 44:44 + nt], in0=mv2[:, 0:nt, 0], scalar=-1.0,
                                               in1=sd2[:, 16:16 + nt], op0=ALU.mult, op1=ALU.mult))
                st.link(v.tensor_tensor(sd2[:, 24:24 + nt], sd2[:, 16:16 + nt], sd2[:, 20:20 + nt], ALU.mult))
                v.scalar_tensor_tensor(out=sd2[:, 28:28 + nt], in0=mv2[:, 0:nt, 0], scalar=-1.0,
                                       in1=sd2[:, 24:24 + nt], op0=ALU.mult, op1=ALU.mult).then_inc(s_s2, 1)
                for j in range(nt):
                    st.mark(v.tensor_scalar(hres[:, bass.ds((4 * c + j) * D, D)], h2[j][:], sd2[:, 40 + j:41 + j],
                                            sd2[:, 44 + j:45 + j], ALU.mult, ALU.add))
                v.wait_ge(s_xf, 4 * c + nt)
                st.wait()

            def chunk(c, par, nt, prev, nxt):
                attend(c, nt)
                if prev:
                    picks(c - 1, 1 - par, prev)
                residual(c, nt)
                if prev:
                    places(c - 1, 1 - par, prev)
                state(c)
                if nxt:
                    ln1(c + 1, nxt)
                ln2(c, nt)

            v.wait_ge(s_txt, 64)
            v.wait_ge(s_x0, 16 * 5)
            ln1(0, 4, True)
            chunk(0, 0, 4, 0, 4)
            chunk(1, 1, 4, 4, 4)
            chunk(2, 0, 4, 4, 4)
            with v.Fori(0, 3) as i:
                st.enter(i, 2 * STEPS_PER_CHUNK)
                chunk(2 * i + 3, 1, 4, 4, 4)
                chunk(2 * i + 4, 0, 4, 4, 4)
            st.leave(3)
            chunk(9, 1, 4, 4, 1)
            chunk(10, 0, 1, 4, 0)
            picks(10, 0, 1)
            places(10, 0, 1)

            v.wait_ge(s_cread, 1)
            cnt, til, cum, fst, one = (ct[:, k, :] for k in range(5))
            st.mark(v.memset(one, 1.0))
            st.mark(v.tensor_scalar(cnt, bank[3][:, 128:136], float(P - 1), None, ALU.add))
            st.link(v.tensor_copy(cti[:, 1, :], bank[3][:, 128:136]))
            st.link(v.tensor_copy(cti[:, 0, :], cnt))
            st.link(v.tensor_scalar(cti[:, 0, :], cti[:, 0, :], 7, None, ALU.arith_shift_right))
            st.link(v.tensor_copy(til, cti[:, 0, :]))
            st.link(v.tensor_tensor_scan(cum, one, til, 0.0, ALU.mult, ALU.add))
            st.link(v.tensor_tensor(fst, cum, til, ALU.subtract))
            sl = cst[:, C_SLOT:C_SLOT + TAB]
            past = tabf[:]
            st.link(v.tensor_tensor(past, sl.unsqueeze(2).to_broadcast([P, TAB, NE]),
                                    cum.unsqueeze(1).to_broadcast([P, TAB, NE]), ALU.is_ge))
            st.link(v.tensor_reduce(slotf[:, 0, :], past, AX.X, ALU.add))
            st.link(v.tensor_tensor(past, past, til.unsqueeze(1).to_broadcast([P, TAB, NE]), ALU.mult))
            st.link(v.tensor_reduce(slotf[:, 1, :], past, AX.X, ALU.add))
            st.link(v.tensor_tensor(slotf[:, 1, :], sl, slotf[:, 1, :], ALU.subtract))
            st.link(v.tensor_scalar(slotf[:, 2, :], slotf[:, 0, :], float(REGION // P), None, ALU.mult))
            st.link(v.tensor_tensor(slotf[:, 1, :], slotf[:, 1, :], slotf[:, 2, :], ALU.add))
            st.link(v.tensor_scalar(slotf[:, 1, :], slotf[:, 1, :], float(P), float(NE * REGION), ALU.mult, ALU.min))
            st.link(v.tensor_scalar(slotf[:, 0, :], slotf[:, 0, :], float(NE - 1), None, ALU.min))
            st.mark(v.tensor_copy(tab[:, 0, :], slotf[:, 1, :]))
            v.tensor_copy(tab[:, 1, :], slotf[:, 0, :]).then_inc(s_tab, 1)
            st.wait()
            t3 = top8[:].rearrange("p (n e) -> p n e", e=8)
            st.link(v.tensor_copy(esum[:], t3[:, :, 0]))
            v.tensor_tensor(t3, t3, esum[:].unsqueeze(2).to_broadcast([P, TILES, 8]), ALU.subtract).then_inc(s_w, 1)
            for k in range(1):
                st.link(v.tensor_tensor(ypj[:], cst[:, C_EXP:C_EXP + NE].unsqueeze(1).to_broadcast([P, 2 * TILES, NE]),
                                        idxf[:].unsqueeze(2).to_broadcast([P, 2 * TILES, NE]), ALU.is_equal))
                st.link(v.tensor_tensor(ypj[:], ypj[:], fst.unsqueeze(1).to_broadcast([P, 2 * TILES, NE]), ALU.mult))
                st.link(v.tensor_reduce(ypos[:], ypj[:], AX.X, ALU.add))
                st.link(v.scalar_tensor_tensor(out=ypos[:], in0=ypos[:], scalar=float(P), in1=rankf[:],
                                               op0=ALU.mult, op1=ALU.add))
                st.link(v.tensor_copy(yposu[:], ypos[:]))
            experts_out(v, 0)
            v.wait_ge(s_exp, 1)
            st.link(v.tensor_reduce(esum[:], t3, AX.X, ALU.add))
            st.link(v.reciprocal(esum[:], esum[:]))
            st.link(v.tensor_tensor(wts[:].rearrange("p (n k) -> p n k", k=2), t3[:, :, 0:2],
                                    esum[:].unsqueeze(2).to_broadcast([P, TILES, 2]), ALU.mult))

            def step(k, b, parts="xght"):
                if "x" in parts:
                    v.wait_ge(s_xh, k + 3)
                    v.tensor_tensor(xl[b][:], bank[5][:, 0:2 * P], xh[b][:].bitcast(F32), ALU.subtract).then_inc(s_xlo, 1)
                if "g" in parts:
                    o = 1 - b
                    v.wait_ge(s_sg, k + 2)
                    v.tensor_tensor(hh[o][:], sg[o][:], bank[2 * o + 1][:, 0:DE], ALU.mult).then_inc(s_hh, 1)
                if "h" in parts:
                    v.wait_ge(s_hth, k + 1)
                    v.tensor_tensor(htl[b][:], bank[4][:, 0:DE], hth[b][:].bitcast(F32), ALU.subtract).then_inc(s_htl, 1)
                if "t" in parts:
                    o = 1 - b
                    v.wait_ge(s_dn, k)
                    v.wait_ge(s_ys[o], 8 * (k - 1 - o) + 16)
                    v.tensor_copy(ysb[o][:], bank[6 + o][:, 0:D]).then_inc(s_y, 1)

            pipeline(v, step, "xght", (2, 1, 0, -1))

            def index(n, j):
                v.tensor_copy(ygi[j][:], yposu[:, bass.ds(2 * n, 2)]).then_inc(s_ygi, 1)

            def combine(n, j, k, stored):
                v.wait_ge(s_yg[j], 32 * k)
                v.scalar_tensor_tensor(out=oacc[j][:], in0=yg[j][0][:], scalar=wts[:, bass.ds(2 * n, 1)],
                                       in1=hres[:, bass.ds(n * D, D)], op0=ALU.mult, op1=ALU.add).then_inc(s_h2, 1)
                v.wait_ge(s_h2, TILES + 1 + n)
                if stored is not None:
                    v.wait_ge(s_out[j], stored)
                v.scalar_tensor_tensor(out=ofin[j][:], in0=yg[j][1][:], scalar=wts[:, bass.ds(2 * n + 1, 1)],
                                       in1=oacc[j][:], op0=ALU.mult, op1=ALU.add).then_inc(s_fin, 1)

            for j in range(4):
                index(j, j)
            with v.Fori(0, TILES // 4 - 1) as i:
                for j in range(4):
                    combine(4 * i + j, j, i + 1, 16 * i + 16)
                    index(4 * i + 4 + j, j)
            for j in range(4):
                combine(TILES - 5 + j, j, TILES // 4, 16 * (TILES // 4))
                if j == 0:
                    index(TILES - 1, 0)
            combine(TILES - 1, 0, TILES // 4 + 1, 16 * (TILES // 4) + 16)


STEPS_PER_CHUNK = 52

_INS = ['x', 'txt', 'L0_tok_ln_gamma', 'L0_tok_ln_beta', 'L0_tok_W', 'L0_tok_b', 'L0_attn_w_key', 'L0_attn_w_value',
        'L0_attn_w_query', 'L0_attn_w_gate', 'L0_attn_w_out', 'L0_ffn_norm_w', 'L0_ffn_router_w', 'L0_ffn_gate_w',
        'L0_ffn_up_w', 'L0_ffn_down_w']


def shape_constants():
    import numpy as np

    c = np.zeros((P, C_ALL), np.float64)
    p = np.arange(P)
    step = p % CHUNK
    for k in range(CHUNKS):
        c[:, C_KEY + k] = WRITE * DECAY ** (-1.0 - (CHUNK * k + step))
    for n in range(TILES):
        c[:, C_TOK + n] = DECAY ** (TQ * n + p // B)
    c[:, C_MASK:C_MASK + CHUNK] = step[:, None] < np.arange(CHUNK)[None]
    right = (p % 16) >= 8
    for k in range(24):
        dr, s = k // 6 - 1, k // 3 % 2
        inner = (right if s == 0 else ~right) if dr in (0, 1) else np.zeros(P, bool)
        c[:, C_STAT + k] = 1.0 + inner
    c[:, C_EXP:C_EXP + NE] = np.arange(NE)
    c[:, C_SLOT:C_SLOT + TAB] = np.arange(TAB)
    return c.astype(np.float32)


def kernel(**inputs):
    import numpy as np
    import concourse.bacc as bacc
    from concourse.bass_utils import run_bass_kernel_spmd

    nc = bacc.Bacc("TRN2", target_bir_lowering=False, num_devices=1)
    arrays, args = {}, []
    for name in _INS:
        a = np.ascontiguousarray(inputs[name])
        arrays[f"in_{name}"] = a
        args.append(nc.dram_tensor(f"in_{name}", a.shape, mybir.dt.from_np(a.dtype), kind="ExternalInput").ap())
    arrays["in_consts"] = shape_constants()
    args.append(nc.dram_tensor("in_consts", (P, C_ALL), F32, kind="ExternalInput").ap())
    args.append(nc.dram_tensor("out_0", (B, SEQ, D), F32, kind="ExternalOutput").ap())
    build(nc, *args)
    r = run_bass_kernel_spmd(nc, [arrays], core_ids=[0])
    return r.results[0]["out_0"]
```

```python
from contextlib import ExitStack

import concourse.bass as bass
from concourse import mybir

ALU = mybir.AluOpType
ACT = mybir.ActivationFunctionType
AX = mybir.AxisListType
F32 = mybir.dt.float32
F32R = mybir.dt.float32r
BF16 = mybir.dt.bfloat16
I32 = mybir.dt.int32
U32 = mybir.dt.uint32

P = 128
B = 32
D = 192
DH = 96
GRID = 6
NPATCH = GRID * GRID
CH = 3
PARTS = 5
PFEAT = 16 * 16 * PARTS * CH
SEQ = 164
TQ = 4
TILES = SEQ // TQ
PTILES = NPATCH // TQ
CHUNK = 16
CT_TILES = CHUNK // TQ
CHUNKS = -(-SEQ // CHUNK)
NH = 8
DK = 64
SPAD = CHUNKS * CHUNK
NE = 8
DE = 384
FC = DE // P
REGION = TILES * P + P
SLOTS = TILES * 2 + NE
TAB = SLOTS + 2
D1 = P
D2 = D - P
LN_EPS = 1e-5
RMS_EPS = 1e-6
DECAY = 0.95
WRITE = 0.1

C_KEY, C_TOK = 0, CHUNKS
C_MASK = C_TOK + TILES
C_STAT = C_MASK + CHUNK
C_EXP = C_STAT + 24
C_SLOT = C_EXP + NE
C_DEST = C_SLOT + TAB
C_PAD = C_DEST + TILES
C_ALL = C_PAD + 2
DROW = D + 3
TOKENS = B * SEQ
GROUP = 4


class Steps:

    def __init__(self, eng, sem):
        self.eng, self.sem, self.base, self.n = eng, sem, 0, 0

    def mark(self, ins):
        self.n += 1
        return ins.then_inc(self.sem, 1)

    def wait(self):
        self.eng.wait_ge(self.sem, self.base + self.n)

    def wait_apart(self):
        self.wait()
        self.eng.nop(nofuse=True)

    def link(self, ins):
        self.mark(ins)
        self.wait()

    def enter(self, trip, per_trip):
        self.start, self.per = self.base + self.n, per_trip
        self.base, self.n = trip * per_trip + self.start, 0

    def leave(self, trips):
        assert self.n == self.per, (self.n, self.per)
        self.base, self.n = self.start + trips * self.per, 0


def build(nc, x, txt, gamma, beta, W, bias, w_key, w_value, w_query, w_gate, w_out,
          norm_w, router_w, gate_w, up_w, down_w, consts, out):
    with ExitStack() as ctx:
        ctx.enter_context(nc.allow_non_contiguous_dma("small transposed parameters"))
        base0 = nc.sbuf_base + (-nc.sbuf_base) % 64
        top = [base0]

        def at(name, shape, dt, offset):
            return nc.alloc_sbuf_tensor_at(name, shape, dt, offset=offset)

        def room(nbytes):
            a = top[0]
            top[0] = a + nbytes + (-nbytes) % 32
            assert top[0] <= nc.sbuf_usable_end, top[0]
            return a

        def sb(name, shape, dt=F32):
            n = 4 if dt != BF16 else 2
            for s in shape[1:]:
                n *= s
            return at(name, shape, dt, room(n))

        def sem(name):
            return ctx.enter_context(nc.semaphore(name))

        r_img = room(CH * 64 * 64 * 4)
        r_xt = room(CH * 64 * 64 * 4)
        r_wc = room(24 * 193 * 4)
        r_hres = room(TILES * D * 4)
        r_gh = room(2 * 2 * NH * D * 4)
        img = at("img", [P, CH, 64, 64], F32, r_img)
        wa_h = at("wa_h", [P, NE * 2 * DE], F32R, r_img)
        wa_l = at("wa_l", [P, NE * 2 * DE], F32R, r_img + NE * 2 * DE * 4)
        wraw = at("wraw", [DH, 2, PFEAT], F32, r_xt)
        gam = at("gam", [DH, PFEAT], F32, r_xt + 2 * PFEAT * 4)
        imgT = at("imgT", [P, 8, 4, CH, P], F32, r_xt)
        raw_u = at("raw_u", [P, NE * FC, D], F32, r_xt)
        raw_g = at("raw_g", [P, NE * FC, D], F32, r_xt + NE * FC * D * 4)
        wd_l = at("wd_l", [P, NE * FC * D], F32R, r_xt)
        r_tail = r_xt + 2 * NE * FC * D * 4
        wk = at("wk", [P, 4, D], F32, r_wc)
        wq = at("wq", [P, 4, D], F32, r_wc + 3072)
        wv = at("wv", [P, 4, D], F32, r_wc + 6144)
        woraw = at("woraw", [DH, 2, NH * DK], F32, r_wc + 9216)
        woT = at("woT", [P, 4, D], F32, r_wc + 13312)
        wcT = at("wcT", [P, 24, 193], F32, r_wc)
        wd_h = at("wd_h", [P, NE * FC * D], F32R, r_wc)
        bet = at("bet", [DH, PFEAT], F32, r_hres)
        junk = at("junk", [DH, PFEAT], F32, r_hres + PFEAT * 4)
        hres = at("hres", [P, TILES * D], F32, r_hres)
        gT = at("gT", [DH, 2, NH, D], F32, r_gh)
        hT = at("hT", [DH, 2, NH, D], F32, r_gh + 2 * NH * D * 4)
        wb = at("wb", [P, NE * 2 * DE], F32R, r_gh)
        xT = [at("xT0", [DH, 2, 512], F32, r_tail), at("xT1", [DH, 2, 512], F32, r_img + 12288)]
        xfT = at("xfT", [DH, 2, 512], F32, r_tail + 4096)
        sm = at("sm", [P, 512], F32, r_tail + 8192)
        r_act = room(2 * 2 * SPAD * NH * 4)
        keysT = at("keysT", [DH, 2, CHUNKS, P], F32, r_act)
        valsT = at("valsT", [DH, 2, CHUNKS, P], F32, r_act + 2 * SPAD * NH * 4)
        sqjunk = at("sqjunk", [P, CH, 32, 32], BF16, r_act)
        strip = [at(f"strip{i}", [P, CH, 4, P], F32, r_act + 6144 + 6144 * i) for i in range(2)]
        raw_d1 = at("raw_d1", [D1, NE, DE], F32, r_tail)
        raw_d2 = at("raw_d2", [D2, NE, DE], F32, r_act)
        dest = at("dest", [P, SLOTS], U32, r_act + 12288)
        r_ffn = r_xt + NE * FC * D * 4
        xh = [at(f"xh{i}", [P, 2 * P], F32R, r_ffn + 1024 * i) for i in range(2)]
        xl = [at(f"xl{i}", [P, 2 * P], F32R, r_ffn + 2048 + 1024 * i) for i in range(2)]
        sg = [at(f"sg{i}", [P, DE], F32, r_ffn + 4096 + 1536 * i) for i in range(2)]
        hh = [at(f"hh{i}", [P, DE], F32, r_ffn + 7168 + 1536 * i) for i in range(2)]
        hth = [at(f"hth{i}", [P, DE], F32R, r_ffn + 10240 + 1536 * i) for i in range(2)]
        htl = [at(f"htl{i}", [P, DE], F32R, r_ffn + 13312 + 1536 * i) for i in range(2)]
        ysb = [at(f"ysb{i}", [P, D], F32, r_ffn + 16384 + 768 * i) for i in range(2)]
        yall = at("yall", [P, TILES * 2 * D], F32, r_img)

        cst = sb("cst", [P, C_ALL])
        ident = sb("ident", [P, P])
        ltri = sb("ltri", [P, P], BF16)
        onesb = sb("onesb", [P, P], BF16)
        sumwb = sb("sumwb", [P, D])
        constb = sb("constb", [P, D])
        colsum = sb("colsum", [DH, 2, 2])
        biasc = sb("biasc", [DH, 2])
        nwc = sb("nwc", [DH, 2])
        nwab = sb("nwab", [P, 2])
        wgT = sb("wgT", [DH, 2, NH])
        rwT = sb("rwT", [DH, 2, NE])
        rws = sb("rws", [DH, 2, NE])
        g8 = sb("g8", [NH, SPAD])
        kgate = sb("kgate", [P, CHUNKS])
        stats = sb("stats", [P, 4, 6])
        mv = sb("mv", [P, 4, 2])
        sc = sb("sc", [P, 32])
        stats2 = sb("stats2", [P, 4, 6])
        mv2 = sb("mv2", [P, 4, 2])
        sd2 = sb("sd2", [P, 48])
        nst = sb("nst", [DH, 2, D])
        top8 = sb("top8", [P, TILES * 8])
        t8 = sb("t8", [P, 4, 8])
        i8 = sb("i8", [P, 4, 8], U32)
        idxf = sb("idxf", [P, TILES * 2])
        rankf = sb("rankf", [P, TILES * 2])
        r_small = room(4 * 1024)
        xn = [at(f"xn{j}", [P, D], F32, r_small + 768 * j) for j in range(4)]
        vb = at("vb", [DH, 2, 2, P], F32, r_small)
        oh = sb("oh", [P, 64])
        ohm = sb("ohm", [P, 64])
        eb = sb("eb", [P, 4, 8], BF16)
        ecum = sb("ecum", [P, 5, 8], BF16)
        posf = sb("posf", [P, 8])
        posu = [sb(f"posu{p}", [P, 8], U32) for p in range(2)]
        arow = sb("arow", [P, D])
        crow = sb("crow", [P, D])
        xfd = [at(f"xf{p}", [P, CT_TILES, DROW], F32, r_img + CH * 64 * 64 * 4 - (2 - p) * (CT_TILES * DROW * 4 + 16))
               for p in range(2)]
        xf = [[xfd[p][:, j, 0:D] for j in range(CT_TILES)] for p in range(2)]
        h2 = [[at(f"h2_{p}_{j}", [P, D], F32, r_img + 20480 * p + 768 * j) for j in range(4)] for p in range(2)]
        kc = [at(f"kc{p}", [DH, 4, P], F32, r_img + 16384 + 2048 * p) for p in range(2)]
        x0 = [at(f"x0_{j}", [P, D], F32, r_img + 4096 + 768 * j) for j in range(2)]
        x0n = [at(f"x0n_{j}", [P, D], F32, r_img + 6144 + 768 * j) for j in range(2)]
        x0T = at("x0T", [DH, 2, SPAD], F32, r_img + 8192)
        zrow = at("zrow", [P, DROW], F32, r_small + 3072)
        tmp = [at(f"tmp{i}", [P, D], F32, r_small + 768 * i) for i in range(2)]
        top_small, top[0] = top[0], r_act + 14336
        tab = sb("tab", [P, 2, TAB], I32)
        slotf = sb("slotf", [P, 3, TAB])
        tabf = sb("tabf", [P, TAB, NE])
        ct = sb("ct", [P, 8, NE])
        cti = sb("cti", [P, 2, NE], I32)
        wts = sb("wts", [P, TILES * 2])
        esum = sb("esum", [P, TILES])
        assert top[0] <= r_act + 2 * 2 * SPAD * NH * 4
        top[0] = top_small
        dnow = [at(f"dnow{i}", [P, 1], U32, r_act + 13760 + 32 * i) for i in range(2)]
        xs = [sb("xs0", [P, 2 * P + 3]), at("xs1", [P, 2 * P + 3], F32, r_act + 12704)]


        disp = nc.dram_tensor("disp", [(NE + 1) * REGION, DROW], F32, kind="Internal").ap()
        ydram = nc.dram_tensor("ydram", [2 * TOKENS + 4 * P, D], F32, kind="Internal").ap()

        bank = [ctx.enter_context(nc.psum_tensor(f"bank{i}", [P, 512], F32)) for i in range(8)]

        s_attw, s_wraw, s_gam, s_bet, s_cst, s_par = (sem(n) for n in (
            "attn_weights_in", "patch_weights_in", "gamma_in", "beta_in", "consts_in", "params_in"))
        s_img, s_border, s_strip, s_txt, s_x0 = (sem(n) for n in ("image_in", "border_zero", "strip_ready", "text_in", "batch0_in"))
        s_rawg, s_rawd = sem("raw_gate_up_in"), sem("raw_down_in")
        s_pool = sem("pool_steps")
        s_dve, s_act = sem("dve_steps"), sem("act_steps")
        s_cons = sem("pool_constants")
        s_pg, s_eg = sem("product_mm"), sem("product_out")
        s_wprep, s_vb, s_row, s_rowout = sem("patch_weights_ready"), sem("row_lhs"), sem("row_mm"), sem("row_out")
        s_wt, s_wtout = sem("wT_mm"), sem("wT_out")
        s_it, s_itout = sem("imgT_mm"), sem("imgT_out")
        s_sq = sem("squares")
        s_pat, s_patout, s_pv, s_psd = sem("patch_mm"), sem("patch_read"), sem("patch_var"), sem("patch_std")
        s_ptok = sem("patch_tokens")
        s_v0, s_sd0, s_x0n, s_x0t, s_x0T = (sem(n) for n in ("var0", "std0", "x0_norm", "x0T_mm", "x0T_out"))
        s_kv, s_kvout, s_vvout, s_g8, s_g8out, s_kg, s_kgr = (sem(n) for n in (
            "kv_mm", "keys_out", "vals_out", "gate_mm", "gate_out", "gate_spread", "gate_ready"))
        s_v1, s_sd1, s_r1, s_xn = sem("var1"), sem("std1"), sem("rstd1"), sem("xn_ready")
        s_t, s_xT = sem("xT_mm"), sem("xT_out")
        s_kc, s_sc, s_sm = sem("keys_copied"), sem("scores_mm"), sem("scores_masked")
        s_rt, s_ar, s_cr = sem("rows_mm"), sem("key_rows"), sem("value_rows")
        s_o, s_h2, s_nu, s_ns = sem("attn_mm"), sem("h2_ready"), sem("state_mm"), sem("state_ready")
        s_v2, s_sd2, s_s2, s_xf = sem("var2"), sem("std2"), sem("rstd2"), sem("xf_ready")
        s_t2, s_xfT, s_lg, s_e, s_pf, s_pos = (sem(n) for n in (
            "xfT_mm", "xfT_out", "logits_mm", "onehots", "prefix_mm", "positions"))
        s_scat = [[sem(f"scattered{p}_{j}") for j in range(4)] for p in range(2)]
        s_et, s_eout = sem("expertT_mm"), [sem("expertT_out_dve"), sem("expertT_out_act")]
        s_cread, s_tab, s_zf = sem("counts_mm"), sem("table"), sem("tail_zeroed")
        s_xs = [sem(f"xs_in{i}") for i in range(2)]
        s_ys = [sem(f"y_stored{i}") for i in range(2)]
        s_xst, s_xh, s_xlo, s_gu, s_sg, s_hh = (sem(n) for n in (
            "xsT_mm", "xsT_high", "xsT_low", "gate_up_mm", "silu", "hidden"))
        s_ht, s_hth, s_htl, s_dn, s_y = (sem(n) for n in (
            "hiddenT_mm", "hiddenT_high", "hiddenT_low", "down_mm", "y_ready"))
        s_exp, s_w, s_dest, s_dnow = (sem(n) for n in (
            "softmax_exp", "weights_ready", "result_rows", "result_rows_copied"))
        s_yg = [sem(f"results_in{i}") for i in range(-(-TILES // GROUP))]
        s_fin, s_out = sem("final_ready"), [sem("out_stored_even"), sem("out_stored_odd")]

        txt_q = txt.rearrange("b (n q) d -> q b n d", q=TQ)
        out_t = out.rearrange("b s d -> s b d")
        hres3 = hres.rearrange("p (n d) -> p n d", d=D)

        block = ctx.enter_context(nc.Block())

        def part_of(dr, s):
            return (1 if s == 0 else 3) if dr <= 0 else (4 if s == 0 else 2)

        wv5 = wraw[:].rearrange("p m (y x c) -> p m y x c", y=16, x=16)

        def pipeline(eng, step, parts, ahead, peel=0):
            first, last = -max(ahead), SLOTS - 1 - min(ahead)
            lo = -min(ahead) + (-min(ahead)) % 2 + peel
            n = (SLOTS - max(ahead) - lo) // 2

            def there(k):
                return "".join(p for p, a in zip(parts, ahead) if 0 <= k + a < SLOTS)

            for k in range(first, lo):
                step(k, k % 2, there(k))
            with eng.Fori(0, n) as i:
                for b in range(2):
                    step(2 * i + (lo + b), b)
            for k in range(lo + 2 * n, last + 1):
                step(k, k % 2, there(k))

        def around(c):
            def tiles(k):
                return min(CT_TILES, TILES - CT_TILES * k) if 0 <= k < CHUNKS else 0

            return tuple(tiles(c + k) if isinstance(c, int) else CT_TILES for k in (-1, 1, 2))

        def experts_out(eng, side):
            done = s_eout[side]
            for n in range(32 + 12):
                eng.wait_ge(s_et, n + 1)
                b = bank[n % 4]
                if n < 32:
                    col, half, rows = DE * (n // 2), n % 2, (D1, D2)[n % 2]
                    src, nw = b[0:rows, 0:DE], nwab[0:rows, half:half + 1]
                    hi = (wb if half else wa_h)[0:rows, col:col + DE]
                    lo = wb[D2:P, col:col + DE] if half else wa_l[:, col:col + DE]
                    if side:
                        ins = nc.scalar.activation(hi, src, ACT.Copy, scale=nw)
                    else:
                        eng.wait_ge(s_eout[1], n + 1)
                        ins = nc.vector.scalar_tensor_tensor(out=lo, in0=src, scalar=nw, in1=hi.bitcast(F32),
                                                             op0=ALU.mult, op1=ALU.subtract)
                else:
                    col = 2 * D * (n - 32)
                    hi, lo = wd_h[:, col:col + 2 * D], wd_l[:, col:col + 2 * D]
                    if side:
                        ins = nc.scalar.copy(hi, b[:, 0:2 * D])
                    else:
                        eng.wait_ge(s_eout[1], n + 1)
                        ins = nc.vector.tensor_tensor(lo, b[:, 0:2 * D], hi.bitcast(F32), ALU.subtract)
                ins.then_inc(done, 1)

        def load_results(eng, t):
            n = min(GROUP, TILES - t)
            eng.dma_start(yall[:, 2 * D * t:2 * D * (t + n)].rearrange("p (n w) -> p n w", n=n),
                          ydram[2 * P * t:2 * P * (t + n), :].rearrange("(n p k) d -> p n (k d)", p=P, k=2)
                          ).then_inc(s_yg[t // GROUP], 16)

        def store_results(eng, odd):
            with eng.Fori(0, (TILES + 1 - odd) // 2) as i:
                n = 2 * i + odd
                eng.wait_ge(s_fin, n + 1)
                eng.dma_start(out_t[bass.ds(n * TQ, TQ)], hres[:, bass.ds(n * D, D)]).then_inc(s_out[odd], 16)

        @block.sync
        def _(sp):
            sp.dma_start(wraw[:], W.rearrange("(m p) f -> p m f", p=DH)).then_inc(s_wraw, 16)
            sp.dma_start(bet[:], beta.partition_broadcast(DH)).then_inc(s_bet, 16)
            sp.dma_start(gam[:], gamma.partition_broadcast(DH)).then_inc(s_gam, 16)
            for c in range(CH):
                for ih in range(2):
                    for jh in range(2):
                        q = 32 * (2 * ih + jh)
                        r0, c0 = 8 - 8 * ih, 8 - 8 * jh
                        sp.dma_start(img[q:q + 32, c, r0:r0 + 56, c0:c0 + 56],
                                     x[:, c, 40 * ih:40 * ih + 56, 40 * jh:40 * jh + 56]).then_inc(s_img, 16)
            sp.wait_ge(s_wprep, 1)
            for q in range(TQ):
                sp.dma_start(hres3[32 * q:32 * q + 32, PTILES:TILES, :], txt_q[q]).then_inc(s_txt, 16)
            sp.wait_ge(s_it, 32)
            sp.wait_ge(s_sq, 18)
            sp.dma_start(x0[0][:], txt[0]).then_inc(s_x0, 16)
            sp.wait_ge(s_ptok, PTILES)
            for q in range(TQ):
                sp.dma_start(x0[1][PTILES * q:PTILES * q + PTILES, :],
                             hres3[32 * q:32 * q + 1, 0:PTILES, :]).then_inc(s_x0, 16)
            sp.wait_ge(s_pat, PTILES)
            sp.dma_start(raw_g[:], gate_w.rearrange("e (c f) d -> f (e c) d", f=P)).then_inc(s_rawg, 16)
            sp.dma_start(raw_u[:], up_w.rearrange("e (c f) d -> f (e c) d", f=P)).then_inc(s_rawg, 16)
            sp.wait_ge(s_kc, CHUNKS)
            sp.dma_start(raw_d2[:], down_w[:, D1:D].rearrange("e p f -> p e f")).then_inc(s_rawd, 16)
            sp.wait_ge(s_lg, CHUNKS)
            sp.dma_start(raw_d1[:], down_w[:, 0:D1].rearrange("e p f -> p e f")).then_inc(s_rawd, 16)
            sp.wait_ge(s_tab, 1)
            for e in range(NE):
                n = sp.value_load(cti[0:1, 1, e:e + 1], min_val=0, max_val=TILES * P)
                sp.dma_start(disp[bass.ds(n + e * REGION, P), :], zrow[:]).then_inc(s_zf, 16)
            sp.dma_start(disp[NE * REGION:NE * REGION + P, :], zrow[:]).then_inc(s_zf, 16)
            sp.wait_ge(s_zf, 16 * (NE + 1))
            for p in range(2):
                for j in range(4):
                    n = len([c for c in range(p, CHUNKS, 2) if 4 * c + j < TILES])
                    sp.wait_ge(s_scat[p][j], 32 * n)

            def load_slot(s, b, first=False):
                if not first:
                    sp.wait_ge(s_xst, s - 1)
                    sp.wait_ge(s_dest, s - 1)
                row = sp.value_load(tab[0:1, 0, bass.ds(s, 1)], min_val=0, max_val=NE * REGION)
                sp.dma_start(xs[b][:, 0:D], disp[bass.ds(row, P), 0:D]).then_inc(s_xs[b], 16)
                sp.dma_start(xs[b][:, D:2 * P + 3], disp[bass.ds(row, P), D1:DROW]).then_inc(s_xs[b], 16)

            load_slot(0, 0, True)
            load_slot(1, 1, True)
            with sp.Fori(0, SLOTS // 2 - 1) as i:
                for b in range(2):
                    load_slot(2 * i + 2 + b, b)

            for b in range(2):
                sp.wait_ge(s_ys[b], 16 * SLOTS // 2)
            for g in range(0, TILES, 2 * GROUP):
                load_results(sp, g)
            store_results(sp, 0)
            sp.wait_ge(s_out[0], 16 * (TILES - TILES // 2))
            sp.wait_ge(s_out[1], 16 * (TILES // 2))

        @block.scalar
        def _(act):
            steps = Steps(act, s_act)
            act.dma_start(wk[:], w_key.rearrange("(c p) d -> p c d", p=P)).then_inc(s_attw, 16)
            act.dma_start(wq[:], w_query.rearrange("(c p) d -> p c d", p=P)).then_inc(s_attw, 16)
            act.dma_start(wv[:], w_value.rearrange("(c p) d -> p c d", p=P)).then_inc(s_attw, 16)
            act.dma_start(woraw[:], w_out.rearrange("(m p) f -> p m f", p=DH)).then_inc(s_attw, 16)
            act.dma_start(cst[:], consts).then_inc(s_cst, 16)
            act.dma_start(biasc[:], bias.rearrange("(m p) -> p m", p=DH)).then_inc(s_par, 16)
            act.dma_start(nwc[:], norm_w.rearrange("(m p) -> p m", p=DH)).then_inc(s_par, 16)
            act.dma_start(nwab[:, 0:1], norm_w[0:D1].unsqueeze(1)).then_inc(s_par, 16)
            act.dma_start(nwab[0:D2, 1:2], norm_w[D1:D].unsqueeze(1)).then_inc(s_par, 16)
            for m in range(2):
                act.dma_start(wgT[:, m, :], w_gate[:, DH * m:DH * m + DH].rearrange("h p -> p h")).then_inc(s_par, 16)
                act.dma_start(rwT[:, m, :], router_w[:, DH * m:DH * m + DH].rearrange("h p -> p h")).then_inc(s_par, 16)

            for k in range(2):
                act.wait_ge(s_pg, k + 1)
                nc.scalar.copy(woT[:, 2 * k:2 * k + 2, :], bank[k][:, 0:384]).then_inc(s_eg, 1)
            for n in range(2 * NH):
                act.wait_ge(s_pg, n + 3)
                dst = (gT if n % 2 == 0 else hT)[:, :, n // 2, :]
                nc.scalar.copy(dst, bank[n % 2][0:DH, 0:384].rearrange("p (m d) -> p m d", m=2)).then_inc(s_eg, 1)
            for g in range(12):
                act.wait_ge(s_wt, g + 1)
                nc.scalar.copy(wcT[:, 2 * g:2 * g + 2, 0:D],
                               bank[g % 2][:, 0:384].rearrange("p (k d) -> p k d", k=2)).then_inc(s_wtout, 1)
            act.wait_ge(s_border, 1)
            act.wait_ge(s_img, 16 * 12)

            def squares(p):
                i, j = p // 3, p % 3
                nc.scalar.activation(sqjunk[:], img[:, :, 16 * i:16 * i + 32, 16 * j:16 * j + 32], ACT.Square,
                                     accum_out=sc[:, p:p + 1]).then_inc(s_sq, 1)
                act.wait_ge(s_sq, 2 * p + 1)
                nc.scalar.activation(sqjunk[:, :, 0:16, 0:16], img[:, :, 16 * i + 8:16 * i + 24, 16 * j + 8:16 * j + 24],
                                     ACT.Square, accum_out=sc[:, 9 + p:10 + p]).then_inc(s_sq, 1)
                act.wait_ge(s_sq, 2 * p + 2)

            for p in range(9):
                squares(p)
            for p in range(9):
                act.wait_ge(s_pv, p + 1)
                nc.scalar.activation(sd2[:, p:p + 1], sd2[:, 16 + p:17 + p], ACT.Sqrt).then_inc(s_psd, 1)
            def std1(c, nt):
                act.wait_ge(s_v1, c + 1)
                nc.scalar.activation(sc[:, 4:4 + nt], sc[:, 0:nt], ACT.Sqrt).then_inc(s_sd1, 1)

            def norm1(c, nt):
                act.wait_ge(s_r1, c + 1)
                for j in range(nt):
                    nc.scalar.activation(xn[j][:], hres[:, bass.ds((4 * c + j) * D, D)], ACT.Identity,
                                         scale=sc[:, 8 + j:9 + j], bias=sc[:, 12 + j:13 + j]).then_inc(s_xn, 1)

            std1(0, 4)
            norm1(0, 4)
            act.wait_ge(s_v0, 1)
            nc.scalar.activation(sd2[:, 0:2], sd2[:, 16:18], ACT.Sqrt).then_inc(s_sd0, 1)
            act.wait_ge(s_x0t, 1)
            nc.scalar.copy(x0T[:, :, NPATCH:SEQ], bank[0][0:DH, 0:256].rearrange("p (m s) -> p m s", m=2)).then_inc(s_x0T, 1)
            act.wait_ge(s_g8, 1)
            nc.scalar.activation(g8[:].rearrange("h (s c) -> h s c", s=CHUNK),
                                 bank[2][0:NH, 0:SPAD].rearrange("h (c s) -> h s c", s=CHUNK), ACT.Sigmoid).then_inc(s_g8out, 1)
            act.wait_ge(s_g8out, 1)
            for h in range(NH):
                act.dma_start(kgate[CHUNK * h:CHUNK * h + CHUNK, :],
                              g8[h:h + 1, :].rearrange("h (s c) -> h s c", s=CHUNK)).then_inc(s_kg, 16)
            def xT_out(c, par, nt):
                for k in range(-(-nt // 2)):
                    act.wait_ge(s_t, 2 * c + k + 1)
                    w = P * min(2, nt - 2 * k)
                    nc.scalar.copy(xT[par][:, :, 256 * k:256 * k + w],
                                   bank[1 + k][0:DH, :].rearrange("p (m s) -> p m s", m=2)[:, :, 0:w]).then_inc(s_xT, 1)

            for h in range(NH):
                act.wait_ge(s_kv, 2 * h + 1)
                nc.scalar.copy(keysT[:, :, :, CHUNK * h:CHUNK * h + CHUNK],
                               bank[4 + h % 2][0:DH, 0:2 * SPAD].rearrange("p (m c s) -> p m c s", m=2, s=CHUNK)
                               ).then_inc(s_kvout, 1)
                if h == 2:
                    xT_out(0, 0, 4)
                if h == 4:
                    std1(1, 4)
                    norm1(1, 4)
            act.wait_ge(s_ns, 1)

            def xfT_out(c, nt):
                for k in range(-(-nt // 2)):
                    act.wait_ge(s_t2, 2 * c + k + 1)
                    w = P * min(2, nt - 2 * k)
                    nc.scalar.copy(xfT[:, :, 256 * k:256 * k + w],
                                   bank[1 + k][0:DH, :].rearrange("p (m s) -> p m s", m=2)[:, :, 0:w]).then_inc(s_xfT, 1)

            def std2(c):
                act.wait_ge(s_v2, c + 1)
                nc.scalar.activation(sd2[:, 8:16], sd2[:, 0:8], ACT.Sqrt).then_inc(s_sd2, 1)

            def norm2(c, par, uses, nt):
                act.wait_ge(s_s2, c + 1)
                for j in range(nt):
                    if uses is not None:
                        act.wait_ge(s_scat[par][j], 32 * uses)
                    nc.scalar.activation(xf[par][j][:], h2[par][j][:], ACT.Identity,
                                         scale=sd2[:, 24 + j:25 + j], bias=sd2[:, 28 + j:29 + j]).then_inc(s_xf, 1)

            def keys(c, par, first=False):
                if not first:
                    act.wait_ge(s_rt, c - 1)
                for k, t in enumerate((keysT, valsT)):
                    ins = nc.scalar.copy(kc[par][:, 2 * k:2 * k + 2, :],
                                         t[:].rearrange("p m c s -> p m (c s)")[:, :, bass.ds(c * P, P)])
                ins.then_inc(s_kc, 1)

            def rows(c):
                act.wait_ge(s_rt, c + 1)
                nc.scalar.activation(crow[:], bank[7][:, D:2 * D], ACT.Copy, scale=kgate[:, bass.ds(c, 1)]).then_inc(s_cr, 1)
                nc.scalar.copy(arow[:], bank[7][:, 0:D]).then_inc(s_ar, 1)

            def chunk(c, par, uses, nt):
                prev, nxt, nxt2 = around(c)
                if nxt:
                    xT_out(c + 1, 1 - par, nxt)
                if nxt2:
                    keys(c + 2, par)
                    std1(c + 2, nxt2)
                if nxt:
                    rows(c + 1)
                if prev:
                    xfT_out(c - 1, prev)
                if nxt2:
                    norm1(c + 2, nxt2)
                std2(c)
                norm2(c, par, uses, nt)

            act.wait_ge(s_kvout, NH)
            act.wait_ge(s_vvout, NH)
            for p in range(2):
                keys(p, p, True)
            rows(0)
            chunk(0, 0, None, 4)
            chunk(1, 1, None, 4)
            with act.Fori(0, 3) as i:
                chunk(2 * i + 2, 0, i + 1, 4)
                chunk(2 * i + 3, 1, i + 1, 4)
            chunk(8, 0, 4, 4)
            chunk(9, 1, 4, 4)
            chunk(10, 0, 5, 1)
            xfT_out(10, 1)

            experts_out(act, 1)
            act.wait_ge(s_w, 1)
            nc.scalar.activation(top8[:], top8[:], ACT.Exp).then_inc(s_exp, 1)

            def step(k, b, parts="xsh"):
                if "x" in parts:
                    act.wait_ge(s_xst, k + 3)
                    nc.scalar.copy(xh[b][:], bank[5][:, 0:2 * P]).then_inc(s_xh, 1)
                if "s" in parts:
                    act.wait_ge(s_gu, k + 2)
                    nc.scalar.activation(sg[1 - b][:], bank[2 * (1 - b)][:, 0:DE], ACT.Silu).then_inc(s_sg, 1)
                if "h" in parts:
                    act.wait_ge(s_ht, k + 1)
                    nc.scalar.copy(hth[b][:], bank[4][:, 0:DE]).then_inc(s_hth, 1)

            pipeline(act, step, "xsh", (2, 1, 0))
            for b in range(2):
                act.wait_ge(s_ys[b], 16 * SLOTS // 2)
            for g in range(GROUP, TILES, 2 * GROUP):
                load_results(act, g)
            store_results(act, 1)

        @block.gpsimd
        def _(pool):
            pool.memset(ident[:], 0.0).then_inc(s_pool, 1)
            pool.memset(onesb[:], 1.0).then_inc(s_pool, 1)
            pool.memset(ltri[:], 1.0).then_inc(s_pool, 1)
            pool.wait_ge(s_pool, 3)
            pool.affine_select(out=ident[:], in_=ident[:], compare_op=ALU.not_equal, fill=1.0, base=0,
                               pattern=[[-1, P]], channel_multiplier=1)
            pool.affine_select(out=ltri[:], in_=ltri[:], compare_op=ALU.is_gt, fill=0.0, base=0,
                               pattern=[[1, P]], channel_multiplier=-1).then_inc(s_cons, 1)

            pool.wait_ge(s_img, 16 * 12)
            pool.wait_ge(s_border, 1)
            for r in range(8):
                if r >= 2:
                    pool.wait_ge(s_it, 4 * (r - 1))
                for c in range(CH):
                    ins = pool.tensor_copy(strip[r % 2][:, c].rearrange("p m (y x) -> p m y x", y=8),
                                           img[:, c, 8 * r:8 * r + 8, :].rearrange("p y (m x) -> p m y x", m=4))
                ins.then_inc(s_strip, 1)

            def scatter(c, par, nt):
                pool.wait_ge(s_pos, c + 1)
                for j in range(nt):
                    pool.wait_ge(s_xf, 4 * c + j + 1)
                    pool.nop(nofuse=True)
                    for k in range(2):
                        pool.indirect_dma_start(disp, bass.IndirectOffsetOnAxis(
                            ap=posu[par][:, 2 * j + k:2 * j + k + 1], axis=0), xfd[par][:, j, :], None
                            ).then_inc(s_scat[par][j], 16)

            with pool.Fori(0, 4) as i:
                scatter(2 * i, 0, 4)
                scatter(2 * i + 1, 1, 4)
            scatter(8, 0, 4)
            scatter(9, 1, 4)
            scatter(10, 0, 1)

            def store(k, b):
                pool.wait_ge(s_y, k + 1)
                pool.tensor_copy(dnow[b][:], dest[:, bass.ds(k, 1)]).then_inc(s_dnow, 1)
                pool.wait_ge(s_dnow, k + 1)
                pool.nop(nofuse=True)
                pool.indirect_dma_start(ydram, bass.IndirectOffsetOnAxis(ap=dnow[b][:], axis=0),
                                        ysb[b][:], None).then_inc(s_ys[b], 16)

            with pool.Fori(0, SLOTS // 2) as i:
                for b in range(2):
                    store(2 * i + b, b)

        @block.tensor
        def _(pe):
            pe.wait_ge(s_cons, 1)
            pe.wait_ge(s_attw, 64)
            for k in range(4):
                for m in range(2):
                    ins = pe.transpose(bank[k // 2][:, 192 * (k % 2) + DH * m:192 * (k % 2) + DH * m + DH],
                                       woraw[:, m, P * k:P * k + P], ident[0:DH, 0:DH])
                if k % 2:
                    ins.then_inc(s_pg, 1)
            for n in range(2 * NH):
                h, o = n // 2, 64 * (n // 2 % 2)
                pe.wait_ge(s_eg, n + 1 if n else 2)
                lhs, rhs = (wk, wq) if n % 2 == 0 else (wv, woT)
                for m in range(2):
                    ins = pe.matmul(bank[n % 2][0:DH, D * m:D * m + D], lhs[o:o + 64, h // 2, DH * m:DH * m + DH],
                                    rhs[o:o + 64, h // 2, :], start=True, stop=True)
                ins.then_inc(s_pg, 1)
            pe.wait_ge(s_wprep, 1)
            for g in range(12):
                if g == 0:
                    pe.wait_ge(s_eg, 2 + 2 * NH)
                if g >= 2:
                    pe.wait_ge(s_wtout, g - 1)
                for kk in range(2):
                    k = 2 * g + kk
                    dr, s, c = k // 6 - 1, k // 3 % 2, k % 3
                    y0 = 8 * ((dr + 1) % 2)
                    for m in range(2):
                        ins = pe.transpose(bank[g % 2][:, D * kk + DH * m:D * kk + DH * m + DH],
                                           wv5[:, m, y0:y0 + 8, :, CH * part_of(dr, s) + c], ident[0:DH, 0:DH])
                ins.then_inc(s_wt, 1)
            pe.wait_ge(s_vb, 1)
            for k in range(2):
                for m in range(2):
                    ins = pe.matmul(bank[2][:, D * k + DH * m:D * k + DH * m + DH], vb[:, k, m, :],
                                    ident[0:DH, 0:DH], start=True, stop=True)
            ins.then_inc(s_row, 1)

            def img_t(g):
                if g >= 2:
                    pe.wait_ge(s_itout, g - 1)
                r, m = g // 4, g % 4
                pe.wait_ge(s_strip, r + 1)
                for c in range(CH):
                    ins = pe.transpose(bank[3 + g % 2][:, P * c:P * c + P], strip[r % 2][:, c, m, :], ident[:])
                ins.then_inc(s_it, 1)

            def patch(p):
                i, j = p // 3, p % 3
                pe.wait_ge(s_itout, min(32, 8 * i + 16))
                if p == 0:
                    pe.wait_ge(s_wtout, 12 + 1)
                if p >= 2:
                    pe.wait_ge(s_patout, p - 1)
                for k in range(24):
                    dr, s, c = k // 6, k // 3 % 2, k % 3
                    ins = pe.matmul(bank[5 + p % 2][:, 0:193], imgT[:, 2 * i + dr, j + s, c, :], wcT[:, k, :],
                                    start=(k == 0), stop=(k == 23))
                ins.then_inc(s_pat, 1)

            for g in range(16):
                img_t(g)
            for i in range(3):
                for j in range(3):
                    if i < 2 and j < 2:
                        for g in range(16 + 8 * i + 4 * j, 20 + 8 * i + 4 * j):
                            img_t(g)
                    patch(3 * i + j)

            pe.wait_ge(s_x0n, 2)
            for m in range(2):
                ins = pe.transpose(bank[0][0:DH, P * m:P * m + P], x0n[0][:, DH * m:DH * m + DH], ident[:])
            for m in range(2):
                ins = pe.transpose(bank[1][0:DH, P * m:P * m + NPATCH], x0n[1][0:NPATCH, DH * m:DH * m + DH],
                                   ident[0:NPATCH, 0:NPATCH])
            ins.then_inc(s_x0t, 1)
            pe.wait_ge(s_x0T, 2)
            for m in range(2):
                ins = pe.matmul(bank[2][0:NH, 0:SPAD], wgT[:, m, :], x0T[:, m, :], start=(m == 0), stop=(m == 1))
            ins.then_inc(s_g8, 1)
            def turn(tiles, nt, ready, c, done):
                for k in range(-(-nt // 2)):
                    pe.wait_ge(ready, 4 * c + min(2 * k + 2, nt))
                    for jj in range(min(2, nt - 2 * k)):
                        for m in range(2):
                            ins = pe.transpose(bank[1 + k][0:DH, 256 * m + P * jj:256 * m + P * jj + P],
                                               tiles[2 * k + jj][:, DH * m:DH * m + DH], ident[:])
                    ins.then_inc(done, 1)

            for n in range(2 * NH):
                if n == 6:
                    turn(xn, 4, s_xn, 0, s_t)
                h, src = n // 2, (gT, hT)[n % 2]
                if n >= 4:
                    pe.wait_ge((s_kvout, s_vvout)[n % 2], h - 1)
                for m in range(2):
                    for k in range(2):
                        ins = pe.matmul(bank[4 + h % 2 + 2 * (n % 2)][0:DH, SPAD * m:SPAD * m + SPAD],
                                        src[:, k, h, DH * m:DH * m + DH], x0T[:, k, :], start=(k == 0), stop=(k == 1))
                ins.then_inc(s_kv, 1)

            def logits(c, nt, first=False):
                if not first:
                    pe.wait_ge(s_pos, c)
                for j in range(nt):
                    if j % 2 == 0:
                        pe.wait_ge(s_xfT, 2 * c + j // 2 + 1)
                    for m in range(2):
                        ins = pe.matmul(bank[3][:, 8 * j:8 * j + 8], xfT[:, m, P * j:P * j + P], rws[:, m, :],
                                        start=(m == 0), stop=(m == 1))
                ins.then_inc(s_lg, 1)

            def ranks(c, nt):
                pe.wait_ge(s_e, c + 1)
                w = 8 * nt
                pe.matmul(bank[3][:, 64:64 + w], ltri[:], eb[:, 0:nt, :], start=True, stop=False)
                pe.matmul(bank[3][:, 64:64 + w], onesb[:], ecum[:, 0:nt, :], start=False, stop=True).then_inc(s_pf, 1)

            def attend(c, par, tiles):
                for j in tiles:
                    o = bank[5 + j // 2][:, D * (j % 2):D * (j % 2) + D]
                    for m in range(2):
                        pe.matmul(o, xT[par][:, m, P * j:P * j + P], nst[:, m, :], start=(m == 0), stop=False)
                    pe.matmul(o, sm[:, P * j:P * j + P], crow[:], start=False, stop=True).then_inc(s_o, 1)

            def scores(c, par, nt):
                w = P * nt
                pe.wait_ge(s_kc, c + 1)
                pe.wait_ge(s_xT, 2 * c + (nt + 1) // 2)
                for m in range(2):
                    ins = pe.matmul(bank[0][:, 0:w], kc[par][:, m, :], xT[par][:, m, 0:w], start=(m == 0), stop=(m == 1))
                ins.then_inc(s_sc, 1)
                for k in range(4):
                    ins = pe.transpose(bank[7][:, DH * k:DH * k + DH], kc[par][:, k, :], ident[0:DH, 0:DH])
                ins.then_inc(s_rt, 1)

            def chunk(c, par, nt, prev2=4, first=False):
                prev, nxt, nxt2 = around(c)
                pe.wait_ge(s_sm, c + 1)
                pe.wait_ge(s_cr, c + 1)
                pe.wait_ge(s_ns, c + 1)
                attend(c, par, range(min(2, nt)))
                if prev2:
                    logits(c - 2, prev2, first)
                attend(c, par, range(2, nt))
                if prev2:
                    ranks(c - 2, prev2)
                if nxt:
                    turn(xn, nxt, s_xn, c + 1, s_t)
                pe.wait_ge(s_ar, c + 1)
                for m in range(2):
                    ins = pe.matmul(bank[4][0:DH, D * m:D * m + D], arow[:, DH * m:DH * m + DH], crow[:],
                                    start=True, stop=True)
                ins.then_inc(s_nu, 1)
                if nxt:
                    scores(c + 1, 1 - par, nxt)
                if prev:
                    turn(xf[1 - par], prev, s_xf, c - 1, s_t2)

            scores(0, 0, 4)
            chunk(0, 0, 4, 0)
            chunk(1, 1, 4, 0)
            chunk(2, 0, 4, 4, True)
            chunk(3, 1, 4)
            with pe.Fori(1, 3) as i:
                chunk(2 * i + 2, 0, 4)
                chunk(2 * i + 3, 1, 4)
            chunk(8, 0, 4)
            chunk(9, 1, 4)
            chunk(10, 0, 1)
            logits(9, 4)
            ranks(9, 4)
            turn(xf[0], 1, s_xf, 10, s_t2)
            logits(10, 1)
            ranks(10, 1)
            pe.wait_ge(s_pos, CHUNKS)
            pe.matmul(bank[3][:, 128:136], onesb[:], ecum[:, 4, :], start=True, stop=True).then_inc(s_cread, 1)

            pe.wait_ge(s_rawg, 32)
            pe.wait_ge(s_tab, 1)
            for n in range(44):
                if n >= 4:
                    pe.wait_ge(s_eout[0], n - 3)
                if n == 20:
                    for p in range(2):
                        for j in range(4):
                            pe.wait_ge(s_scat[p][j], 32 * len([c for c in range(p, CHUNKS, 2) if 4 * c + j < TILES]))
                b = bank[n % 4]
                if n < 32:
                    e, which, half = n // 4, n // 2 % 2, n % 2
                    for c in range(FC):
                        ins = pe.transpose(b[0:(D1, D2)[half], P * c:P * c + P],
                                           (raw_g, raw_u)[which][:, FC * e + c, D1 * half:(D1, D)[half]], ident[:])
                else:
                    if n == 32:
                        pe.wait_ge(s_rawd, 32)
                    for kk in range(2):
                        g = 2 * (n - 32) + kk
                        e, c = g // FC, g % FC
                        pe.transpose(b[:, D * kk:D * kk + D1], raw_d1[:, e, P * c:P * c + P], ident[:])
                        ins = pe.transpose(b[:, D * kk + D1:D * kk + D], raw_d2[:, e, P * c:P * c + P], ident[0:D2, 0:D2])
                ins.then_inc(s_et, 1)
            pe.wait_ge(s_eout[0], 44)

            gate_reg = [pe.alloc_register(f"gate_expert{b}") for b in range(2)]
            down_reg = [pe.alloc_register(f"down_expert{b}") for b in range(2)]
            for b in range(2):
                pe.reg_load(gate_reg[b], tab[0:1, 1, b:b + 1])
                pe.reg_load(down_reg[b], tab[0:1, 1, b:b + 1])

            def step(k, b, parts="xght"):
                if "x" in parts:
                    pe.wait_ge(s_xs[b], 16 * (k - b + 4))
                    if not isinstance(k, int) or k >= -1:
                        pe.wait_ge(s_xlo, k + 2)
                    for m in range(2):
                        ins = pe.transpose(bank[5][:, P * m:P * m + P], xs[b][:, P * m:P * m + P], ident[:])
                    ins.then_inc(s_xst, 1)
                if "g" in parts:
                    o = 1 - b
                    e = pe.snap(gate_reg[o], min_val=0, max_val=NE - 1)
                    pe.wait_ge(s_xlo, k + 2)
                    for which in range(2):
                        cols = bass.ds(e * (2 * DE) + DE * which, DE)
                        acc = bank[2 * o + which][:, 0:DE]
                        pe.matmul(acc, xh[o][:, 0:P], wa_h[:, cols], start=True, stop=False)
                        pe.matmul(acc, xh[o][:, 0:P], wa_l[:, cols], start=False, stop=False)
                        pe.matmul(acc, xl[o][:, 0:P], wa_h[:, cols], start=False, stop=False)
                        pe.matmul(acc, xh[o][:, P:2 * P], wb[:, cols], start=False, stop=False)
                        ins = pe.matmul(acc, xl[o][0:D2, P:2 * P], wb[0:D2, cols], start=False, stop=True)
                    ins.then_inc(s_gu, 1)
                if "h" in parts:
                    pe.wait_ge(s_hh, k + 1)
                    if not isinstance(k, int) or k >= 1:
                        pe.wait_ge(s_htl, k)
                    for c in range(FC):
                        ins = pe.transpose(bank[4][:, P * c:P * c + P], hh[b][:, P * c:P * c + P], ident[:])
                    ins.then_inc(s_ht, 1)
                if "t" in parts:
                    o = 1 - b
                    e = pe.snap(down_reg[o], min_val=0, max_val=NE - 1)
                    pe.wait_ge(s_htl, k)
                    for c in range(FC):
                        cols = bass.ds(e * (FC * D) + c * D, D)
                        acc = bank[6 + o][:, 0:D]
                        pe.matmul(acc, hth[o][:, P * c:P * c + P], wd_h[:, cols], start=(c == 0), stop=False)
                        pe.matmul(acc, hth[o][:, P * c:P * c + P], wd_l[:, cols], start=False, stop=False)
                        ins = pe.matmul(acc, htl[o][:, P * c:P * c + P], wd_h[:, cols], start=False, stop=(c == FC - 1))
                    ins.then_inc(s_dn, 1)
                if "g" in parts:
                    pe.reg_mov(down_reg[1 - b], gate_reg[1 - b])
                    if not isinstance(k, int) or k + 3 < TAB:
                        pe.reg_load(gate_reg[1 - b], tab[0:1, 1, bass.ds(k + 3, 1)])

            pipeline(pe, step, "xght", (2, 1, 0, -1))

        @block.vector
        def _(v):
            st = Steps(v, s_dve)
            for ih in range(2):
                v.memset(img[64 * ih:64 * ih + 64, :, 56 * ih:56 * ih + 8, :], 0.0)
                for jh in range(2):
                    a, r0 = 64 * ih + 32 * jh, 8 - 8 * ih
                    ins = v.memset(img[a:a + 32, :, r0:r0 + 56, 56 * jh:56 * jh + 8], 0.0)
            ins.then_inc(s_border, 1)
            v.wait_ge(s_wraw, 16)
            v.wait_ge(s_bet, 16)
            for m in range(2):
                st.link(v.tensor_tensor_reduce(junk[:], wraw[:, m, :], bet[:], 1.0, 0.0, ALU.mult, ALU.add,
                                               colsum[:, 1, m:m + 1]))
            v.wait_ge(s_gam, 16)
            for m in range(2):
                st.link(v.tensor_tensor_reduce(wraw[:, m, :], wraw[:, m, :], gam[:], 1.0, 0.0, ALU.mult, ALU.add,
                                               colsum[:, 0, m:m + 1]))
            for m in range(2):
                for dr in range(2):
                    for s in range(2):
                        px, ox = (8, 0) if s == 0 else (0, 8)
                        y0 = 8 * ((dr + 1) % 2)
                        k = CH * part_of(dr, s)
                        dst = wv5[:, m, y0:y0 + 8, px:px + 8, k:k + CH]
                        st.mark(v.tensor_tensor(dst, dst, wv5[:, m, 8 * dr:8 * dr + 8, ox:ox + 8, 0:CH], ALU.add))
            v.wait_ge(s_par, 16 * 8)
            st.mark(v.tensor_tensor(colsum[:, 1, :], colsum[:, 1, :], biasc[:], ALU.add))
            st.wait()
            v.memset(vb[:], 1.0).then_inc(s_wprep, 1)
            v.wait_ge(s_wprep, 1)
            for k in range(2):
                for m in range(2):
                    st.mark(v.tensor_scalar(vb[:, k, m, :], vb[:, k, m, :], colsum[:, k, m:m + 1], None, ALU.mult))
            st.wait()
            for m in range(2):
                st.mark(v.tensor_scalar(rws[:, m, :], rwT[:, m, :], nwc[:, m:m + 1], None, ALU.mult))
            v.memset(ecum[:], 0.0).then_inc(s_vb, 1)
            v.wait_ge(s_row, 1)
            st.mark(v.tensor_copy(sumwb[:], bank[2][:, 0:D]))
            st.mark(v.tensor_copy(constb[:], bank[2][:, D:2 * D]))
            v.wait_ge(s_cst, 16)
            v.wait_ge(s_wt, 12)
            v.tensor_copy(wcT[:, :, D:D + 1], cst[:, C_STAT:C_STAT + 24].unsqueeze(2)).then_inc(s_wtout, 1)

            def img_out(g):
                v.wait_ge(s_it, g + 1)
                v.tensor_copy(imgT[:, g // 4, g % 4, :, :],
                              bank[3 + g % 2][:, 0:CH * P].rearrange("p (c t) -> p c t", c=CH)).then_inc(s_itout, 1)

            def patch_out(p):
                i, j = p // 3, p % 3
                acc = bank[5 + p % 2]
                mean, var, q, rs = (sd2[:, 25 + k:26 + k] for k in range(4))
                v.wait_ge(s_pat, p + 1)
                v.wait_ge(s_sq, 2 * p + 2)
                st.mark(v.tensor_scalar(mean, acc[:, D:D + 1], -1.0 / PFEAT, None, ALU.mult))
                st.link(v.tensor_tensor(var, sc[:, p:p + 1], sc[:, 9 + p:10 + p], ALU.add))
                st.link(v.tensor_tensor(q, mean, mean, ALU.mult))
                st.link(v.tensor_scalar(var, var, 1.0 / PFEAT, LN_EPS, ALU.mult, ALU.add))
                v.tensor_tensor(sd2[:, 16 + p:17 + p], var, q, ALU.subtract).then_inc(s_pv, 1)
                t = tmp[p % 2]
                v.scalar_tensor_tensor(out=t[:], in0=sumwb[:], scalar=mean, in1=acc[:, 0:D],
                                       op0=ALU.mult, op1=ALU.add).then_inc(s_patout, 1)
                v.wait_ge(s_patout, p + 1)
                v.wait_ge(s_psd, p + 1)
                st.link(v.reciprocal(rs, sd2[:, p:p + 1]))
                for q4 in range(4):
                    tt = GRID * (3 * (q4 // 2) + i) + 3 * (q4 % 2) + j
                    a, o = 32 * q4, 32 * (tt % TQ)
                    ins = v.scalar_tensor_tensor(out=hres3[o:o + 32, tt // TQ, :], in0=t[a:a + 32, :],
                                                 scalar=rs[a:a + 32, :], in1=constb[a:a + 32, :],
                                                 op0=ALU.mult, op1=ALU.add)
                ins.then_inc(s_ptok, 1)

            for g in range(16):
                img_out(g)
            for i in range(3):
                for j in range(3):
                    if i < 2 and j < 2:
                        for g in range(16 + 8 * i + 4 * j, 20 + 8 * i + 4 * j):
                            img_out(g)
                    if 3 * i + j:
                        patch_out(3 * i + j - 1)
            patch_out(8)

            def ln1_var(c, nt):
                for j in range(nt):
                    st.mark(v.bn_stats(stats[:, j, :], hres[:, bass.ds((4 * c + j) * D, D)]))
                st.wait_apart()
                for j in range(nt):
                    st.mark(v.bn_aggr(mv[:, j, :], stats[:, j, :]))
                st.wait()
                v.tensor_scalar(sc[:, 0:nt], mv[:, 0:nt, 1], LN_EPS, None, ALU.add).then_inc(s_v1, 1)

            def ln1_scale(c, nt, first=False):
                v.wait_ge(s_sd1, c + 1)
                if not first:
                    v.wait_ge(s_t, 2 * c)
                st.link(v.reciprocal(sc[:, 8:8 + nt], sc[:, 4:4 + nt]))
                st.mark(v.tensor_scalar(sc[:, 16:16 + nt], sc[:, 8:8 + nt], 1.0, None, ALU.add))
                v.scalar_tensor_tensor(out=sc[:, 12:12 + nt], in0=mv[:, 0:nt, 0], scalar=-1.0, in1=sc[:, 8:8 + nt],
                                       op0=ALU.mult, op1=ALU.mult).then_inc(s_r1, 1)

            def ln1_add(c, nt):
                v.wait_ge(s_r1, c + 1)
                for j in range(nt):
                    t = hres[:, bass.ds((4 * c + j) * D, D)]
                    v.wait_ge(s_xn, 4 * c + j + 1)
                    st.mark(v.tensor_scalar(t, t, sc[:, 16 + j:17 + j], sc[:, 12 + j:13 + j], ALU.mult, ALU.add))

            v.wait_ge(s_ptok, PTILES)
            ln1_var(0, 4)
            ln1_scale(0, 4, True)
            v.wait_ge(s_x0, 16 * 5)
            v.memset(x0T[:, :, SEQ:SPAD], 0.0)
            rows = (P, NPATCH)
            st.link(v.memset(zrow[:], 0.0))
            st.mark(v.tensor_copy(zrow[:, D + 1:DROW], cst[:, C_PAD:C_PAD + 2]))
            st.mark(v.memset(sd2[:], 1.0))
            for k in range(2):
                st.mark(v.bn_stats(stats[0:rows[k], k, :], x0[k][0:rows[k], :]))
            st.wait()
            for k in range(2):
                st.mark(v.bn_aggr(mv[0:rows[k], k, :], stats[0:rows[k], k, :]))
            st.wait()
            for k in range(2):
                ins = v.tensor_scalar(sd2[0:rows[k], 16 + k:17 + k], mv[0:rows[k], k, 1:2], LN_EPS, None, ALU.add)
            ins.then_inc(s_v0, 1)
            v.wait_ge(s_sd0, 1)
            st.link(v.reciprocal(sd2[:, 4:6], sd2[:, 0:2]))
            for k in range(2):
                v.tensor_scalar(x0n[k][0:rows[k], :], x0[k][0:rows[k], :], mv[0:rows[k], k, 0:1],
                                sd2[0:rows[k], 4 + k:5 + k], ALU.subtract, ALU.mult).then_inc(s_x0n, 1)
            v.wait_ge(s_x0t, 1)
            for m in range(2):
                ins = v.tensor_copy(x0T[:, m, 0:NPATCH].rearrange("p (n q) -> p q n", q=TQ),
                                    bank[1][0:DH, P * m:P * m + NPATCH].rearrange("p (q n) -> p q n", q=TQ))
            ins.then_inc(s_x0T, 1)
            ln1_add(0, 4)
            for h in range(NH):
                v.wait_ge(s_kv, 2 * h + 2)
                v.tensor_copy(valsT[:, :, :, CHUNK * h:CHUNK * h + CHUNK],
                              bank[6 + h % 2][0:DH, 0:2 * SPAD].rearrange("p (m c s) -> p m c s", m=2, s=CHUNK)
                              ).then_inc(s_vvout, 1)
                if h == 2:
                    ln1_var(1, 4)
                if h == 4:
                    ln1_scale(1, 4)
                if h == 6:
                    ln1_add(1, 4)
            v.wait_ge(s_kg, 16 * NH)
            st.mark(v.tensor_tensor(kgate[:], kgate[:], cst[:, C_KEY:C_KEY + CHUNKS], ALU.mult))
            v.memset(nst[:], 0.0).then_inc(s_ns, 1)
            v.wait_ge(s_ns, 1)

            def attend(c, nt, first=False):
                w = P * nt
                v.wait_ge(s_sc, c + 1)
                v.tensor_tensor(sm[:, 0:w].rearrange("p (t b) -> p t b", b=B),
                                bank[0][:, 0:w].rearrange("p (t b) -> p t b", b=B),
                                cst[:, C_MASK:C_MASK + TQ * nt].unsqueeze(2).to_broadcast([P, TQ * nt, B]),
                                ALU.mult).then_inc(s_sm, 1)

            def picks(c, par, nt):
                v.wait_ge(s_lg, c + 1)
                v.nop(nofuse=True)
                for j in range(nt):
                    st.mark(v.max(t8[:, j, :], bank[3][:, 8 * j:8 * j + 8]))
                st.wait_apart()
                for j in range(nt):
                    st.mark(v.max_index(i8[:, j, :], t8[:, j, :], bank[3][:, 8 * j:8 * j + 8]))
                st.mark(v.tensor_copy(top8[:, bass.ds(c * 32, 8 * nt)], t8[:, 0:nt, :].rearrange("p j e -> p (j e)")))
                st.wait()
                fi = idxf[:, bass.ds(c * 8, 2 * nt)]
                st.link(v.tensor_copy(fi.rearrange("p (j k) -> p j k", k=2), i8[:, 0:nt, 0:2]))
                ohv = oh[:, 0:16 * nt]
                st.link(v.tensor_tensor(ohv.rearrange("p (a e) -> p a e", e=NE),
                                        cst[:, C_EXP:C_EXP + NE].unsqueeze(1).to_broadcast([P, 2 * nt, NE]),
                                        fi.unsqueeze(2).to_broadcast([P, 2 * nt, NE]), ALU.is_equal))
                o4 = ohv.rearrange("p (j k e) -> p j k e", k=2, e=NE)
                st.link(v.tensor_tensor(eb[:, 0:nt, :], o4[:, :, 0, :], o4[:, :, 1, :], ALU.add))
                for j in range(nt - 1):
                    st.link(v.tensor_tensor(ecum[:, j + 1, :], ecum[:, j, :], eb[:, j, :], ALU.add))
                v.tensor_tensor(ecum[:, 4, :], ecum[:, nt - 1, :], eb[:, nt - 1, :], ALU.add).then_inc(s_e, 1)

            def places(c, par, nt, wait_e=None):
                v.wait_ge(s_pf, c + 1)
                v.wait_ge(s_e, c + 1)
                st.mark(v.tensor_copy(ecum[:, 0, :], ecum[:, 4, :]))
                st.mark(v.tensor_copy(xfd[par][:, 0:nt, D + 1:DROW],
                                      cst[:, bass.ds(4 * c + C_DEST, nt)].unsqueeze(2).to_broadcast([P, nt, 2])))
                st.mark(v.tensor_copy(xfd[par][:, 0:nt, D],
                                      idxf[:, bass.ds(c * 8, 2 * nt)].rearrange("p (j k) -> p j k", k=2)[:, :, 0]))
                fi = idxf[:, bass.ds(c * 8, 2 * nt)]
                rk = rankf[:, bass.ds(c * 8, 2 * nt)]
                st.link(v.tensor_tensor(ohm[:, 0:16 * nt].rearrange("p (j k e) -> p j k e", k=2, e=NE),
                                        oh[:, 0:16 * nt].rearrange("p (j k e) -> p j k e", k=2, e=NE),
                                        bank[3][:, 64:64 + 8 * nt].rearrange("p (j e) -> p j e", e=NE).unsqueeze(2)
                                        .to_broadcast([P, nt, 2, NE]), ALU.mult))
                st.link(v.tensor_reduce(rk, ohm[:, 0:16 * nt].rearrange("p (a e) -> p a e", e=NE), AX.X, ALU.add))
                st.link(v.scalar_tensor_tensor(out=posf[:, 0:2 * nt], in0=fi, scalar=float(REGION), in1=rk,
                                               op0=ALU.mult, op1=ALU.add))
                v.tensor_copy(posu[par][:, 0:2 * nt], posf[:, 0:2 * nt]).then_inc(s_pos, 1)

            def residual(c, par, nt):
                for j in range(nt):
                    v.wait_ge(s_o, 4 * c + min(j // 2 * 2 + 2, nt))
                    v.scalar_tensor_tensor(out=h2[par][j][:], in0=bank[5 + j // 2][:, D * (j % 2):D * (j % 2) + D],
                                           scalar=cst[:, bass.ds(4 * c + (j + C_TOK), 1)],
                                           in1=hres[:, bass.ds((4 * c + j) * D, D)], op0=ALU.mult, op1=ALU.add
                                           ).then_inc(s_h2, 1)

            def state(c):
                v.wait_ge(s_nu, c + 1)
                v.tensor_tensor(nst[:], nst[:], bank[4][0:DH, 0:384].rearrange("p (m d) -> p m d", m=2),
                                ALU.add).then_inc(s_ns, 1)

            def ln2_var(c, par, nt):
                v.wait_ge(s_h2, 4 * c + nt)
                for j in range(nt):
                    st.mark(v.bn_stats(stats2[:, j, :], h2[par][j][:]))
                st.wait_apart()
                for j in range(nt):
                    st.mark(v.bn_aggr(mv2[:, j, :], stats2[:, j, :]))
                st.wait()
                st.link(v.tensor_scalar(sd2[:, 0:nt], mv2[:, 0:nt, 1], LN_EPS, None, ALU.add))
                st.link(v.reciprocal(sd2[:, 32:32 + nt], sd2[:, 0:nt]))
                st.link(v.tensor_tensor(sd2[:, 36:36 + nt], mv2[:, 0:nt, 1], sd2[:, 32:32 + nt], ALU.mult))
                v.tensor_scalar(sd2[:, 4:4 + nt], sd2[:, 36:36 + nt], RMS_EPS, None, ALU.add).then_inc(s_v2, 1)

            def ln2_scale(c, par, nt):
                v.wait_ge(s_sd2, c + 1)
                st.link(v.reciprocal(sd2[:, 16:24], sd2[:, 8:16]))
                st.mark(v.tensor_scalar(sd2[:, 40:40 + nt], sd2[:, 16:16 + nt], 1.0, None, ALU.add))
                st.mark(v.scalar_tensor_tensor(out=sd2[:, 44:44 + nt], in0=mv2[:, 0:nt, 0], scalar=-1.0,
                                               in1=sd2[:, 16:16 + nt], op0=ALU.mult, op1=ALU.mult))
                st.link(v.tensor_tensor(sd2[:, 24:24 + nt], sd2[:, 16:16 + nt], sd2[:, 20:20 + nt], ALU.mult))
                v.scalar_tensor_tensor(out=sd2[:, 28:28 + nt], in0=mv2[:, 0:nt, 0], scalar=-1.0,
                                       in1=sd2[:, 24:24 + nt], op0=ALU.mult, op1=ALU.mult).then_inc(s_s2, 1)
                for j in range(nt):
                    st.mark(v.tensor_scalar(hres[:, bass.ds((4 * c + j) * D, D)], h2[par][j][:], sd2[:, 40 + j:41 + j],
                                            sd2[:, 44 + j:45 + j], ALU.mult, ALU.add))

            def chunk(c, par, nt):
                prev, nxt, nxt2 = around(c)
                residual(c, par, nt)
                state(c)
                if nxt2:
                    ln1_var(c + 2, nxt2)
                if nxt:
                    attend(c + 1, nxt)
                if nxt2:
                    ln1_scale(c + 2, nxt2)
                ln2_var(c, par, nt)
                if nxt2:
                    ln1_add(c + 2, nxt2)
                if prev:
                    picks(c - 1, 1 - par, prev)
                ln2_scale(c, par, nt)
                if prev:
                    places(c - 1, 1 - par, prev)

            v.wait_ge(s_txt, 64)
            v.wait_ge(s_x0, 16 * 5)
            attend(0, 4)
            chunk(0, 0, 4)
            chunk(1, 1, 4)
            with v.Fori(0, 3) as i:
                st.enter(i, 2 * STEPS_PER_CHUNK)
                chunk(2 * i + 2, 0, 4)
                chunk(2 * i + 3, 1, 4)
            st.leave(3)
            chunk(8, 0, 4)
            chunk(9, 1, 4)
            chunk(10, 0, 1)
            picks(10, 0, 1)
            places(10, 0, 1)

            v.wait_ge(s_cread, 1)
            cnt, til, cum, fst, one = (ct[:, k, :] for k in range(5))
            st.mark(v.memset(one, 1.0))
            st.mark(v.tensor_scalar(cnt, bank[3][:, 128:136], float(P - 1), None, ALU.add))
            st.link(v.tensor_copy(cti[:, 1, :], bank[3][:, 128:136]))
            st.link(v.tensor_copy(cti[:, 0, :], cnt))
            st.link(v.tensor_scalar(cti[:, 0, :], cti[:, 0, :], 7, None, ALU.arith_shift_right))
            st.link(v.tensor_copy(til, cti[:, 0, :]))
            st.link(v.tensor_tensor_scan(cum, one, til, 0.0, ALU.mult, ALU.add))
            st.link(v.tensor_tensor(fst, cum, til, ALU.subtract))
            sl = cst[:, C_SLOT:C_SLOT + TAB]
            past = tabf[:]
            st.link(v.tensor_tensor(past, sl.unsqueeze(2).to_broadcast([P, TAB, NE]),
                                    cum.unsqueeze(1).to_broadcast([P, TAB, NE]), ALU.is_ge))
            st.link(v.tensor_reduce(slotf[:, 0, :], past, AX.X, ALU.add))
            st.link(v.tensor_tensor(past, past, til.unsqueeze(1).to_broadcast([P, TAB, NE]), ALU.mult))
            st.link(v.tensor_reduce(slotf[:, 1, :], past, AX.X, ALU.add))
            st.link(v.tensor_tensor(slotf[:, 1, :], sl, slotf[:, 1, :], ALU.subtract))
            st.link(v.tensor_scalar(slotf[:, 2, :], slotf[:, 0, :], float(REGION // P), None, ALU.mult))
            st.link(v.tensor_tensor(slotf[:, 1, :], slotf[:, 1, :], slotf[:, 2, :], ALU.add))
            st.link(v.tensor_scalar(slotf[:, 1, :], slotf[:, 1, :], float(P), float(NE * REGION), ALU.mult, ALU.min))
            st.link(v.tensor_scalar(slotf[:, 0, :], slotf[:, 0, :], float(NE - 1), None, ALU.min))
            st.mark(v.tensor_copy(tab[:, 0, :], slotf[:, 1, :]))
            v.tensor_copy(tab[:, 1, :], slotf[:, 0, :]).then_inc(s_tab, 1)
            st.wait()
            t3 = top8[:].rearrange("p (n e) -> p n e", e=8)
            st.link(v.tensor_copy(esum[:], t3[:, :, 0]))
            v.tensor_tensor(t3, t3, esum[:].unsqueeze(2).to_broadcast([P, TILES, 8]), ALU.subtract).then_inc(s_w, 1)
            experts_out(v, 0)
            v.wait_ge(s_exp, 1)
            st.link(v.tensor_reduce(esum[:], t3, AX.X, ALU.add))
            st.link(v.reciprocal(esum[:], esum[:]))
            st.link(v.tensor_tensor(wts[:].rearrange("p (n k) -> p n k", k=2), t3[:, :, 0:2],
                                    esum[:].unsqueeze(2).to_broadcast([P, TILES, 2]), ALU.mult))

            def step(k, b, parts="xght"):
                if "x" in parts:
                    v.wait_ge(s_xst, k + 3)
                    v.scalar_tensor_tensor(out=dest[:, bass.ds(k + 2, 1)], in0=xs[b][:, 2 * P:2 * P + 1],
                                           scalar=slotf[:, 0, bass.ds(k + 2, 1)],
                                           in1=xs[b][:, 2 * P + 1 + b:2 * P + 2 + b],
                                           op0=ALU.not_equal, op1=ALU.add).then_inc(s_dest, 1)
                    v.wait_ge(s_xh, k + 3)
                    v.tensor_tensor(xl[b][:], bank[5][:, 0:2 * P], xh[b][:].bitcast(F32), ALU.subtract).then_inc(s_xlo, 1)
                if "g" in parts:
                    o = 1 - b
                    v.wait_ge(s_sg, k + 2)
                    v.tensor_tensor(hh[o][:], sg[o][:], bank[2 * o + 1][:, 0:DE], ALU.mult).then_inc(s_hh, 1)
                if "h" in parts:
                    v.wait_ge(s_hth, k + 1)
                    v.tensor_tensor(htl[b][:], bank[4][:, 0:DE], hth[b][:].bitcast(F32), ALU.subtract).then_inc(s_htl, 1)
                if "t" in parts:
                    o = 1 - b
                    v.wait_ge(s_dn, k)
                    if not isinstance(k, int) or k > 2:
                        v.wait_ge(s_ys[o], 8 * (k - 1 - o))
                    v.tensor_copy(ysb[o][:], bank[6 + o][:, 0:D]).then_inc(s_y, 1)

            pipeline(v, step, "xght", (2, 1, 0, -1), peel=2)

            for n in range(TILES):
                if n % GROUP == 0:
                    v.wait_ge(s_yg[n // GROUP], 16)
                if n % 2 == 0:
                    pair = range(n, min(n + 2, TILES))
                    for k in range(2):
                        for a in pair:
                            t, y = hres[:, D * a:D * (a + 1)], yall[:, 2 * D * a + D * k:2 * D * a + D * k + D]
                            ins = v.scalar_tensor_tensor(out=t, in0=y, scalar=wts[:, 2 * a + k:2 * a + k + 1], in1=t,
                                                         op0=ALU.mult, op1=ALU.add)
                            if k:
                                ins.then_inc(s_fin, 1)
                            else:
                                st.mark(ins)
                        st.wait()


STEPS_PER_CHUNK = 54

_INS = ['x', 'txt', 'L0_tok_ln_gamma', 'L0_tok_ln_beta', 'L0_tok_W', 'L0_tok_b', 'L0_attn_w_key', 'L0_attn_w_value',
        'L0_attn_w_query', 'L0_attn_w_gate', 'L0_attn_w_out', 'L0_ffn_norm_w', 'L0_ffn_router_w', 'L0_ffn_gate_w',
        'L0_ffn_up_w', 'L0_ffn_down_w']


def shape_constants():
    import numpy as np

    c = np.zeros((P, C_ALL), np.float64)
    p = np.arange(P)
    step = p % CHUNK
    for k in range(CHUNKS):
        c[:, C_KEY + k] = WRITE * DECAY ** (-1.0 - (CHUNK * k + step))
    for n in range(TILES):
        c[:, C_TOK + n] = DECAY ** (TQ * n + p // B)
    c[:, C_MASK:C_MASK + CHUNK] = step[:, None] < np.arange(CHUNK)[None]
    right = (p % 16) >= 8
    for k in range(24):
        dr, s = k // 6 - 1, k // 3 % 2
        inner = (right if s == 0 else ~right) if dr in (0, 1) else np.zeros(P, bool)
        c[:, C_STAT + k] = 1.0 + inner
    c[:, C_EXP:C_EXP + NE] = np.arange(NE)
    c[:, C_SLOT:C_SLOT + TAB] = np.arange(TAB)
    c[:, C_DEST:C_DEST + TILES] = 2 * (P * np.arange(TILES)[None] + p[:, None])
    c[:, C_PAD] = 2 * (TOKENS + p)
    c[:, C_PAD + 1] = 2 * (TOKENS + P + p)
    return c.astype(np.float32)


def kernel(**inputs):
    import numpy as np
    import concourse.bacc as bacc
    from concourse.bass_utils import run_bass_kernel_spmd

    nc = bacc.Bacc("TRN2", target_bir_lowering=False, num_devices=1)
    arrays, args = {}, []
    for name in _INS:
        a = np.ascontiguousarray(inputs[name])
        arrays[f"in_{name}"] = a
        args.append(nc.dram_tensor(f"in_{name}", a.shape, mybir.dt.from_np(a.dtype), kind="ExternalInput").ap())
    arrays["in_consts"] = shape_constants()
    args.append(nc.dram_tensor("in_consts", (P, C_ALL), F32, kind="ExternalInput").ap())
    args.append(nc.dram_tensor("out_0", (B, SEQ, D), F32, kind="ExternalOutput").ap())
    build(nc, *args)
    r = run_bass_kernel_spmd(nc, [arrays], core_ids=[0])
    return r.results[0]["out_0"]
```
